# Optimizing a Trainium2 kernel written in Bass

```python
import numpy as np
import jax
import jax.numpy as jnp

def _softmax(x, axis=-1):
    return jax.nn.softmax(x, axis=axis)

def _gelu(x):
    return jax.nn.gelu(x, approximate=True)

def _silu(x):
    return jax.nn.silu(x)

def _sigmoid(x):
    return jax.nn.sigmoid(x)

def _layernorm(x, axis=-1, eps=1e-05):
    m = jnp.mean(x, axis=axis, keepdims=True)
    v = jnp.var(x, axis=axis, keepdims=True)
    return (x - m) / jnp.sqrt(v + eps)

def _scatter_add(tgt, idx, src, axis=0):
    return tgt.at[idx].add(src)

def _segment_sum(src, seg, n):
    return jax.ops.segment_sum(src, seg, n)
kernel_name = 'mk_sandwich_d2_jaxref_r8_d17510'

def setup_inputs(seed: int=0):
    np.random.seed(seed)
    _w = jnp.asarray

    def _L0_attn_setup():
        import jax, jax.numpy as jnp
        import numpy as np
        D_MODEL = 128
        N_HEADS = 16
        D_HEAD = 64
        B, S = (8, 128)
        EPS = 1.1920929e-07
        key = jax.random.key(seed)
        k1, k2, k3 = jax.random.split(key, 3)
        x = jax.random.normal(k1, (B, S, D_MODEL), dtype=jnp.float32)
        W_qkv = jax.random.normal(k2, (3 * N_HEADS * D_HEAD, D_MODEL), dtype=jnp.float32) * 0.02
        b_qkv = jnp.zeros((3 * N_HEADS * D_HEAD,), dtype=jnp.float32)
        W_o = jax.random.normal(k3, (D_MODEL, N_HEADS * D_HEAD), dtype=jnp.float32) * 0.02
        b_o = jnp.zeros((D_MODEL,), dtype=jnp.float32)
        return {'x': x, 'W_qkv': W_qkv, 'b_qkv': b_qkv, 'W_o': W_o, 'b_o': b_o}
    _L0_attn_in = _L0_attn_setup()

    def _L0_ffn_setup():
        import jax, jax.numpy as jnp
        import numpy as np
        DIM, HEADS, EXPERTS, DFF = (128, 16, 8, 512)
        EPS = 1e-05

        def layernorm(x, g, b):
            mu = jnp.mean(x, -1, keepdims=True)
            var = jnp.mean(jnp.square(x - mu), -1, keepdims=True)
            return (x - mu) * jax.lax.rsqrt(var + EPS) * g + b
        key = jax.random.key(seed)
        ks = jax.random.split(key, 12)
        s = lambda d: 1.0 / np.sqrt(d)
        return {'x': jax.random.normal(ks[0], (2, 256, DIM), jnp.float32), 'conv_w': jax.random.normal(ks[1], (DIM, DIM, 3), jnp.float32) * s(DIM * 3), 'conv_b': jnp.zeros((DIM,), jnp.float32), 'wqkv': jax.random.normal(ks[2], (3 * DIM, DIM), jnp.float32) * s(DIM), 'bqkv': jnp.zeros((3 * DIM,), jnp.float32), 'wo': jax.random.normal(ks[3], (DIM, DIM), jnp.float32) * s(DIM), 'bo': jnp.zeros((DIM,), jnp.float32), 'ln1_g': jnp.ones((DIM,), jnp.float32), 'ln1_b': jnp.zeros((DIM,), jnp.float32), 'gate_w': jax.random.normal(ks[4], (DIM, EXPERTS), jnp.float32) * s(DIM), 'gate_b': jnp.zeros((EXPERTS,), jnp.float32), 'w1': jax.random.normal(ks[5], (EXPERTS, DIM, DFF), jnp.float32) * s(DIM), 'b1': jnp.zeros((EXPERTS, DFF), jnp.float32), 'w2': jax.random.normal(ks[6], (EXPERTS, DFF, DIM), jnp.float32) * s(DFF), 'b2': jnp.zeros((EXPERTS, DIM), jnp.float32), 'ln2_g': jnp.ones((DIM,), jnp.float32), 'ln2_b': jnp.zeros((DIM,), jnp.float32)}
    _L0_ffn_in = _L0_ffn_setup()

    def _L1_attn_setup():
        import jax, jax.numpy as jnp
        import numpy as np
        N_HEADS = 16

        def _rotate_half(t):
            shp = t.shape
            t2 = t.reshape(*shp[:-1], shp[-1] // 2, 2)
            return jnp.stack((-t2[..., 1], t2[..., 0]), axis=-1).reshape(shp)
        key = jax.random.key(seed)
        k1, k2, k3 = jax.random.split(key, 3)
        B, N, D = (2, 256, 128)
        x = jax.random.normal(k1, (B, N, D), dtype=jnp.float32)
        w_qkv = jax.random.normal(k2, (D, 3 * D), dtype=jnp.float32) * D ** (-0.5)
        w_proj = jax.random.normal(k3, (D, D), dtype=jnp.float32) * D ** (-0.5)
        return {'x': x, 'w_qkv': w_qkv, 'w_proj': w_proj}
    _L1_attn_in = _L1_attn_setup()

    def _L1_ffn_setup():
        import jax, jax.numpy as jnp
        import numpy as np
        DIM, HEADS, FFN, E = (128, 16, 512, 8)
        B, S = (2, 128)
        EPS = 1e-05

        def _ln(x, g, b):
            mu = jnp.mean(x, axis=-1, keepdims=True)
            var = jnp.mean((x - mu) ** 2, axis=-1, keepdims=True)
            return (x - mu) * jax.lax.rsqrt(var + EPS) * g + b
        key = jax.random.key(seed)
        ks = jax.random.split(key, 20)
        sd = 0.02
        d, f = (DIM, FFN)
        return {'x': jax.random.normal(ks[0], (B, S, d), jnp.float32), 'ln1_g': jnp.ones((d,), jnp.float32), 'ln1_b': jnp.zeros((d,), jnp.float32), 'Wqkv': jax.random.normal(ks[1], (d, 3 * d), jnp.float32) * sd, 'bqkv': jnp.zeros((3 * d,), jnp.float32), 'Wo': jax.random.normal(ks[2], (d, d), jnp.float32) * sd, 'bo': jnp.zeros((d,), jnp.float32), 'ln2_g': jnp.ones((d,), jnp.float32), 'ln2_b': jnp.zeros((d,), jnp.float32), 'gate_w': jax.random.normal(ks[3], (d, E), jnp.float32) * sd, 'W1': jax.random.normal(ks[4], (E, d, f), jnp.float32) * sd, 'b1': jnp.zeros((E, f), jnp.float32), 'W2': jax.random.normal(ks[5], (E, f, d), jnp.float32) * sd, 'b2': jnp.zeros((E, d), jnp.float32), 'rW1': jax.random.normal(ks[6], (d, f), jnp.float32) * sd, 'rb1': jnp.zeros((f,), jnp.float32), 'rW2': jax.random.normal(ks[7], (f, d), jnp.float32) * sd, 'rb2': jnp.zeros((d,), jnp.float32), 'coef_w': jax.random.normal(ks[8], (d, 2), jnp.float32) * sd, 'coef_b': jnp.zeros((2,), jnp.float32)}
    _L1_ffn_in = _L1_ffn_setup()
    _d = {'L0_attn_x': _L0_attn_in['x'], 'L0_attn_W_qkv': _L0_attn_in['W_qkv'], 'L0_attn_b_qkv': _L0_attn_in['b_qkv'], 'L0_attn_W_o': _L0_attn_in['W_o'], 'L0_attn_b_o': _L0_attn_in['b_o'], 'L0_ffn_conv_w': _L0_ffn_in['conv_w'], 'L0_ffn_conv_b': _L0_ffn_in['conv_b'], 'L0_ffn_wqkv': _L0_ffn_in['wqkv'], 'L0_ffn_bqkv': _L0_ffn_in['bqkv'], 'L0_ffn_wo': _L0_ffn_in['wo'], 'L0_ffn_bo': _L0_ffn_in['bo'], 'L0_ffn_ln1_g': _L0_ffn_in['ln1_g'], 'L0_ffn_ln1_b': _L0_ffn_in['ln1_b'], 'L0_ffn_gate_w': _L0_ffn_in['gate_w'], 'L0_ffn_gate_b': _L0_ffn_in['gate_b'], 'L0_ffn_w1': _L0_ffn_in['w1'], 'L0_ffn_b1': _L0_ffn_in['b1'], 'L0_ffn_w2': _L0_ffn_in['w2'], 'L0_ffn_b2': _L0_ffn_in['b2'], 'L0_ffn_ln2_g': _L0_ffn_in['ln2_g'], 'L0_ffn_ln2_b': _L0_ffn_in['ln2_b'], 'L1_attn_w_qkv': _L1_attn_in['w_qkv'], 'L1_attn_w_proj': _L1_attn_in['w_proj'], 'L1_ffn_ln1_g': _L1_ffn_in['ln1_g'], 'L1_ffn_ln1_b': _L1_ffn_in['ln1_b'], 'L1_ffn_Wqkv': _L1_ffn_in['Wqkv'], 'L1_ffn_bqkv': _L1_ffn_in['bqkv'], 'L1_ffn_Wo': _L1_ffn_in['Wo'], 'L1_ffn_bo': _L1_ffn_in['bo'], 'L1_ffn_ln2_g': _L1_ffn_in['ln2_g'], 'L1_ffn_ln2_b': _L1_ffn_in['ln2_b'], 'L1_ffn_gate_w': _L1_ffn_in['gate_w'], 'L1_ffn_W1': _L1_ffn_in['W1'], 'L1_ffn_b1': _L1_ffn_in['b1'], 'L1_ffn_W2': _L1_ffn_in['W2'], 'L1_ffn_b2': _L1_ffn_in['b2'], 'L1_ffn_rW1': _L1_ffn_in['rW1'], 'L1_ffn_rb1': _L1_ffn_in['rb1'], 'L1_ffn_rW2': _L1_ffn_in['rW2'], 'L1_ffn_rb2': _L1_ffn_in['rb2'], 'L1_ffn_coef_w': _L1_ffn_in['coef_w'], 'L1_ffn_coef_b': _L1_ffn_in['coef_b']}
    _x0 = _d['L0_attn_x']
    _d['L0_attn_x'] = jax.random.normal(jax.random.fold_in(jax.random.key(seed), 1), (1, 2048, 128), dtype=_x0.dtype)
    del _x0
    return _d

def reference(L0_attn_x, L0_attn_W_qkv, L0_attn_b_qkv, L0_attn_W_o, L0_attn_b_o, L0_ffn_conv_w, L0_ffn_conv_b, L0_ffn_wqkv, L0_ffn_bqkv, L0_ffn_wo, L0_ffn_bo, L0_ffn_ln1_g, L0_ffn_ln1_b, L0_ffn_gate_w, L0_ffn_gate_b, L0_ffn_w1, L0_ffn_b1, L0_ffn_w2, L0_ffn_b2, L0_ffn_ln2_g, L0_ffn_ln2_b, L1_attn_w_qkv, L1_attn_w_proj, L1_ffn_ln1_g, L1_ffn_ln1_b, L1_ffn_Wqkv, L1_ffn_bqkv, L1_ffn_Wo, L1_ffn_bo, L1_ffn_ln2_g, L1_ffn_ln2_b, L1_ffn_gate_w, L1_ffn_W1, L1_ffn_b1, L1_ffn_W2, L1_ffn_b2, L1_ffn_rW1, L1_ffn_rb1, L1_ffn_rW2, L1_ffn_rb2, L1_ffn_coef_w, L1_ffn_coef_b):

    def _L0_attn_ref(x, W_qkv, b_qkv, W_o, b_o):
        import jax, jax.numpy as jnp
        import numpy as np
        D_MODEL = 128
        N_HEADS = 16
        D_HEAD = 64
        B, S = (8, 128)
        EPS = 1.1920929e-07
        normed = x * jax.lax.rsqrt(jnp.mean(x * x, axis=-1, keepdims=True) + EPS)
        qkv = normed @ W_qkv.T + b_qkv
        qkv = qkv.reshape(*qkv.shape[:-1], N_HEADS, D_HEAD, 3)
        q, k, v = (qkv[..., 0], qkv[..., 1], qkv[..., 2])
        scores = jnp.einsum('bqhd,bkhd->bhqk', q, k)
        seq = x.shape[-2]
        causal_mask = jnp.triu(jnp.ones((seq, seq), dtype=bool), k=1)
        scores = jnp.where(causal_mask, -jnp.inf, scores)
        attn = jax.nn.softmax(scores, axis=-2)
        z = jnp.einsum('bhqk,bkhd->bqhd', attn, v)
        z = z.reshape(*z.shape[:-2], N_HEADS * D_HEAD)
        return z @ W_o.T + b_o

    def _L0_ffn_ref(x, conv_w, conv_b, wqkv, bqkv, wo, bo, ln1_g, ln1_b, gate_w, gate_b, w1, b1, w2, b2, ln2_g, ln2_b):
        import jax, jax.numpy as jnp
        import numpy as np
        DIM, HEADS, EXPERTS, DFF = (128, 16, 8, 512)
        EPS = 1e-05

        def layernorm(x, g, b):
            mu = jnp.mean(x, -1, keepdims=True)
            var = jnp.mean(jnp.square(x - mu), -1, keepdims=True)
            return (x - mu) * jax.lax.rsqrt(var + EPS) * g + b
        B, S, D = x.shape
        H, dh = (HEADS, D // HEADS)
        xt = jnp.transpose(x, (0, 2, 1))
        xt = jax.lax.conv_general_dilated(xt, conv_w, (1,), [(1, 1)], dimension_numbers=('NCH', 'OIH', 'NCH'))
        x = jnp.transpose(xt + conv_b[None, :, None], (0, 2, 1))
        qkv = x @ wqkv.T + bqkv
        q, k, v = jnp.split(qkv, 3, axis=-1)
        q = q.reshape(B, S, H, dh).transpose(0, 2, 1, 3)
        k = k.reshape(B, S, H, dh).transpose(0, 2, 1, 3)
        v = v.reshape(B, S, H, dh).transpose(0, 2, 1, 3)
        scores = jnp.einsum('bhqd,bhkd->bhqk', q, k) / jnp.sqrt(jnp.float32(dh))
        attn = jax.nn.softmax(scores, axis=-1)
        ctx = jnp.einsum('bhqk,bhkd->bhqd', attn, v)
        ctx = ctx.transpose(0, 2, 1, 3).reshape(B, S, D)
        attn_out = ctx @ wo.T + bo
        x = layernorm(x + attn_out, ln1_g, ln1_b)
        probs = jax.nn.softmax(x @ gate_w + gate_b, axis=-1)
        h = jax.nn.relu(jnp.einsum('bsd,edf->bsef', x, w1) + b1)
        y = jnp.einsum('bsef,efd->bsed', h, w2) + b2
        moe_out = jnp.einsum('bse,bsed->bsd', probs, y)
        x = layernorm(x + moe_out, ln2_g, ln2_b)
        return x

    def _L1_attn_ref(x, w_qkv, w_proj):
        import jax, jax.numpy as jnp
        import numpy as np
        N_HEADS = 16

        def _rotate_half(t):
            shp = t.shape
            t2 = t.reshape(*shp[:-1], shp[-1] // 2, 2)
            return jnp.stack((-t2[..., 1], t2[..., 0]), axis=-1).reshape(shp)
        B, N, D = x.shape
        H = N_HEADS
        hd = D // H
        qkv = x @ w_qkv
        qkv = qkv.reshape(B, N, 3, H, hd).transpose(2, 0, 3, 1, 4)
        q, k, v = (qkv[0], qkv[1], qkv[2])
        inv_freq = 1.0 / 10000.0 ** (jnp.arange(0, hd, 2, dtype=jnp.float32) / hd)
        freqs = jnp.arange(N, dtype=jnp.float32)[:, None] * inv_freq[None, :]
        sin = jnp.repeat(jnp.sin(freqs), 2, axis=-1)[None, None]
        cos = jnp.repeat(jnp.cos(freqs), 2, axis=-1)[None, None]
        q = q * cos + _rotate_half(q) * sin
        k = k * cos + _rotate_half(k) * sin
        scale = hd ** (-0.5)
        attn = jax.nn.softmax(jnp.einsum('bhqd,bhkd->bhqk', q, k) * scale, axis=-1)
        out = jnp.einsum('bhqk,bhkd->bhqd', attn, v)
        out = out.transpose(0, 2, 1, 3).reshape(B, N, D)
        return out @ w_proj

    def _L1_ffn_ref(x, ln1_g, ln1_b, Wqkv, bqkv, Wo, bo, ln2_g, ln2_b, gate_w, W1, b1, W2, b2, rW1, rb1, rW2, rb2, coef_w, coef_b):
        import jax, jax.numpy as jnp
        import numpy as np
        DIM, HEADS, FFN, E = (128, 16, 512, 8)
        B, S = (2, 128)
        EPS = 1e-05

        def _ln(x, g, b):
            mu = jnp.mean(x, axis=-1, keepdims=True)
            var = jnp.mean((x - mu) ** 2, axis=-1, keepdims=True)
            return (x - mu) * jax.lax.rsqrt(var + EPS) * g + b
        b, s, d = x.shape
        h, dh = (HEADS, d // HEADS)
        xn = _ln(x, ln1_g, ln1_b)
        qkv = xn @ Wqkv + bqkv
        q, k, v = jnp.split(qkv, 3, axis=-1)
        q = q.reshape(b, s, h, dh)
        k = k.reshape(b, s, h, dh)
        v = v.reshape(b, s, h, dh)
        scores = jnp.einsum('bqhd,bkhd->bhqk', q, k) / jnp.sqrt(jnp.float32(dh))
        attn = jax.nn.softmax(scores, axis=-1)
        ctx = jnp.einsum('bhqk,bkhd->bqhd', attn, v).reshape(b, s, d)
        x = x + ctx @ Wo + bo
        xn2 = _ln(x, ln2_g, ln2_b)
        xt = xn2.reshape(b * s, d)
        probs = jax.nn.softmax(xt @ gate_w, axis=-1)
        gate_val = jnp.max(probs, axis=-1, keepdims=True)
        expert_idx = jnp.argmax(probs, axis=-1)
        oh = jax.nn.one_hot(expert_idx, E, dtype=xt.dtype)
        xe = jnp.einsum('te,td->etd', oh, xt)
        he = jax.nn.gelu(jnp.einsum('etd,edf->etf', xe, W1) + b1[:, None, :], approximate=False)
        ye = jnp.einsum('etf,efd->etd', he, W2) + b2[:, None, :]
        moe_out = jnp.einsum('te,etd->td', oh, ye) * gate_val
        rm = jax.nn.gelu(xt @ rW1 + rb1, approximate=False) @ rW2 + rb2
        coef = jax.nn.softmax(xt @ coef_w + coef_b, axis=-1)
        ff = moe_out * coef[:, 0:1] + rm * coef[:, 1:2]
        return x + ff.reshape(b, s, d)
    x = L0_attn_x
    x = x + _layernorm(_L0_attn_ref(_layernorm(x, axis=-1), L0_attn_W_qkv, L0_attn_b_qkv, L0_attn_W_o, L0_attn_b_o), axis=-1)
    x = x + _layernorm(_L0_ffn_ref(_layernorm(x, axis=-1), L0_ffn_conv_w, L0_ffn_conv_b, L0_ffn_wqkv, L0_ffn_bqkv, L0_ffn_wo, L0_ffn_bo, L0_ffn_ln1_g, L0_ffn_ln1_b, L0_ffn_gate_w, L0_ffn_gate_b, L0_ffn_w1, L0_ffn_b1, L0_ffn_w2, L0_ffn_b2, L0_ffn_ln2_g, L0_ffn_ln2_b), axis=-1)
    x = x + _layernorm(_L1_attn_ref(_layernorm(x, axis=-1), L1_attn_w_qkv, L1_attn_w_proj), axis=-1)
    x = x + _layernorm(_L1_ffn_ref(_layernorm(x, axis=-1), L1_ffn_ln1_g, L1_ffn_ln1_b, L1_ffn_Wqkv, L1_ffn_bqkv, L1_ffn_Wo, L1_ffn_bo, L1_ffn_ln2_g, L1_ffn_ln2_b, L1_ffn_gate_w, L1_ffn_W1, L1_ffn_b1, L1_ffn_W2, L1_ffn_b2, L1_ffn_rW1, L1_ffn_rb1, L1_ffn_rW2, L1_ffn_rb2, L1_ffn_coef_w, L1_ffn_coef_b), axis=-1)
    return x

_drawn_inputs = setup_inputs


def setup_inputs(seed=0):
    import zlib

    import numpy as np

    out = dict(_drawn_inputs(seed))
    spreads = {'L0_attn_b_qkv': (0.0, 0.1),
     'L0_attn_b_o': (0.0, 0.1),
     'L0_ffn_conv_b': (0.0, 0.1),
     'L0_ffn_bqkv': (0.0, 0.1),
     'L0_ffn_bo': (0.0, 0.1),
     'L0_ffn_ln1_g': (1.0, 0.2),
     'L0_ffn_ln1_b': (0.0, 0.1),
     'L0_ffn_gate_b': (0.0, 0.548),
     'L0_ffn_b1': (0.0, 0.493),
     'L0_ffn_b2': (0.0, 0.38),
     'L0_ffn_ln2_g': (1.0, 0.2),
     'L0_ffn_ln2_b': (0.0, 0.1),
     'L1_ffn_ln1_g': (1.0, 0.6),
     'L1_ffn_ln1_b': (0.0, 0.8),
     'L1_ffn_bqkv': (0.0, 0.8),
     'L1_ffn_bo': (0.0, 0.28),
     'L1_ffn_ln2_g': (1.0, 0.6),
     'L1_ffn_ln2_b': (0.0, 0.8),
     'L1_ffn_b1': (0.0, 0.8),
     'L1_ffn_b2': (0.0, 0.8),
     'L1_ffn_rb1': (0.0, 0.8),
     'L1_ffn_rb2': (0.0, 0.522),
     'L1_ffn_coef_b': (0.0, 0.8)}
    factors = {'L1_ffn_Wqkv': 4.876,
     'L1_ffn_Wo': 3.501,
     'L1_ffn_gate_w': 8.0,
     'L1_ffn_W1': 8.0,
     'L1_ffn_W2': 8.0,
     'L1_ffn_rW1': 6.778,
     'L1_ffn_rW2': 6.516,
     'L1_ffn_coef_w': 8.0}
    for name, (base, spread) in spreads.items():
        noise = np.random.default_rng([zlib.crc32(name.encode()), seed]).standard_normal(out[name].shape)
        drawn = base * np.exp(spread * noise) if base else spread * noise
        out[name] = jnp.asarray(drawn.astype(out[name].dtype))
    for name, factor in factors.items():
        out[name] = (out[name] * factor).astype(out[name].dtype)
    return out
```

```python
from contextlib import ExitStack

import concourse.bass as bass
from concourse import mybir

F32 = mybir.dt.float32
BF16 = mybir.dt.bfloat16
ALU = mybir.AluOpType
ACT = mybir.ActivationFunctionType
X_AXIS = mybir.AxisListType.X

P = 128
S = 2048
NT = S // P
CW = 512
NC = S // CW
TPC = CW // P
EPS = 1e-5
RMS_EPS = 1.1920929e-07
MASKED = -1e30

AD = 64
PAIRS = 8
RING = 6
LAG = 2
PROJ = 3 * NC
PROJ_FROM = 20

H = 16
DH = 8
SLOTS = 6
MROW = SLOTS * DH
VC = 32
SCALE = float(DH) ** -0.5

E0, E1 = 8, 9
FFN = 512
FC = FFN // P

ROWS = [(r // NT, r % NT) for r in range(2 * NT)]


def row_chunks(i):
    return [(c, P * (i % TPC) if c == i // TPC else 0) for c in range(i // TPC, NC)]


def pair_plan(projects):
    j, plan = 0, []
    for r, (_, i) in enumerate(ROWS):
        n = len(row_chunks(i))
        followed = projects and r >= PROJ_FROM
        plan.append((j, n, j + n if followed else None))
        j += n + followed
    return plan, j


PLAN, PER_PAIR = pair_plan(True)
LAST_PLAN, _ = pair_plan(False)
assert 2 * NT - PROJ_FROM == PROJ


def ring_user_before(pair, j):
    base = PROJ + pair * PER_PAIR
    if j >= RING:
        return base + j - RING + 1
    n = PROJ if isinstance(pair, int) and pair == 0 else PER_PAIR
    last = n - 1 - (n - 1 - j) % RING
    return base - n + last + 1


def run_pairs(eng, emit):
    emit(0, 0)
    with eng.Fori(0, (PAIRS - 2) // 2) as i:
        emit(i * 2 + 1, 1)
        emit(i * 2 + 2, 0)
    emit(PAIRS - 1, 1)


def run_heads(eng, emit):
    emit(0, 0, 0)
    with eng.Fori(0, (H - 2) // 2) as i:
        emit(i * 2 + 1, 1, i)
        emit(i * 2 + 2, 0, i + 1)
    emit(H - 1, 1, H // 2 - 1)


def run_experts(eng, n, emit):
    emit(0, 0, 0)
    emit(1, 1, 0)
    with eng.Fori(0, 3) as i:
        emit(i * 2 + 2, 0, i + 1)
        emit(i * 2 + 3, 1, i + 1)
    if n == E1:
        emit(8, 0, 4)


MAX_TILES = [[]] + [[] for _ in range(NT - 1)]
for _q in range(NT):
    MAX_TILES[1 + _q * 14 // NT].append(_q)


def is_int(x):
    return isinstance(x, int)


def sandwich_kernel(nc, t, out):
    ctx = ExitStack()
    with ctx:
        def sb(name, shape, dt=F32):
            return ctx.enter_context(nc.sbuf_tensor(name, shape, dt))

        def sem(name):
            return ctx.enter_context(nc.semaphore(name))

        parts_dram = nc.dram_tensor("parts_dram", (3, 2, 3, H, DH, S), BF16, kind="Internal").ap()
        z_dram = nc.dram_tensor("z_dram", (3, 2, H, DH, S), F32, kind="Internal").ap()

        ps = ctx.enter_context(nc.psum_tensor("ps", [P, 8, CW], F32))
        MISC = 7

        X = sb("X", [P, S])
        XH = sb("XH", [P, S])
        XTp = sb("XTp", [P, S + 2])
        XT = XTp[:, 1:S + 1]
        Y = sb("Y", [P, S])
        probs = sb("probs", [P, 4, S])
        arena = sb("arena", [P, 13 * S])
        QS = [sb(f"QS{p}", [P, S], BF16) for p in range(2)]
        KS = [sb(f"KS{p}", [P, S], BF16) for p in range(2)]
        VS = sb("VS", [P, 2, NT, VC])
        QT = [arena[:, 0 * S:1 * S], arena[:, 1 * S:2 * S]]
        KT = [arena[:, 2 * S:3 * S], arena[:, 3 * S:4 * S]]
        VA = [arena[:, 4 * S:5 * S], Y[:, :]]
        ZA = arena[:, 5 * S:13 * S]
        CT = arena[:, 0 * S:1 * S]
        CM = arena[:, 1 * S:2 * S]
        T = [arena[:, (2 + n) * S:(3 + n) * S] for n in range(4)]
        ZT, ZS = T[0], T[1]
        COS, SIN = arena[:, 6 * S:7 * S], arena[:, 7 * S:8 * S]
        PARTS = [arena[:, 8 * S:8 * S + 3 * S // 2].bitcast(BF16),
                 arena[:, 10 * S:10 * S + 3 * S // 2].bitcast(BF16)]
        ACC = T[2]
        VALL = Y
        HT = [probs[:, 0, :], probs[:, 1, :]]
        W1S = [probs[:, 2, 0:FFN], probs[:, 2, FFN:2 * FFN]]
        W2S = [probs[:, 2, 2 * FFN:3 * FFN], probs[:, 2, 3 * FFN:4 * FFN]]
        ZST = T[3][:, 0:2 * CW].rearrange("p (n c) -> p n c", n=2)
        late = arena[:, 23 * S // 2:13 * S]
        B1S = sb("B1S", [P, 2, FC])
        WT = probs[0:E1, 3, :]

        w_a = sb("w_a", [P, 3 * P])
        bqk_a = sb("bqk_a", [P, 2])
        bv_a = sb("bv_a", [P, P])
        wo_a = sb("wo_a", [P, PAIRS * P])
        bo_a = sb("bo_a", [P, P])
        conv_w = late[:, 0:3 * P]
        conv_b = sb("conv_b", [P, 1])
        wqkv = late[:, 3 * P:12 * P].rearrange("p (s n) -> p s n", s=3)
        wrot = late[:, 12 * P:14 * P]
        bqk = sb("bqk", [P, 3, 2])
        bv = late[:, 14 * P:16 * P].rearrange("p (s n) -> p s n", s=2)
        wo = late[:, 16 * P:19 * P].rearrange("p (s n) -> p s n", s=3)
        bo = late[:, 19 * P:21 * P].rearrange("p (s n) -> p s n", s=2)
        lnrow = sb("lnrow", [P, 4, P])
        lncol = sb("lncol", [P, 6])
        gw = sb("gw", [P, 2, 10])
        gb = sb("gb", [P, 10])
        rank = sb("rank", [P, E0])
        b2s = sb("b2s", [E1, 2, P])
        ident = sb("ident", [P, P])
        identb = sb("identb", [P, P], BF16)
        maskb = sb("maskb", [P, P], BF16)

        stats = sb("stats", [P, NT, 6])
        mv = sb("mv", [P, NT, 2])
        var = sb("var", [P, NT])
        std = sb("std", [P, NT])
        rstd = sb("rstd", [P, NT])
        amx = sb("amx", [P, 4, NC])
        anm = sb("anm", [P, 4])
        als = sb("als", [P, 4, NC])
        asum = sb("asum", [P, 4])
        arl = sb("arl", [P, 4])
        VR = sb("VR", [P, 4, AD])
        mx = sb("mx", [P, NT, 2])
        nm = sb("nm", [P, NT])
        nr = sb("nr", [P, NT])
        mb = sb("mb", [P, P], BF16)
        mT = sb("mT", [3 * NT, P], BF16)
        gl = sb("gl", [P, NT, 10])
        ge = sb("ge", [P, NT, 10])
        gp = sb("gp", [P, NT, E0])
        gm = sb("gm", [P, NT])
        gs = sb("gs", [P, NT])
        g2 = sb("g2", [P, NT])
        wgt = sb("wgt", [P, E1, NT])
        WPE = wgt[:, :, :].rearrange("p e t -> p t e")

        ld_x = sem("ld_x")
        ld_early = sem("ld_early")
        ld_late = sem("ld_late")
        consts_made = sem("consts_made")
        pool_step = sem("pool_step")
        dve_step = sem("dve_step")
        ones_loaded = sem("ones_loaded")
        staging_cleared = sem("staging_cleared")
        tables_loaded = sem("tables_loaded")
        wrot_made = sem("wrot_made")
        var_ready = sem("var_ready")
        std_ready = sem("std_ready")
        xhat_ready = sem("xhat_ready")
        turned = sem("turned")
        turned_out = sem("turned_out")
        proj_ready = sem("proj_ready")
        conv_ready = sem("conv_ready")
        conv_out = sem("conv_out")
        a_weights = sem("a_weights")
        a_ready = sem("a_ready")
        a_max = sem("a_max")
        a_negmax = sem("a_negmax")
        a_read = sem("a_read")
        a_sum = sem("a_sum")
        a_rsum = sem("a_rsum")
        a_vscaled = sem("a_vscaled")
        a_vbiased = sem("a_vbiased")
        a_pv = sem("a_pv")
        a_zout = sem("a_zout")
        qkv_ready = sem("qkv_ready")
        qkv_out = sem("qkv_out")
        q_part = sem("q_part")
        k_part = sem("k_part")
        parts_stored = sem("parts_stored")
        v_biased = sem("v_biased")
        qk_staged = [sem(f"qk_staged{p}") for p in range(2)]
        max_rows = [sem(f"max_rows{p}") for p in range(2)]
        smax_ready = sem("smax_ready")
        smax_done = sem("smax_done")
        m_step = sem("m_step")
        m_ready = sem("m_ready")
        m_turned = sem("m_turned")
        m_copied = sem("m_copied")
        st_ready = sem("st_ready")
        exp_done = sem("exp_done")
        pv_done = sem("pv_done")
        z_copied = sem("z_copied")
        z_stored = [sem(f"z_stored{p}") for p in range(2)]
        z_loaded = sem("z_loaded")
        v_staged = sem("v_staged")
        ctx_ready = sem("ctx_ready")
        logits_ready = sem("logits_ready")
        shifted = sem("shifted")
        gate_exp = sem("gate_exp")
        wgt_ready = sem("wgt_ready")
        wgt_turned = sem("wgt_turned")
        wgt_out = sem("wgt_out")
        b2_ready = sem("b2_ready")
        acc_started = sem("acc_started")
        w_staged = [sem(f"w_staged{p}") for p in range(2)]
        h_ready = sem("h_ready")
        h_out = sem("h_out")
        y_ready = sem("y_ready")
        y_used = sem("y_used")
        final_ready = sem("final_ready")
        stored = sem("stored")

        def bc(ap):
            return ap.partition_broadcast(P)

        EARLY_LOADS = [(wo_a[:, :], t["a_wo"]), (bo_a[:, :], bc(t["a_bo"]))]
        LATE_LOADS = [
            (conv_w, t["conv_w"]), (conv_b[:, :], t["conv_b"]),
            (wqkv[:, 0, :], t["wqkv0"]), (wqkv[:, 1, :], t["wqkv1"]), (wqkv[:, 2, :], t["wqkv2"]),
            (bqk[:, 0, :], t["bqk0"]), (bqk[:, 2, :], t["bqk2"]),
            (bv[:, 0, :], bc(t["bv0"])), (bv[:, 1, :], bc(t["bv2"])),
            (wo[:, 0, :], t["wo0"]), (wo[:, 1, :], t["wo1"]), (wo[:, 2, :], t["wo2"]),
            (bo[:, 0, :], bc(t["bo0"])), (bo[:, 1, :], bc(t["bo2"])),
            (lnrow[:, 0, :], bc(t["ln_b1_g"])), (lnrow[:, 1, :], bc(t["ln_b1_b"])),
            (lnrow[:, 2, :], bc(t["ln_b2_g"])), (lnrow[:, 3, :], bc(t["ln_b2_b"])),
            (lncol[:, :], t["lncol"]),
            (gw[:, 0, 0:E0], t["gate_w0"]), (gw[:, 1, :], t["gate_w1"]),
            (gb[:, 0:E0], bc(t["gate_b"])), (gb[:, E0:10], bc(t["coef_b"])),
            (rank[:, :], bc(t["rank"])),
            (b2s[0:E0, 0, :], t["b2_0"]), (b2s[:, 1, :], t["b2_1"]),
        ]
        N_EARLY, N_LATE = 16 * len(EARLY_LOADS), 16 * len(LATE_LOADS)

        LNCOL = {3: (0, 1), 5: (2, 3), 6: (4, 5)}
        TURN = [(XH, XT), (XH, XT), (CT, CM), (XH, XT), (XH, XT), (XH, XT), (XH, XT)]
        XHAT_OF = {0: 1, 1: 2, 3: 3, 4: 4, 5: 5, 6: 6}
        BLOCKS = [["q", "k", "v"], ["q", "qr", "k", "kr", "v"], ["q", "k", "v"]]
        FIRST_BLOCK = [0, 3, 8]
        QKV_SRC = [CT, XT, XT]
        N_STAGE_DMA = 10

        block = ctx.enter_context(nc.Block())

        @block.sync
        def _(sp):
            sp.dma_start(X[:, :].rearrange("p (t d) -> p t d", d=P),
                         t["x"].rearrange("(t p) d -> p t d", p=P)).then_inc(ld_x, 16)

            def load_pair(n):
                if not (is_int(n) and n == 0):
                    sp.wait_ge(a_vbiased, n)
                at = bass.ds(n, 1)
                sp.dma_start(w_a[:, :], t["a_w"][at].rearrange("a p n -> (a p) n")).then_inc(a_weights, 16)
                sp.dma_start(bqk_a[:, :], t["a_bqk"][at].rearrange("a p n -> (a p) n")).then_inc(a_weights, 16)
                sp.dma_start(bv_a[:, :], t["a_bv"][at].rearrange("a n -> (a n)").partition_broadcast(P)
                             ).then_inc(a_weights, 16)

            load_pair(0)
            for dst, src in EARLY_LOADS:
                sp.dma_start(dst, src).then_inc(ld_early, 16)
            sp.wait_ge(staging_cleared, 1)
            for p in range(2):
                sp.dma_start(KS[p][MROW:MROW + 3, :], t["ones"]).then_inc(ones_loaded, 16)
            with sp.Fori(1, PAIRS) as n:
                load_pair(n)

            def stage(s, h, p):
                at = bass.ds(h, 1)
                q, k = parts_dram[s, 0], parts_dram[s, 1]

                def part(src, a, b):
                    return src[a:b, at].rearrange("n a d t -> (n a) d t")

                for dst, row, src, a, b in [
                        (QS, 0, q, 0, 3), (QS, 3, q, 0, 1), (QS, 4, q, 0, 1), (QS, 5, q, 1, 2),
                        (KS, 0, k, 0, 1), (KS, 1, k, 0, 1), (KS, 2, k, 0, 1), (KS, 3, k, 1, 3), (KS, 5, k, 1, 2)]:
                    sp.dma_start(dst[p][row * DH:(row + b - a) * DH, :], part(src, a, b)
                                 ).then_inc(qk_staged[p], 16)
                sp.dma_start(QS[p][MROW:MROW + 3, :], t["zeros"]).then_inc(qk_staged[p], 16)

            def put_max_rows(g, p):
                sp.wait_ge(m_copied, g + 1)
                for n in range(3):
                    sp.dma_start(QS[p][MROW + n:MROW + n + 1, :], mT[n * NT:(n + 1) * NT, :]
                                 ).then_inc(max_rows[p], 16)

            def store_z(s, h, g, p):
                sp.wait_ge(z_copied, g + 1)
                for c in range(NC):
                    dst = z_dram[s, :, bass.ds(h, 1), :, c * CW:(c + 1) * CW]
                    sp.dma_start(dst.rearrange("z a d t -> z (a d) t"), ZST[32 * c:32 * c + 2 * DH, p, :]
                                 ).then_inc(z_stored[p], 16)

            def experts(layer, n):
                def emit(e, p, k):
                    x = E0 * layer + e
                    if is_int(x) and x < 2:
                        sp.wait_ge(pv_done, NT * H)
                    elif is_int(e) and e < 2:
                        sp.wait_ge(pv_done, NT * H * 3)
                    if not (is_int(e) and e < 2):
                        sp.wait_ge(y_ready, x * NC - NC)
                    at = bass.ds(x, 1)
                    sp.dma_start(W1S[p], t["w1"][at].rearrange("a p n -> (a p) n")).then_inc(w_staged[p], 16)
                    sp.dma_start(W2S[p], t["w2"][at].rearrange("a p n -> (a p) n")).then_inc(w_staged[p], 16)
                    sp.dma_start(B1S[:, p, :], t["b1"][at].rearrange("a p n -> (a p) n")).then_inc(w_staged[p], 16)
                run_experts(sp, n, emit)

            def attention(s):
                for n in range(3):
                    sp.wait_ge(q_part, 3 * s + n + 1)
                    sp.dma_start(parts_dram[s, 0, n], PARTS[0][:, n * S:(n + 1) * S]).then_inc(parts_stored, 16)
                for n in range(3):
                    sp.wait_ge(k_part, 3 * s + n + 1)
                    sp.dma_start(parts_dram[s, 1, n], PARTS[1][:, n * S:(n + 1) * S]).then_inc(parts_stored, 16)
                sp.wait_ge(parts_stored, 96 * (s + 1))
                stage(s, 0, 0)
                stage(s, 1, 1)
                put_max_rows(H * s, 0)

                def emit(h, p, k):
                    g = H * s + h
                    first, last = is_int(h) and h == 0, is_int(h) and h == H - 1
                    if not first and not last:
                        sp.wait_ge(st_ready, g * NC * NT)
                        stage(s, h + 1, 1 - p)
                    if not first:
                        store_z(s, h - 1, g - 1, 1 - p)
                    if not last:
                        put_max_rows(g + 1, 1 - p)
                    if last:
                        store_z(s, h, g, p)
                run_heads(sp, emit)
                for p in range(2):
                    sp.wait_ge(z_stored[p], 16 * NC * (H // 2) * (s + 1))
                sp.dma_start(ZT, z_dram[s, 0].rearrange("h d t -> (h d) t")).then_inc(z_loaded, 16)
                sp.dma_start(ZS, z_dram[s, 1].rearrange("h d t -> (h d) t")).then_inc(z_loaded, 16)

            sp.wait_ge(proj_ready, 4)
            for dst, src in LATE_LOADS:
                sp.dma_start(dst, src).then_inc(ld_late, 16)
            attention(0)
            experts(0, E0)
            sp.dma_start(COS, t["cos"]).then_inc(tables_loaded, 16)
            sp.dma_start(SIN, t["sin"]).then_inc(tables_loaded, 16)
            attention(1)
            attention(2)
            experts(1, E1)
            sp.wait_ge(final_ready, 1)
            sp.dma_start(out.rearrange("(t p) d -> p t d", p=P),
                         X[:, :].rearrange("p (t d) -> p t d", d=P)).then_inc(stored, 16)
            sp.wait_ge(stored, 16)

        @block.gpsimd
        def _(pool):
            steps = [0]

            def step(ins):
                ins.then_inc(pool_step, 1)
                steps[0] += 1
                pool.wait_ge(pool_step, steps[0])

            pool.memset(XTp[:, 0:1], 0.0)
            pool.memset(XTp[:, S + 1:S + 2], 0.0)
            pool.memset(ident[:, :], 0.0)
            pool.memset(identb[:, :], 0.0)
            step(pool.memset(maskb[:, :], 0.0))
            pool.affine_select(out=ident[:, :], in_=ident[:, :], compare_op=ALU.not_equal, fill=1.0,
                               base=0, pattern=[[-1, P]], channel_multiplier=1)
            pool.affine_select(out=identb[:, :], in_=identb[:, :], compare_op=ALU.not_equal, fill=1.0,
                               base=0, pattern=[[-1, P]], channel_multiplier=1)
            pool.affine_select(out=maskb[:, :], in_=maskb[:, :], compare_op=ALU.is_ge, fill=MASKED,
                               base=0, pattern=[[1, P]], channel_multiplier=-1).then_inc(consts_made, 1)
            for p in range(2):
                pool.memset(QS[p][:, :], 0.0)
                pool.memset(KS[p][:, :], 0.0)
            pool.memset(mb[:, :], 0.0)
            pool.memset(VS[:, :, :, :], 1.0).then_inc(staging_cleared, 1)
            pool.wait_ge(staging_cleared, 1)
            def bias_v(pair, p, count):
                pool.wait_ge(a_read, count)
                v = VA[p].rearrange("p (t d) -> p t d", d=P)
                pool.tensor_tensor(v, v, bv_a[:, :].unsqueeze(1).broadcast_to([P, NT, P]), ALU.add
                                   ).then_inc(a_vbiased, 1)

            pool.wait_ge(a_weights, 48)
            bias_v(0, 0, PROJ)

            def emit_pair(pair, p):
                if is_int(pair) and pair == PAIRS - 1:
                    return
                bias_v(pair + 1, 1 - p, PROJ + pair * PER_PAIR + PER_PAIR)
            run_pairs(pool, emit_pair)

            def attention(s):
                first = 4 * FIRST_BLOCK[s]
                names = BLOCKS[s]
                k_at = first + 4 * (names.index("k") + 1)
                kr_at = first + 4 * (names.index("kr") + 1) if "kr" in names else 0
                pool.wait_ge(qkv_out, max(k_at, kr_at))
                if s == 1:
                    pool.wait_ge(tables_loaded, 32)
                    step(pool.tensor_tensor(T[2], T[2], COS, ALU.mult))
                    step(pool.tensor_tensor(T[3], T[3], SIN, ALU.mult))
                    step(pool.tensor_tensor(T[2], T[2], T[3], ALU.add))
                hi, mid, lo = (PARTS[1][:, n * S:(n + 1) * S] for n in range(3))
                if s:
                    pool.wait_ge(parts_stored, 96 * s)
                pool.tensor_copy(hi, T[2]).then_inc(k_part, 1)
                pool.wait_ge(k_part, 3 * s + 1)
                step(pool.tensor_tensor(T[2], T[2], hi, ALU.subtract))
                pool.tensor_copy(mid, T[2]).then_inc(k_part, 1)
                pool.wait_ge(k_part, 3 * s + 2)
                pool.tensor_tensor(lo, T[2], mid, ALU.subtract).then_inc(k_part, 1)
                pool.wait_ge(ld_late, N_LATE)
                pool.wait_ge(qkv_out, first + 4 * len(names))
                if s != 1:
                    v = VALL[:, :].rearrange("p (t d) -> p t d", d=P)
                    pool.tensor_tensor(v, v, bv[:, s // 2, :].unsqueeze(1).broadcast_to([P, NT, P]), ALU.add
                                       ).then_inc(v_biased, 1)
                    pool.wait_ge(v_biased, s // 2 + 1)

                def emit(h, p, k):
                    g = H * s + h
                    if not is_int(g) or g >= 2:
                        pool.wait_ge(pv_done, (g - 1) * NT)
                    src = VALL[:, :].rearrange("p (t d) -> p t d", d=P)[:, :, bass.ds(h * DH, DH)]
                    pool.tensor_copy(VS[:, p, :, 0:DH], src).then_inc(v_staged, 1)
                run_heads(pool, emit)

            attention(0)
            pool.wait_ge(ld_late, N_LATE)
            src = wqkv[:, 1, 0:2 * P].rearrange("p (n two) -> p n two", two=2)
            dst = wrot.rearrange("p (n two) -> p n two", two=2)
            pool.tensor_scalar(dst[:, :, 0], src[:, :, 1], -1.0, None, ALU.mult)
            pool.tensor_copy(dst[:, :, 1], src[:, :, 0]).then_inc(wrot_made, 1)
            attention(1)
            attention(2)

        @block.scalar
        def _(act):
            def copy(out_, in_, bias=0.0, scale=1.0):
                return act.activation(out_, in_, ACT.Identity, bias=bias, scale=scale)

            def root(n):
                act.wait_ge(var_ready, n)
                act.activation(std[:, :], var[:, :], ACT.Sqrt).then_inc(std_ready, 1)

            def turn_out(k):
                bias, scale = 0.0, 1.0
                if k in LNCOL:
                    g, b = LNCOL[k]
                    act.wait_ge(ld_late, N_LATE)
                    scale, bias = lncol[:, g:g + 1], lncol[:, b:b + 1]
                for b_ in range(4):
                    act.wait_ge(turned, 4 * k + b_ + 1)
                    copy(TURN[k][1][:, b_ * CW:(b_ + 1) * CW], ps[:, b_, :], bias, scale).then_inc(turned_out, 1)

            def project_out(n, j, p):
                kind, c = n // NC, n % NC
                dst = (QT, KT, VA)[kind][p][:, c * CW:(c + 1) * CW]
                bias = bqk_a[:, kind:kind + 1] if kind < 2 else 0.0
                copy(dst, ps[:, j % RING, :], bias).then_inc(a_read, 1)

            root(1)
            root(2)
            turn_out(0)
            act.wait_ge(a_weights, 48)
            for n in range(PROJ):
                act.wait_ge(a_ready, n + 1)
                project_out(n, n, 0)

            def z_out(head, pair, hh):
                act.wait_ge(a_pv, (head + 1) * NT)
                for c in range(NC):
                    ins = copy(ZA[AD * hh:AD * hh + AD, bass.ds(pair * S + c * CW, CW)],
                               ps[AD * (c % 2):AD * (c % 2) + AD, 6 + c // 2, :])
                ins.then_inc(a_zout, 1)

            def emit_pair(pair, p):
                first, last = is_int(pair) and pair == 0, is_int(pair) and pair == PAIRS - 1
                for r, (hh, i) in enumerate(ROWS):
                    R = pair * 2 * NT + r
                    j, n, after = (LAST_PLAN if last else PLAN)[r]
                    if i == LAG and not (first and hh == 0):
                        if hh:
                            z_out(pair * 2, pair, 0)
                        else:
                            z_out(pair * 2 - 1, pair - 1, 1)
                    act.wait_ge(a_negmax, R + 1)
                    if not (first and r < 4):
                        act.wait_ge(a_pv, R - 3)
                    for ci, (c, off) in enumerate(row_chunks(i)):
                        act.activation(probs[:, r % 4, c * CW + off:(c + 1) * CW], ps[:, (j + ci) % RING, off:],
                                       ACT.Exp, bias=anm[:, r % 4:r % 4 + 1],
                                       accum_out=als[:, r % 4, ci:ci + 1]).then_inc(a_read, 1)
                    if after is not None:
                        if r == PROJ_FROM:
                            act.wait_ge(a_weights, pair * 48 + 96)
                        act.wait_ge(a_ready, PROJ + pair * PER_PAIR + after + 1)
                        project_out(r - PROJ_FROM, after, 1 - p)
                if last:
                    z_out(PAIRS * 2 - 1, PAIRS - 1, 1)
            run_pairs(act, emit_pair)

            def conv():
                for c in range(NC):
                    act.wait_ge(conv_ready, c + 1)
                    copy(CT[:, c * CW:(c + 1) * CW], ps[:, 4 + c, :], conv_b[:, 0:1]).then_inc(conv_out, 1)

            def qkv(s):
                if s:
                    act.wait_ge(v_staged, H * s)
                for n, name in enumerate(BLOCKS[s]):
                    b = FIRST_BLOCK[s] + n
                    dst = {"q": T[0], "qr": T[1], "k": T[2], "kr": T[3], "v": VALL[:, :]}[name]
                    bias = 0.0
                    if s != 1 and name in "qk":
                        bias = bqk[:, s, "qk".index(name):"qk".index(name) + 1]
                    for c in range(NC):
                        act.wait_ge(qkv_ready, 4 * b + c + 1)
                        copy(dst[:, c * CW:(c + 1) * CW], ps[:, 4 * (b % 2) + c, :], bias).then_inc(qkv_out, 1)

            def attention(s):
                def z_copy(g, p, k):
                    act.wait_ge(pv_done, (g + 1) * NT)
                    if not (is_int(g) and g < 2):
                        act.wait_ge(z_stored[p], (k + 8 * s) * 16 * NC)
                    copy(ZST[:, p, :], ps[:, 6, :]).then_inc(z_copied, 1)

                def emit(h, p, k):
                    g = H * s + h
                    first, last = is_int(h) and h == 0, is_int(h) and h == H - 1
                    for kt in range(NT):
                        if not (is_int(g) and g == 0 and kt < 4):
                            act.wait_ge(pv_done, g * NT + kt - 3)
                        for c in range(NC):
                            act.wait_ge(st_ready, g * NT * NC + kt * NC + c + 1)
                            act.activation(probs[:, kt % 4, c * CW:(c + 1) * CW], ps[:, 4 + c % 2, :],
                                           ACT.Exp, scale=SCALE).then_inc(exp_done, 1)
                        if kt == 0 and not first:
                            z_copy(g - 1, 1 - p, k if p else k - 1)
                    if last:
                        z_copy(g, p, k)
                run_heads(act, emit)

            def mixture(layer, n):
                act.wait_ge(shifted, layer + 1)
                if layer:
                    act.activation(ge[:, :, :], gl[:, :, :], ACT.Exp).then_inc(gate_exp, 1)
                else:
                    act.activation(ge[:, :, 0:E0], gl[:, :, 0:E0], ACT.Exp).then_inc(gate_exp, 1)
                for b_ in range(4):
                    act.wait_ge(wgt_turned, 4 * layer + b_ + 1)
                    copy(WT[0:n, b_ * CW:(b_ + 1) * CW], ps[0:n, b_, :]).then_inc(wgt_out, 1)

                def emit(e, p, k):
                    act.wait_ge(w_staged[p], (k + 4 * layer + 1) * 48)
                    for c in range(NC):
                        chunk = (e + E0 * layer) * NC + c
                        if not (is_int(e) and e == 0 and layer == 0 and c < 2):
                            act.wait_ge(y_ready, chunk - 1)
                        for f in range(FC):
                            act.wait_ge(h_ready, chunk * FC + f + 1)
                            act.activation(HT[c % 2][:, f * CW:(f + 1) * CW], ps[:, f, :],
                                           ACT.Gelu if layer else ACT.Relu,
                                           bias=B1S[:, p, f:f + 1]).then_inc(h_out, 1)
                run_experts(act, n, emit)

            act.wait_ge(ld_late, N_LATE)
            root(3)
            root(4)
            turn_out(1)
            conv()
            turn_out(2)
            qkv(0)
            attention(0)
            root(5)
            turn_out(3)
            mixture(0, E0)
            root(6)
            root(7)
            root(8)
            turn_out(4)
            qkv(1)
            attention(1)
            root(9)
            root(10)
            root(11)
            turn_out(5)
            qkv(2)
            attention(2)
            root(12)
            turn_out(6)
            mixture(1, E1)
            root(13)

        @block.tensor
        def _(pe):
            def mm(out_, lhsT, rhs, start=True, stop=True):
                return pe.matmul(out_, lhsT, rhs, start=start, stop=stop, skip_group_check=True)

            def turn(k):
                if k == 2:
                    pe.wait_ge(conv_out, 4)
                else:
                    pe.wait_ge(xhat_ready, XHAT_OF[k])
                if k >= 1:
                    pe.wait_ge(turned_out, 4 * k)
                src = TURN[k][0]
                for n in range(NT):
                    ins = pe.transpose(ps[:, n // TPC, (n % TPC) * P:(n % TPC + 1) * P],
                                       src[:, n * P:(n + 1) * P], ident[:, :])
                    if n % TPC == TPC - 1:
                        ins.then_inc(turned, 1)

            def project(n, j, p):
                kind, c = n // NC, n % NC
                bank = ps[:, j % RING, :]
                w = w_a[:, kind * P:(kind + 1) * P]
                if kind < 2:
                    return mm(bank, w, XT[:, c * CW:(c + 1) * CW])
                for m in range(TPC):
                    tok = (c * TPC + m) * P
                    ins = mm(bank[:, m * P:(m + 1) * P], XT[:, tok:tok + P], w)
                return ins

            pe.wait_ge(consts_made, 1)
            turn(0)
            pe.wait_ge(turned_out, 4)
            pe.wait_ge(a_weights, 48)
            for n in range(PROJ):
                if n >= RING:
                    pe.wait_ge(a_read, n - RING + 1)
                project(n, n, 0).then_inc(a_ready, 1)

            def pv(pair, r, p):
                hh, i = ROWS[r]
                R = pair * 2 * NT + r
                pe.wait_ge(a_vscaled, R + 1)
                if i == 0 and not (is_int(pair) and pair == 0 and hh == 0):
                    pe.wait_ge(a_zout, pair * 2 + hh)
                for c, off in row_chunks(i):
                    ins = mm(ps[AD * (c % 2):AD * (c % 2) + AD, 6 + c // 2, off:], VR[:, r % 4, :],
                             probs[:, r % 4, c * CW + off:(c + 1) * CW], start=(i == 0), stop=(i == 4 * c + 3))
                ins.then_inc(a_pv, 1)

            def emit_pair(pair, p):
                first, last = is_int(pair) and pair == 0, is_int(pair) and pair == PAIRS - 1
                pe.wait_ge(a_read, pair * PER_PAIR + PROJ - 0)
                for r, (hh, i) in enumerate(ROWS):
                    j, n, after = (LAST_PLAN if last else PLAN)[r]
                    half = slice(AD * hh, AD * hh + AD)
                    for ci, (c, off) in enumerate(row_chunks(i)):
                        jj = j + ci
                        pe.wait_ge(a_read, ring_user_before(pair, jj))
                        bank = ps[:, jj % RING, :]
                        diagonal = c == i // TPC
                        ins = mm(bank[:, off:], KT[p][half, i * P:(i + 1) * P],
                                 QT[p][half, c * CW + off:(c + 1) * CW], stop=not diagonal)
                        if diagonal:
                            ins = mm(bank[:, off:off + P], identb[:, :], maskb[:, :], start=False)
                        ins.then_inc(a_ready, 1)
                    if after is not None:
                        if r == PROJ_FROM:
                            pe.wait_ge(a_weights, pair * 48 + 96)
                        pe.wait_ge(a_read, ring_user_before(pair, after))
                        project(r - PROJ_FROM, after, 1 - p).then_inc(a_ready, 1)
                    if r >= LAG:
                        pv(pair, r - LAG, p)
                    elif not first:
                        pv(pair - 1, r - LAG + 2 * NT, 1 - p)
                if last:
                    pv(pair, 2 * NT - 2, p)
                    pv(pair, 2 * NT - 1, p)
            run_pairs(pe, emit_pair)

            def project_tokens(k, src_ready, parts):
                src_ready()
                for n in range(NT):
                    for m, (lhs, rhs) in enumerate(parts):
                        ins = mm(ps[:, n // TPC, (n % TPC) * P:(n % TPC + 1) * P], lhs[:, n * P:(n + 1) * P],
                                 rhs, start=(m == 0), stop=(m == len(parts) - 1))
                    if n % TPC == TPC - 1:
                        ins.then_inc(proj_ready, 1)

            def heads_out():
                pe.wait_ge(a_zout, 2 * PAIRS)
                pe.wait_ge(ld_early, N_EARLY)
            project_tokens(0, heads_out, [(ZA[:, n * S:(n + 1) * S], wo_a[:, n * P:(n + 1) * P])
                                          for n in range(PAIRS)])

            def conv():
                pe.wait_ge(turned_out, 8)
                pe.wait_ge(ld_late, N_LATE)
                for c in range(NC):
                    for j in range(3):
                        ins = mm(ps[:, 4 + c, :], conv_w[:, j * P:(j + 1) * P], XTp[:, c * CW + j:c * CW + j + CW],
                                 start=(j == 0), stop=(j == 2))
                    ins.then_inc(conv_ready, 1)

            def qkv(s, turned_before):
                pe.wait_ge(turned_out, turned_before)
                if s == 1:
                    pe.wait_ge(wrot_made, 1)
                src = QKV_SRC[s]
                for n, name in enumerate(BLOCKS[s]):
                    b = FIRST_BLOCK[s] + n
                    if n >= 2:
                        pe.wait_ge(qkv_out, 4 * (b - 1))
                    w = {"q": wqkv[:, s, 0:P], "k": wqkv[:, s, P:2 * P], "v": wqkv[:, s, 2 * P:],
                         "qr": wrot[:, 0:P], "kr": wrot[:, P:]}[name]
                    for c in range(NC):
                        bank = ps[:, 4 * (b % 2) + c, :]
                        if name != "v":
                            ins = mm(bank, w, src[:, c * CW:(c + 1) * CW])
                        else:
                            for m in range(TPC):
                                tok = (c * TPC + m) * P
                                ins = mm(bank[:, m * P:(m + 1) * P], src[:, tok:tok + P], w)
                        ins.then_inc(qkv_ready, 1)

            def attention(s):
                def max_scores(g, p, q, js):
                    for j in js:
                        half = j // 2
                        if j % 2 == 0:
                            u = g * 2 * NT + 2 * q + half
                            if not (is_int(u) and u < 2):
                                pe.wait_ge(smax_done, u - 1)
                        ins = mm(ps[:, 2 * half + j % 2, :], QS[p][:, q * P:(q + 1) * P],
                                 KS[p][:, j * CW:(j + 1) * CW])
                        if j % 2:
                            ins.then_inc(smax_ready, 1)

                def turn_max(g):
                    pe.wait_ge(m_ready, g + 1)
                    pe.transpose(ps[:, MISC, 0:P // 2].bitcast(BF16), mb[:, :], identb[:, :]
                                 ).then_inc(m_turned, 1)

                def pv(g, p, kt):
                    pe.wait_ge(exp_done, g * NT * NC + kt * NC + NC)
                    if kt == 0 and not (is_int(g) and g == 0):
                        pe.wait_ge(z_copied, g)
                    for c in range(NC):
                        ins = mm(ps[32 * c:32 * c + VC, 6, :], VS[:, p, kt, :],
                                 probs[:, kt % 4, c * CW:(c + 1) * CW], start=(kt == 0), stop=(kt == NT - 1))
                    ins.then_inc(pv_done, 1)

                pe.wait_ge(qkv_out, 4 * (FIRST_BLOCK[s] + len(BLOCKS[s])))
                pe.wait_ge(ones_loaded, 32)
                pe.wait_ge(qk_staged[0], 16 * N_STAGE_DMA * (8 * s + 1))
                for q in range(NT):
                    max_scores(H * s, 0, q, range(NC))
                turn_max(H * s)

                def emit(h, p, k):
                    g = H * s + h
                    first, last = is_int(h) and h == 0, is_int(h) and h == H - 1
                    kn = k + 1 if p else k
                    pe.wait_ge(max_rows[p], (k + 8 * s + 1) * 48)
                    pe.wait_ge(v_staged, g + 1)
                    for kt in range(NT):
                        extra = [] if last else [(q, j) for q in MAX_TILES[kt] for j in range(NC)]
                        if kt == 1 and not last:
                            pe.wait_ge(qk_staged[1 - p], (kn + 8 * s + 1) * 16 * N_STAGE_DMA)
                        for c in range(NC):
                            for q, j in extra[c * len(extra) // NC:(c + 1) * len(extra) // NC]:
                                max_scores(g + 1, 1 - p, q, [j])
                            chunk = g * NT * NC + kt * NC + c
                            if not (is_int(chunk) and chunk < 2):
                                pe.wait_ge(exp_done, chunk - 1)
                            mm(ps[:, 4 + c % 2, :], KS[p][:, kt * P:(kt + 1) * P],
                               QS[p][:, c * CW:(c + 1) * CW]).then_inc(st_ready, 1)
                            if c == 1:
                                if kt:
                                    pv(g, p, kt - 1)
                                elif not first:
                                    pv(g - 1, 1 - p, NT - 1)
                    if not last:
                        turn_max(g + 1)
                    if last:
                        pv(g, p, NT - 1)
                run_heads(pe, emit)

            def mixture(layer, n, turned_before):
                pe.wait_ge(turned_out, turned_before)
                width = 10 if layer else E0
                for m in range(NT):
                    ins = mm(ps[:, 4, m * 16:m * 16 + width], XT[:, m * P:(m + 1) * P], gw[:, layer, 0:width])
                ins.then_inc(logits_ready, 1)
                pe.wait_ge(wgt_ready, layer + 1)
                for m in range(NT):
                    ins = pe.transpose(ps[0:n, m // TPC, (m % TPC) * P:(m % TPC + 1) * P], wgt[:, 0:n, m],
                                       ident[:, :])
                    if m % TPC == TPC - 1:
                        ins.then_inc(wgt_turned, 1)
                for m in range(NT):
                    if m % TPC == 0:
                        pe.wait_ge(wgt_out, 4 * layer + m // TPC + 1)
                    ins = mm(ps[:, 4 + m // TPC, (m % TPC) * P:(m % TPC + 1) * P], WT[0:n, m * P:(m + 1) * P],
                             b2s[0:n, layer, :])
                    if m % TPC == TPC - 1:
                        ins.then_inc(b2_ready, 1)
                pe.wait_ge(acc_started, layer + 1)

                def down(e, p, c):
                    chunk = (e + E0 * layer) * NC + c
                    pe.wait_ge(h_out, chunk * FC + FC)
                    if not (is_int(chunk) and chunk < 2):
                        pe.wait_ge(y_used, chunk - 1)
                    for m in range(TPC):
                        for f in range(FC):
                            ins = mm(ps[:, 4 + c % 2, m * P:(m + 1) * P],
                                     HT[c % 2][:, f * CW + m * P:f * CW + (m + 1) * P],
                                     W2S[p][:, f * P:(f + 1) * P], start=(f == 0), stop=(f == FC - 1))
                    ins.then_inc(y_ready, 1)

                def emit(e, p, k):
                    pe.wait_ge(w_staged[p], (k + 4 * layer + 1) * 48)
                    for c in range(NC):
                        for f in range(FC):
                            unit = ((e + E0 * layer) * NC + c) * FC + f
                            if not (is_int(unit) and unit < FC):
                                pe.wait_ge(h_out, unit - FC + 1)
                            mm(ps[:, f, :], W1S[p][:, f * P:(f + 1) * P], XT[:, c * CW:(c + 1) * CW]
                               ).then_inc(h_ready, 1)
                        if c:
                            down(e, p, c - 1)
                        elif not (is_int(e) and e == 0):
                            down(e - 1, 1 - p, NC - 1)
                run_experts(pe, n, emit)
                down(n - 1, (n - 1) % 2, NC - 1)

            def ctx_is_ready(k):
                return lambda: pe.wait_ge(ctx_ready, k)

            turn(1)
            conv()
            turn(2)
            qkv(0, 12)
            attention(0)
            project_tokens(1, ctx_is_ready(1), [(ZT, wo[:, 0, :])])
            turn(3)
            mixture(0, E0, 16)
            turn(4)
            qkv(1, 20)
            attention(1)
            project_tokens(2, ctx_is_ready(2), [(ZT, wo[:, 1, :])])
            turn(5)
            qkv(2, 24)
            attention(2)
            project_tokens(3, ctx_is_ready(3), [(ZT, wo[:, 2, :])])
            turn(6)
            mixture(1, E1, 28)

        @block.vector
        def _(dve):
            steps = [0]
            roots = [0]

            def step(ins):
                ins.then_inc(dve_step, 1)
                steps[0] += 1
                dve.wait_ge(dve_step, steps[0])

            def tiles(a):
                return a.rearrange("p (t d) -> p t d", d=P)

            def tile(a, n):
                return a[:, n * P:(n + 1) * P]

            def moments(src):
                for n in range(NT):
                    ins = dve.bn_stats(stats[:, n, :], tile(src, n))
                step(ins)
                for n in range(NT):
                    ins = dve.bn_aggr(mv[:, n, :], stats[:, n, :])
                step(ins)

            def inverse_root():
                roots[0] += 1
                dve.wait_ge(std_ready, roots[0])
                step(dve.reciprocal(rstd[:, :], std[:, :]))

            def layer_norm(src, dst):
                moments(src)
                dve.tensor_scalar(var[:, :], mv[:, :, 1], EPS, None, ALU.add).then_inc(var_ready, 1)
                inverse_root()
                for n in range(NT):
                    ins = dve.tensor_scalar(tile(dst, n), tile(src, n), mv[:, n, 0:1], rstd[:, n:n + 1],
                                            ALU.subtract, ALU.mult)
                step(ins)

            def rms_norm(a):
                moments(a)
                step(dve.tensor_tensor(var[:, :], mv[:, :, 0], mv[:, :, 0], ALU.mult))
                step(dve.tensor_tensor(var[:, :], var[:, :], mv[:, :, 1], ALU.add))
                dve.tensor_scalar(var[:, :], var[:, :], RMS_EPS, None, ALU.add).then_inc(var_ready, 1)
                inverse_root()
                for n in range(NT):
                    ins = dve.tensor_scalar(tile(a, n), tile(a, n), rstd[:, n:n + 1], None, ALU.mult)
                step(ins)

            def along(row, n=NT):
                return row.unsqueeze(1).broadcast_to([P, n, P])

            def projected(k, dst, bias):
                for b in range(4):
                    dve.wait_ge(proj_ready, 4 * k + b + 1)
                    d = dst[:, b * CW:(b + 1) * CW]
                    if bias is None:
                        ins = dve.tensor_copy(d, ps[:, b, :])
                    else:
                        ins = dve.tensor_tensor(tiles(d), tiles(ps[:, b, :]), along(bias, TPC), ALU.add)
                step(ins)

            def add(dst, a, b):
                step(dve.tensor_tensor(dst, a, b, ALU.add))

            def xhat():
                dve.sem_inc(xhat_ready, 1)

            x, xh, y = X[:, :], XH[:, :], Y[:, :]
            dve.wait_ge(staging_cleared, 1)
            dve.wait_ge(ld_x, 16)
            layer_norm(x, xh)
            rms_norm(xh)
            xhat()

            def normalise(pair, r, p, plan=PLAN):
                hh, i = ROWS[r]
                R = pair * 2 * NT + r
                j, n, _ = plan[r]
                dve.wait_ge(a_read, pair * PER_PAIR + PROJ + j + n)
                q = r % 4
                dve.tensor_reduce(asum[:, q:q + 1], als[:, q, 0:n], X_AXIS, ALU.add).then_inc(a_sum, 1)
                dve.wait_ge(a_sum, R + 1)
                dve.reciprocal(arl[:, q:q + 1], asum[:, q:q + 1]).then_inc(a_rsum, 1)
                dve.wait_ge(a_rsum, R + 1)
                if not (is_int(R) and R < 4):
                    dve.wait_ge(a_pv, R - 3)
                dve.tensor_scalar(VR[:, q, :], VA[p][:, i * P + AD * hh:i * P + AD * hh + AD], arl[:, q:q + 1],
                                  None, ALU.mult).then_inc(a_vscaled, 1)

            def emit_pair(pair, p):
                first, last = is_int(pair) and pair == 0, is_int(pair) and pair == PAIRS - 1
                maxima = 0
                for r, (hh, i) in enumerate(ROWS):
                    R = pair * 2 * NT + r
                    j, n, _ = (LAST_PLAN if last else PLAN)[r]
                    q = r % 4
                    for ci, (c, off) in enumerate(row_chunks(i)):
                        dve.wait_ge(a_ready, pair * PER_PAIR + PROJ + j + ci + 1)
                        if n == 1:
                            dve.tensor_reduce(anm[:, q:q + 1], ps[:, (j + ci) % RING, off:], X_AXIS, ALU.max,
                                              negate=True).then_inc(a_negmax, 1)
                        else:
                            dve.tensor_reduce(amx[:, q, ci:ci + 1], ps[:, (j + ci) % RING, off:], X_AXIS, ALU.max
                                              ).then_inc(a_max, 1)
                            maxima += 1
                    if n > 1:
                        dve.wait_ge(a_max, pair * MAXIMA + maxima)
                        dve.tensor_reduce(anm[:, q:q + 1], amx[:, q, 0:n], X_AXIS, ALU.max, negate=True
                                          ).then_inc(a_negmax, 1)
                    if r == 0:
                        dve.wait_ge(a_vbiased, pair + 1)
                    if r:
                        normalise(pair, r - 1, p, LAST_PLAN if last else PLAN)
                    elif not first:
                        normalise(pair - 1, 2 * NT - 1, 1 - p)
                if last:
                    normalise(pair, 2 * NT - 1, p, LAST_PLAN)
            MAXIMA = 2 * sum(len(row_chunks(i)) for i in range(NT) if len(row_chunks(i)) > 1)
            run_pairs(dve, emit_pair)

            dve.wait_ge(ld_early, N_EARLY)
            dve.wait_ge(a_pv, 2 * NT * PAIRS)
            projected(0, y, bo_a[:, :])
            layer_norm(y, xh)
            add(x, x, xh)
            layer_norm(x, xh)
            xhat()

            dve.wait_ge(ld_late, N_LATE)

            def split_q(s):
                first = 4 * FIRST_BLOCK[s]
                dve.wait_ge(qkv_out, first + (8 if s == 1 else 4))
                if s == 1:
                    dve.wait_ge(tables_loaded, 32)
                    step(dve.tensor_tensor(T[0], T[0], COS, ALU.mult))
                    step(dve.tensor_tensor(T[1], T[1], SIN, ALU.mult))
                    step(dve.tensor_tensor(T[0], T[0], T[1], ALU.add))
                if s:
                    dve.wait_ge(parts_stored, 96 * s)
                hi, mid, lo = (PARTS[0][:, n * S:(n + 1) * S] for n in range(3))
                dve.tensor_copy(hi, T[0]).then_inc(q_part, 1)
                dve.wait_ge(q_part, 3 * s + 1)
                step(dve.tensor_tensor(T[0], T[0], hi, ALU.subtract))
                dve.tensor_copy(mid, T[0]).then_inc(q_part, 1)
                dve.wait_ge(q_part, 3 * s + 2)
                dve.tensor_tensor(lo, T[0], mid, ALU.subtract).then_inc(q_part, 1)

            def attention(s):
                def maxima(g):
                    for q in range(NT):
                        for half in range(2):
                            dve.wait_ge(smax_ready, g * 2 * NT + 2 * q + half + 1)
                            dve.tensor_reduce(mx[:, q, half:half + 1],
                                              ps[:, 2 * half:2 * half + 2, :].rearrange("p b n -> p (b n)"),
                                              X_AXIS, ALU.max).then_inc(smax_done, 1)
                    dve.wait_ge(smax_done, g * 2 * NT + 2 * NT)
                    dve.tensor_reduce(nm[:, :], mx[:, :, :], X_AXIS, ALU.max, negate=True).then_inc(m_step, 1)
                    dve.wait_ge(m_step, g * 4 + 1)
                    dve.tensor_copy(mb[:, 0:NT], nm[:, :]).then_inc(m_step, 1)
                    dve.wait_ge(m_step, g * 4 + 2)
                    dve.tensor_tensor(nr[:, :], nm[:, :], mb[:, 0:NT], ALU.subtract).then_inc(m_step, 1)
                    dve.wait_ge(m_step, g * 4 + 3)
                    dve.tensor_copy(mb[:, NT:2 * NT], nr[:, :]).then_inc(m_step, 1)
                    dve.wait_ge(m_step, g * 4 + 4)
                    dve.tensor_tensor(mb[:, 2 * NT:3 * NT], nr[:, :], mb[:, NT:2 * NT], ALU.subtract).then_inc(m_ready, 1)

                def copy_rows(g, before):
                    dve.wait_ge(m_turned, g + 1)
                    if before:
                        dve.wait_ge(*before)
                    dve.tensor_copy(mT[:, :], ps[0:3 * NT, MISC, 0:P // 2].bitcast(BF16)).then_inc(m_copied, 1)

                maxima(H * s)
                copy_rows(H * s, (max_rows[1], 48 * 8 * s) if s else None)

                def emit(h, p, k):
                    g = H * s + h
                    if is_int(h) and h == H - 1:
                        return
                    maxima(g + 1)
                    copy_rows(g + 1, (max_rows[p], (k + 8 * s + 1) * 48))
                run_heads(dve, emit)
                dve.wait_ge(z_loaded, 32 * (s + 1))
                step(dve.reciprocal(ZS, ZS))
                dve.tensor_tensor(ZT, ZT, ZS, ALU.mult).then_inc(ctx_ready, 1)

            def gates(layer):
                dve.wait_ge(logits_ready, layer + 1)
                raw = ps[:, 4, 0:NT * 16].rearrange("p (t e) -> p t e", e=16)
                L, G = gl[:, :, 0:E0], ge[:, :, 0:E0]

                def wide(a, n=E0):
                    return a.unsqueeze(2).broadcast_to([P, NT, n])

                if layer:
                    dve.tensor_copy(L, raw[:, :, 0:E0])
                    step(dve.tensor_tensor(gl[:, :, E0:10], raw[:, :, E0:10],
                                           gb[:, E0:10].unsqueeze(1).broadcast_to([P, NT, 2]), ALU.add))
                else:
                    step(dve.tensor_tensor(L, raw[:, :, 0:E0], gb[:, 0:E0].unsqueeze(1).broadcast_to([P, NT, E0]),
                                           ALU.add))
                step(dve.tensor_reduce(gm[:, :], L, X_AXIS, ALU.max))
                if layer:
                    step(dve.tensor_reduce(g2[:, :], gl[:, :, E0:10], X_AXIS, ALU.max))
                    step(dve.tensor_tensor(gl[:, :, E0:10], gl[:, :, E0:10], wide(g2[:, :], 2), ALU.subtract))
                dve.tensor_tensor(L, L, wide(gm[:, :]), ALU.subtract).then_inc(shifted, 1)
                dve.wait_ge(gate_exp, layer + 1)
                step(dve.tensor_reduce(gs[:, :], G, X_AXIS, ALU.add))
                step(dve.reciprocal(gs[:, :], gs[:, :]))
                if not layer:
                    dve.tensor_tensor(WPE[:, :, 0:E0], G, wide(gs[:, :]), ALU.mult).then_inc(wgt_ready, 1)
                    return
                step(dve.tensor_tensor(gp[:, :, :], G, wide(gs[:, :]), ALU.mult))
                step(dve.tensor_reduce(gm[:, :], gp[:, :, :], X_AXIS, ALU.max))
                step(dve.tensor_tensor(gp[:, :, :], gp[:, :, :], wide(gm[:, :]), ALU.is_equal))
                step(dve.tensor_tensor(gp[:, :, :], gp[:, :, :], rank[:, :].unsqueeze(1).broadcast_to([P, NT, E0]),
                                       ALU.mult))
                step(dve.tensor_reduce(g2[:, :], gp[:, :, :], X_AXIS, ALU.max))
                step(dve.tensor_tensor(gp[:, :, :], gp[:, :, :], wide(g2[:, :]), ALU.is_equal))
                step(dve.tensor_reduce(gs[:, :], ge[:, :, E0:10], X_AXIS, ALU.add))
                step(dve.reciprocal(gs[:, :], gs[:, :]))
                step(dve.tensor_tensor(ge[:, :, E0:10], ge[:, :, E0:10], wide(gs[:, :], 2), ALU.mult))
                step(dve.tensor_tensor(gm[:, :], gm[:, :], ge[:, :, E0], ALU.mult))
                dve.tensor_tensor(WPE[:, :, 0:E0], gp[:, :, :], wide(gm[:, :]), ALU.mult)
                dve.tensor_copy(wgt[:, E0, :], ge[:, :, E0 + 1]).then_inc(wgt_ready, 1)

            def mixture(layer, n):
                gates(layer)
                for b in range(4):
                    dve.wait_ge(b2_ready, 4 * layer + b + 1)
                    ins = dve.tensor_copy(ACC[:, b * CW:(b + 1) * CW], ps[:, 4 + b, :])
                ins.then_inc(acc_started, 1)
                dve.wait_ge(acc_started, layer + 1)
                scalars = wgt[:, :, :].rearrange("p e t -> p (e t)")

                def emit(e, p, k):
                    for c in range(NC):
                        chunk = (e + E0 * layer) * NC + c
                        dve.wait_ge(y_ready, chunk + 1)
                        if not (is_int(chunk) and chunk < 1):
                            dve.wait_ge(y_used, chunk)
                        for m in range(TPC):
                            a = tile(ACC, c * TPC + m)
                            ins = dve.scalar_tensor_tensor(
                                out=a, in0=ps[:, 4 + c % 2, m * P:(m + 1) * P],
                                scalar=scalars[:, bass.ds(e * NT + c * TPC + m, 1)], in1=a, op0=ALU.mult, op1=ALU.add)
                        ins.then_inc(y_used, 1)
                run_experts(dve, n, emit)
                dve.wait_ge(y_used, (E0 * layer + n) * NC)

            split_q(0)
            attention(0)
            projected(1, y, bo[:, 0, :])
            add(y, y, CM)
            layer_norm(y, xh)
            xhat()
            step(dve.tensor_tensor(tiles(CM), tiles(xh), along(lnrow[:, 0, :]), ALU.mult))
            step(dve.tensor_tensor(tiles(CM), tiles(CM), along(lnrow[:, 1, :]), ALU.add))
            mixture(0, E0)
            add(y, CM, ACC)
            layer_norm(y, xh)
            step(dve.tensor_tensor(tiles(xh), tiles(xh), along(lnrow[:, 2, :]), ALU.mult))
            step(dve.tensor_tensor(tiles(y), tiles(xh), along(lnrow[:, 3, :]), ALU.add))
            layer_norm(y, xh)
            add(x, x, xh)
            layer_norm(x, xh)
            xhat()
            split_q(1)
            attention(1)
            projected(2, y, None)
            layer_norm(y, xh)
            add(x, x, xh)
            layer_norm(x, CM)
            layer_norm(CM, xh)
            xhat()
            split_q(2)
            attention(2)
            projected(3, y, bo[:, 1, :])
            add(CM, CM, y)
            layer_norm(CM, xh)
            xhat()
            mixture(1, E1)
            add(y, CM, ACC)
            layer_norm(y, xh)
            dve.tensor_tensor(x, x, xh, ALU.add).then_inc(final_ready, 1)


def kernel(**inputs):
    import numpy as np
    import concourse.bacc as bacc
    from concourse import mybir as _mybir
    from concourse.bass_utils import run_bass_kernel_spmd

    g = {k: np.asarray(v) for k, v in inputs.items()}
    a = {}
    a["x"] = g["L0_attn_x"].reshape(S, P)
    w = g["L0_attn_W_qkv"].reshape(PAIRS, 2, AD, 3, P)
    a["a_w"] = w.transpose(0, 4, 3, 1, 2).reshape(PAIRS, P, 3 * P)
    b = g["L0_attn_b_qkv"].reshape(PAIRS, 2 * AD, 3)
    a["a_bqk"] = b[:, :, 0:2]
    a["a_bv"] = b[:, :, 2]
    a["a_wo"] = g["L0_attn_W_o"].T.reshape(PAIRS, P, P).transpose(1, 0, 2).reshape(P, PAIRS * P)
    a["a_bo"] = g["L0_attn_b_o"]
    a["conv_w"] = g["L0_ffn_conv_w"].transpose(1, 2, 0).reshape(P, 3 * P)
    a["conv_b"] = g["L0_ffn_conv_b"].reshape(P, 1)
    a["wqkv0"] = g["L0_ffn_wqkv"].T
    a["wqkv1"] = g["L1_attn_w_qkv"]
    a["wqkv2"] = g["L1_ffn_Wqkv"]
    for n, name in (("0", "L0_ffn_bqkv"), ("2", "L1_ffn_bqkv")):
        b = g[name].reshape(3, P)
        a["bqk" + n] = b[0:2].T
        a["bv" + n] = b[2]
    a["wo0"], a["bo0"] = g["L0_ffn_wo"].T, g["L0_ffn_bo"]
    a["wo1"] = g["L1_attn_w_proj"]
    a["wo2"], a["bo2"] = g["L1_ffn_Wo"], g["L1_ffn_bo"]
    a["ln_b1_g"], a["ln_b1_b"] = g["L0_ffn_ln1_g"], g["L0_ffn_ln1_b"]
    a["ln_b2_g"], a["ln_b2_b"] = g["L0_ffn_ln2_g"], g["L0_ffn_ln2_b"]
    a["lncol"] = np.stack([g["L0_ffn_ln1_g"], g["L0_ffn_ln1_b"], g["L1_ffn_ln1_g"], g["L1_ffn_ln1_b"],
                           g["L1_ffn_ln2_g"], g["L1_ffn_ln2_b"]], axis=1)
    a["gate_w0"] = g["L0_ffn_gate_w"]
    a["gate_w1"] = np.concatenate([g["L1_ffn_gate_w"], g["L1_ffn_coef_w"]], axis=1)
    a["gate_b"], a["coef_b"] = g["L0_ffn_gate_b"], g["L1_ffn_coef_b"]
    a["b2_0"] = g["L0_ffn_b2"]
    a["b2_1"] = np.concatenate([g["L1_ffn_b2"], g["L1_ffn_rb2"][None]], axis=0)
    a["w1"] = np.concatenate([g["L0_ffn_w1"], g["L1_ffn_W1"], g["L1_ffn_rW1"][None]], axis=0)
    w2 = np.concatenate([g["L0_ffn_w2"], g["L1_ffn_W2"], g["L1_ffn_rW2"][None]], axis=0)
    a["w2"] = w2.reshape(-1, FC, P, P).transpose(0, 2, 1, 3).reshape(-1, P, FC * P)
    b1 = np.concatenate([g["L0_ffn_b1"], g["L1_ffn_b1"], g["L1_ffn_rb1"][None]], axis=0)
    a["b1"] = b1.reshape(-1, FC, P).transpose(0, 2, 1)
    inv_freq = (np.float32(1.0) / np.float32(10000.0) ** (np.arange(0, DH, 2, dtype=np.float32) / np.float32(DH))
                ).astype(np.float32)
    freqs = np.arange(S, dtype=np.float32)[:, None] * inv_freq[None, :]
    a["cos"] = np.tile(np.repeat(np.cos(freqs), 2, axis=1), (1, H)).T
    a["sin"] = np.tile(np.repeat(np.sin(freqs), 2, axis=1), (1, H)).T
    a["rank"] = np.arange(E0, 0, -1).astype(np.float32)
    bf = _mybir.dt.np(BF16) if hasattr(_mybir.dt, "np") else np.dtype("bfloat16")
    a["ones"] = np.ones((3, S), dtype=bf)
    a["zeros"] = np.zeros((3, S), dtype=bf)

    nc = bacc.Bacc("TRN2", target_bir_lowering=False, num_devices=1)
    arrays, t = {}, {}
    for name, v in a.items():
        v = np.ascontiguousarray(v)
        arrays[f"in_{name}"] = v
        t[name] = nc.dram_tensor(f"in_{name}", v.shape, _mybir.dt.from_np(v.dtype), kind="ExternalInput").ap()
    out = nc.dram_tensor("out_0", (S, P), F32, kind="ExternalOutput").ap()
    sandwich_kernel(nc, t, out)
    r = run_bass_kernel_spmd(nc, [arrays], core_ids=[0])
    return r.results[0]["out_0"].reshape(1, S, P)
```

```python
from contextlib import ExitStack

import concourse.bass as bass
from concourse import mybir

F32 = mybir.dt.float32
BF16 = mybir.dt.bfloat16
ALU = mybir.AluOpType
ACT = mybir.ActivationFunctionType
X_AXIS = mybir.AxisListType.X

P = 128
S = 2048
NT = S // P
CW = 512
NC = S // CW
TPC = CW // P
EPS = 1e-5
RMS_EPS = 1.1920929e-07
MASKED = -1e30

AD = 64
PAIRS = 8
RING = 6
LAG = 2
PROJ = 3 * NC
PROJ_FROM = 20

H = 16
DH = 8
SLOTS = 6
MROW = SLOTS * DH
VC = 32
SCALE = float(DH) ** -0.5

E0, E1 = 8, 9
FFN = 512
FC = FFN // P

ROWS = [(r // NT, r % NT) for r in range(2 * NT)]


def row_chunks(i):
    return [(c, P * (i % TPC) if c == i // TPC else 0) for c in range(i // TPC, NC)]


def pair_plan(projects):
    j, plan = 0, []
    for r, (_, i) in enumerate(ROWS):
        n = len(row_chunks(i))
        followed = projects and r >= PROJ_FROM
        plan.append((j, n, j + n if followed else None))
        j += n + followed
    return plan, j


PLAN, PER_PAIR = pair_plan(True)
LAST_PLAN, _ = pair_plan(False)
assert 2 * NT - PROJ_FROM == PROJ


def ring_user_before(pair, j):
    base = PROJ + pair * PER_PAIR
    if j >= RING:
        return base + j - RING + 1
    n = PROJ if isinstance(pair, int) and pair == 0 else PER_PAIR
    last = n - 1 - (n - 1 - j) % RING
    return base - n + last + 1


def run_pairs(eng, emit):
    emit(0, 0)
    with eng.Fori(0, (PAIRS - 2) // 2) as i:
        emit(i * 2 + 1, 1)
        emit(i * 2 + 2, 0)
    emit(PAIRS - 1, 1)


def run_heads(eng, emit):
    emit(0, 0, 0)
    with eng.Fori(0, (H - 2) // 2) as i:
        emit(i * 2 + 1, 1, i)
        emit(i * 2 + 2, 0, i + 1)
    emit(H - 1, 1, H // 2 - 1)


def run_experts(eng, n, emit):
    emit(0, 0, 0)
    emit(1, 1, 0)
    with eng.Fori(0, 3) as i:
        emit(i * 2 + 2, 0, i + 1)
        emit(i * 2 + 3, 1, i + 1)
    if n == E1:
        emit(8, 0, 4)


MAX_FROM, MAX_GROUPS = 2, 12


def max_products(kt, c):
    slot, slots, n = (kt - MAX_FROM) * NC + c, MAX_GROUPS * NC, NT * NC
    if not 0 <= slot < slots:
        return []
    return [(m // NC, m % NC) for m in range(slot * n // slots, (slot + 1) * n // slots)]


ST_RING = 3


def st_bank(m):
    return 4 + m % ST_RING


def st_read_before(m):
    n = NT * NC
    return m - ST_RING + 1 if m >= ST_RING else max(j for j in range(-n, 0) if (j + n) % ST_RING == m % ST_RING) + 1


def is_int(x):
    return isinstance(x, int)


def sandwich_kernel(nc, t, out):
    ctx = ExitStack()
    with ctx:
        def sb(name, shape, dt=F32):
            return ctx.enter_context(nc.sbuf_tensor(name, shape, dt))

        def sem(name):
            return ctx.enter_context(nc.semaphore(name))

        q_dram = nc.dram_tensor("q_dram", (3, H, 3 * DH + 3, S), BF16, kind="Internal").ap()
        k_dram = nc.dram_tensor("k_dram", (3, H, 3 * DH, S), BF16, kind="Internal").ap()
        z_dram = nc.dram_tensor("z_dram", (3, H, P, CW), F32, kind="Internal").ap()

        ps = ctx.enter_context(nc.psum_tensor("ps", [P, 8, CW], F32))

        X = sb("X", [P, S])
        XH = sb("XH", [P, S])
        XTp = sb("XTp", [P, S + 2])
        XT = XTp[:, 1:S + 1]
        Y = sb("Y", [P, S])
        probs = sb("probs", [P, 4, S])
        arena = sb("arena", [P, 13 * S])
        QS = [sb(f"QS{p}", [P, S], BF16) for p in range(2)]
        KS = [sb(f"KS{p}", [P, S], BF16) for p in range(2)]
        VS = sb("VS", [P, 2, NT, VC])
        QT = [arena[:, 0 * S:1 * S], arena[:, 1 * S:2 * S]]
        KT = [arena[:, 2 * S:3 * S], arena[:, 3 * S:4 * S]]
        VA = [arena[:, 4 * S:5 * S], Y[:, :]]
        ZA = arena[:, 5 * S:13 * S]
        CT = arena[:, 0 * S:1 * S]
        CM = arena[:, 1 * S:2 * S]
        T = [arena[:, (2 + n) * S:(3 + n) * S] for n in range(4)]
        ZT, ZS = T[0], T[1]
        COS, SIN = arena[:, 6 * S:7 * S], arena[:, 7 * S:8 * S]
        PARTS = [arena[:, 8 * S:8 * S + 3 * S // 2].bitcast(BF16),
                 arena[:, 10 * S:10 * S + 3 * S // 2].bitcast(BF16)]
        ACC = T[2]
        VALL = Y
        HT = [probs[:, 0, :], probs[:, 1, :]]
        W1S = [probs[:, 2, 0:FFN], probs[:, 2, FFN:2 * FFN]]
        W2S = [probs[:, 2, 2 * FFN:3 * FFN], probs[:, 2, 3 * FFN:4 * FFN]]
        ZST = T[3][:, 0:2 * CW].rearrange("p (n c) -> p n c", n=2)
        late = arena[:, 23 * S // 2:13 * S]
        B1S = sb("B1S", [P, 2, FC])
        WT = probs[0:E1, 3, :]

        w_a = sb("w_a", [P, 3 * P])
        bqk_a = sb("bqk_a", [P, 2])
        bv_a = sb("bv_a", [P, P])
        wo_a = sb("wo_a", [P, PAIRS * P])
        bo_a = sb("bo_a", [P, P])
        conv_w = late[:, 0:3 * P]
        conv_b = sb("conv_b", [P, 1])
        wqkv = late[:, 3 * P:12 * P].rearrange("p (s n) -> p s n", s=3)
        wrot = late[:, 12 * P:14 * P]
        bqk = sb("bqk", [P, 3, 2])
        bv = late[:, 14 * P:16 * P].rearrange("p (s n) -> p s n", s=2)
        wo = late[:, 16 * P:19 * P].rearrange("p (s n) -> p s n", s=3)
        bo = late[:, 19 * P:21 * P].rearrange("p (s n) -> p s n", s=2)
        lnrow = sb("lnrow", [P, 4, P])
        lncol = sb("lncol", [P, 6])
        gw = sb("gw", [P, 2, 10])
        gb = sb("gb", [P, 10])
        rank = sb("rank", [P, E0])
        b2s = sb("b2s", [E1, 2, P])
        ident = sb("ident", [P, P])
        identb = sb("identb", [P, P], BF16)
        maskb = sb("maskb", [P, P], BF16)

        stats = sb("stats", [P, NT, 6])
        mean = sb("mean", [P, NT])
        shift = sb("shift", [P, NT])
        half = sb("half", [P, 3, NT])
        idle = sb("idle", [P, 1])
        var = sb("var", [P, NT])
        std = sb("std", [P, NT])
        rstd = sb("rstd", [P, NT])
        amx = sb("amx", [P, 4, NC])
        anm = sb("anm", [P, 4])
        als = sb("als", [P, 4, NC])
        asum = sb("asum", [P, 4])
        arl = sb("arl", [P, 4])
        VR = sb("VR", [P, 4, AD])
        mx = sb("mx", [P, NT, NC])
        nm = sb("nm", [P, NT])
        nr = sb("nr", [P, NT])
        mb = sb("mb", [P, P], BF16)
        mT = sb("mT", [3 * NT, P], BF16)
        gl = sb("gl", [P, NT, 10])
        ge = sb("ge", [P, NT, 10])
        gp = sb("gp", [P, NT, E0])
        gm = sb("gm", [P, NT])
        gs = sb("gs", [P, NT])
        g2 = sb("g2", [P, NT])
        wgt = sb("wgt", [P, E1, NT])
        WPE = wgt[:, :, :].rearrange("p e t -> p t e")

        ld_x = sem("ld_x")
        ld_early = sem("ld_early")
        ld_late = sem("ld_late")
        consts_made = sem("consts_made")
        pool_step = sem("pool_step")
        dve_step = sem("dve_step")
        ones_loaded = sem("ones_loaded")
        staging_cleared = sem("staging_cleared")
        tables_loaded = sem("tables_loaded")
        wrot_made = sem("wrot_made")
        var_ready = sem("var_ready")
        std_ready = sem("std_ready")
        shift_ready = sem("shift_ready")
        scaled_dve = sem("scaled_dve")
        scaled_act = sem("scaled_act")
        turned = sem("turned")
        turned_out = sem("turned_out")
        proj_ready = sem("proj_ready")
        conv_ready = sem("conv_ready")
        conv_out = sem("conv_out")
        a_weights = sem("a_weights")
        a_ready = sem("a_ready")
        a_max = sem("a_max")
        a_negmax = sem("a_negmax")
        a_read = sem("a_read")
        a_sum = sem("a_sum")
        a_rsum = sem("a_rsum")
        a_vscaled = sem("a_vscaled")
        a_vbiased = sem("a_vbiased")
        a_pv = sem("a_pv")
        a_zout = sem("a_zout")
        qkv_ready = sem("qkv_ready")
        v_out = sem("v_out")
        high_ready = sem("high_ready")
        rest_ready = sem("rest_ready")
        mid_ready = sem("mid_ready")
        low_ready = sem("low_ready")
        turned_cos = sem("turned_cos")
        turned_sin = sem("turned_sin")
        rotated = sem("rotated")
        zeros_stored = sem("zeros_stored")
        parts_stored = sem("parts_stored")
        v_biased = sem("v_biased")
        qk_staged = [sem(f"qk_staged{p}") for p in range(2)]
        max_rows = [sem(f"max_rows{p}") for p in range(2)]
        smax_ready = sem("smax_ready")
        smax_done = sem("smax_done")
        m_step = sem("m_step")
        m_ready = sem("m_ready")
        m_turned = sem("m_turned")
        m_copied = sem("m_copied")
        st_ready = sem("st_ready")
        exp_done = sem("exp_done")
        pv_done = sem("pv_done")
        z_copied = sem("z_copied")
        z_stored = [sem(f"z_stored{p}") for p in range(2)]
        z_loaded = [sem(f"z_loaded{c}") for c in range(NC)]
        z_inverted = sem("z_inverted")
        v_staged = sem("v_staged")
        ctx_ready = sem("ctx_ready")
        logits_ready = sem("logits_ready")
        shifted = sem("shifted")
        gate_exp = sem("gate_exp")
        wgt_ready = sem("wgt_ready")
        wgt_turned = sem("wgt_turned")
        wgt_out = sem("wgt_out")
        b2_ready = sem("b2_ready")
        acc_started = sem("acc_started")
        w_staged = [sem(f"w_staged{p}") for p in range(2)]
        h_ready = sem("h_ready")
        h_out = sem("h_out")
        y_ready = sem("y_ready")
        y_used = sem("y_used")
        final_ready = sem("final_ready")
        stored = sem("stored")

        def bc(ap):
            return ap.partition_broadcast(P)

        EARLY_LOADS = [(wo_a[:, :], t["a_wo"]), (bo_a[:, :], bc(t["a_bo"]))]
        LATE_LOADS = [
            (conv_w, t["conv_w"]), (conv_b[:, :], t["conv_b"]),
            (wqkv[:, 0, :], t["wqkv0"]), (wqkv[:, 1, :], t["wqkv1"]), (wqkv[:, 2, :], t["wqkv2"]),
            (bqk[:, 0, :], t["bqk0"]), (bqk[:, 2, :], t["bqk2"]),
            (bv[:, 0, :], bc(t["bv0"])), (bv[:, 1, :], bc(t["bv2"])),
            (wo[:, 0, :], t["wo0"]), (wo[:, 1, :], t["wo1"]), (wo[:, 2, :], t["wo2"]),
            (bo[:, 0, :], bc(t["bo0"])), (bo[:, 1, :], bc(t["bo2"])),
            (lnrow[:, 0, :], bc(t["ln_b1_g"])), (lnrow[:, 1, :], bc(t["ln_b1_b"])),
            (lnrow[:, 2, :], bc(t["ln_b2_g"])), (lnrow[:, 3, :], bc(t["ln_b2_b"])),
            (lncol[:, :], t["lncol"]),
            (gw[:, 0, 0:E0], t["gate_w0"]), (gw[:, 1, :], t["gate_w1"]),
            (gb[:, 0:E0], bc(t["gate_b"])), (gb[:, E0:10], bc(t["coef_b"])),
            (rank[:, :], bc(t["rank"])),
            (b2s[0:E0, 0, :], t["b2_0"]), (b2s[:, 1, :], t["b2_1"]),
        ]
        N_EARLY, N_LATE = 16 * len(EARLY_LOADS), 16 * len(LATE_LOADS)

        LNCOL = {3: (0, 1), 5: (2, 3), 6: (4, 5)}
        TURN = [(XH, XT), (XH, XT), (CT, CM), (XH, XT), (XH, XT), (XH, XT), (XH, XT)]
        NORMS = [(X, XH), (XH, XH), (Y, XH), (X, XH), (Y, XH), (Y, XH), (Y, XH), (X, XH), (Y, XH),
                 (X, CM), (CM, XH), (CM, XH), (Y, XH)]
        RMS = 1
        NORM_OF = {0: 1, 1: 3, 3: 4, 4: 7, 5: 10, 6: 11}
        ON_ACT = [(3,), (6, 7), (11,), (14, 15)]
        BLOCKS = [["q", "k", "v"], ["q", "qr", "k", "kr", "v"], ["q", "k", "v"]]
        QKV_BASE = [0, 12, 32, 44]
        QKV_SRC = [CT, XT, XT]

        def part(n, which):
            at = which * S + (n % NC) * CW
            return PARTS[n // NC][:, at:at + CW]

        def rest(n):
            return T[2 * (n // NC)][:, (n % NC) * CW:(n % NC + 1) * CW]

        N_STAGE_DMA = 8

        block = ctx.enter_context(nc.Block())

        @block.sync
        def _(sp):
            sp.dma_start(X[:, :].rearrange("p (t d) -> p t d", d=P),
                         t["x"].rearrange("(t p) d -> p t d", p=P)).then_inc(ld_x, 16)

            def load_pair(n):
                if not (is_int(n) and n == 0):
                    sp.wait_ge(a_vbiased, n)
                at = bass.ds(n, 1)
                sp.dma_start(w_a[:, :], t["a_w"][at].rearrange("a p n -> (a p) n")).then_inc(a_weights, 16)
                sp.dma_start(bqk_a[:, :], t["a_bqk"][at].rearrange("a p n -> (a p) n")).then_inc(a_weights, 16)
                sp.dma_start(bv_a[:, :], t["a_bv"][at].rearrange("a n -> (a n)").partition_broadcast(P)
                             ).then_inc(a_weights, 16)

            load_pair(0)
            for dst, src in EARLY_LOADS:
                sp.dma_start(dst, src).then_inc(ld_early, 16)
            for s in range(3):
                sp.dma_start(q_dram[s, :, 3 * DH:, :], t["zeros"]).then_inc(zeros_stored, 16)
            sp.wait_ge(staging_cleared, 1)
            for p in range(2):
                sp.dma_start(KS[p][MROW:MROW + 3, :], t["ones"]).then_inc(ones_loaded, 16)
            with sp.Fori(1, PAIRS) as n:
                load_pair(n)

            def stage(s, h, p):
                at = bass.ds(h, 1)

                def rows(dst, row, src, a, b):
                    sp.dma_start(dst[p][row:row + b - a, :], src[s, at, a:b].rearrange("a d t -> (a d) t")
                                 ).then_inc(qk_staged[p], 16)

                rows(QS, 0, q_dram, 0, 2 * DH)
                rows(KS, DH, k_dram, 0, 3 * DH)
                rows(KS, 0, k_dram, 0, DH)
                rows(QS, 2 * DH, q_dram, 0, DH)
                rows(QS, 3 * DH, q_dram, 0, 2 * DH)
                rows(KS, 4 * DH, k_dram, DH, 2 * DH)
                rows(KS, 5 * DH, k_dram, 0, DH)
                rows(QS, 5 * DH, q_dram, 2 * DH, 3 * DH + 3)

            def put_max_rows(g, p):
                sp.wait_ge(m_copied, g + 1)
                sp.dma_start(QS[p][MROW:MROW + 3, :], mT[:, :]).then_inc(max_rows[p], 16)

            def store_z(s, h, g, p):
                sp.wait_ge(z_copied, g + 1)
                sp.dma_start(z_dram[s, bass.ds(h, 1)].rearrange("a p t -> (a p) t"), ZST[:, p, :]
                             ).then_inc(z_stored[p], 16)

            def experts(layer, n):
                def emit(e, p, k):
                    x = E0 * layer + e
                    if is_int(x) and x < 2:
                        sp.wait_ge(pv_done, NT * H)
                    elif is_int(e) and e < 2:
                        sp.wait_ge(pv_done, NT * H * 3)
                    if not (is_int(e) and e < 2):
                        sp.wait_ge(y_ready, x * NC - NC)
                    at = bass.ds(x, 1)
                    sp.dma_start(W1S[p], t["w1"][at].rearrange("a p n -> (a p) n")).then_inc(w_staged[p], 16)
                    sp.dma_start(W2S[p], t["w2"][at].rearrange("a p n -> (a p) n")).then_inc(w_staged[p], 16)
                    sp.dma_start(B1S[:, p, :], t["b1"][at].rearrange("a p n -> (a p) n")).then_inc(w_staged[p], 16)
                run_experts(sp, n, emit)

            def attention(s):
                for n, dram in enumerate((q_dram, k_dram)):
                    for part, done, count in ((0, high_ready, 8 * s + 4 * n + 4), (1, mid_ready, 8 * s + 4 * n + 4),
                                              (2, low_ready, 8 * s + 4 * n + 4)):
                        sp.wait_ge(done, count)
                        sp.dma_start(dram[s, :, part * DH:(part + 1) * DH, :], PARTS[n][:, part * S:(part + 1) * S]
                                     ).then_inc(parts_stored, 16)
                sp.wait_ge(parts_stored, 96 * (s + 1))
                sp.wait_ge(zeros_stored, 48)
                stage(s, 0, 0)
                stage(s, 1, 1)
                put_max_rows(H * s, 0)

                def emit(h, p, k):
                    g = H * s + h
                    first, last = is_int(h) and h == 0, is_int(h) and h == H - 1
                    if not first and not last:
                        sp.wait_ge(st_ready, g * NC * NT)
                        stage(s, h + 1, 1 - p)
                    if not first:
                        store_z(s, h - 1, g - 1, 1 - p)
                    if not last:
                        put_max_rows(g + 1, 1 - p)
                    if last:
                        store_z(s, h, g, p)
                run_heads(sp, emit)
                for p in range(2):
                    sp.wait_ge(z_stored[p], 16 * (H // 2) * (s + 1))
                for c in range(NC):
                    for n, dst in enumerate((ZS, ZT)):
                        row = 32 * c + DH * (1 - n)
                        sp.dma_start(dst[:, c * CW:(c + 1) * CW], z_dram[s, :, row:row + DH, :]
                                     ).then_inc(z_loaded[c], 16)

            sp.wait_ge(proj_ready, 4)
            for dst, src in LATE_LOADS:
                sp.dma_start(dst, src).then_inc(ld_late, 16)
            attention(0)
            experts(0, E0)
            sp.dma_start(COS, t["cos"]).then_inc(tables_loaded, 16)
            sp.dma_start(SIN, t["sin"]).then_inc(tables_loaded, 16)
            attention(1)
            attention(2)
            experts(1, E1)
            sp.wait_ge(final_ready, 1)
            sp.dma_start(out.rearrange("(t p) d -> p t d", p=P),
                         X[:, :].rearrange("p (t d) -> p t d", d=P)).then_inc(stored, 16)
            sp.wait_ge(stored, 16)

        @block.gpsimd
        def _(pool):
            steps = [0]

            def step(ins):
                ins.then_inc(pool_step, 1)
                steps[0] += 1
                pool.wait_ge(pool_step, steps[0])

            pool.memset(XTp[:, 0:1], 0.0)
            pool.memset(XTp[:, S + 1:S + 2], 0.0)
            pool.memset(ident[:, :], 0.0)
            pool.memset(identb[:, :], 0.0)
            step(pool.memset(maskb[:, :], 0.0))
            pool.affine_select(out=ident[:, :], in_=ident[:, :], compare_op=ALU.not_equal, fill=1.0,
                               base=0, pattern=[[-1, P]], channel_multiplier=1)
            pool.affine_select(out=identb[:, :], in_=identb[:, :], compare_op=ALU.not_equal, fill=1.0,
                               base=0, pattern=[[-1, P]], channel_multiplier=1)
            pool.affine_select(out=maskb[:, :], in_=maskb[:, :], compare_op=ALU.is_ge, fill=MASKED,
                               base=0, pattern=[[1, P]], channel_multiplier=-1).then_inc(consts_made, 1)
            for p in range(2):
                pool.memset(QS[p][:, :], 0.0)
                pool.memset(KS[p][:, :], 0.0)
            pool.memset(mb[:, :], 0.0)
            pool.memset(idle[:, :], 1.0)
            pool.memset(VS[:, :, :, :], 1.0).then_inc(staging_cleared, 1)
            pool.wait_ge(staging_cleared, 1)
            def bias_v(pair, p, count):
                pool.wait_ge(a_read, count)
                v = VA[p].rearrange("p (t d) -> p t d", d=P)
                pool.tensor_tensor(v, v, bv_a[:, :].unsqueeze(1).broadcast_to([P, NT, P]), ALU.add
                                   ).then_inc(a_vbiased, 1)

            pool.wait_ge(a_weights, 48)
            bias_v(0, 0, PROJ)

            def emit_pair(pair, p):
                if is_int(pair) and pair == PAIRS - 1:
                    return
                bias_v(pair + 1, 1 - p, PROJ + pair * PER_PAIR + PER_PAIR)
            run_pairs(pool, emit_pair)

            def attention(s):
                if s == 1:
                    for n in range(2 * NC):
                        pool.wait_ge(turned_sin, n + 1)
                        q = T[0][:, n * CW:(n + 1) * CW] if n < NC else T[2][:, (n - NC) * CW:(n - NC + 1) * CW]
                        r = T[1][:, n * CW:(n + 1) * CW] if n < NC else T[3][:, (n - NC) * CW:(n - NC + 1) * CW]
                        pool.tensor_tensor(q, q, r, ALU.add).then_inc(rotated, 1)
                pool.wait_ge(ld_late, N_LATE)
                pool.wait_ge(v_out, 4 * (s + 1))
                if s != 1:
                    v = VALL[:, :].rearrange("p (t d) -> p t d", d=P)
                    pool.tensor_tensor(v, v, bv[:, s // 2, :].unsqueeze(1).broadcast_to([P, NT, P]), ALU.add
                                       ).then_inc(v_biased, 1)
                    pool.wait_ge(v_biased, s // 2 + 1)

                def emit(h, p, k):
                    g = H * s + h
                    if not is_int(g) or g >= 2:
                        pool.wait_ge(pv_done, (g - 1) * NT)
                    src = VALL[:, :].rearrange("p (t d) -> p t d", d=P)[:, :, bass.ds(h * DH, DH)]
                    pool.tensor_copy(VS[:, p, :, 0:DH], src).then_inc(v_staged, 1)
                run_heads(pool, emit)

            attention(0)
            pool.wait_ge(ld_late, N_LATE)
            src = wqkv[:, 1, 0:2 * P].rearrange("p (n two) -> p n two", two=2)
            dst = wrot.rearrange("p (n two) -> p n two", two=2)
            pool.tensor_scalar(dst[:, :, 0], src[:, :, 1], -1.0, None, ALU.mult)
            pool.tensor_copy(dst[:, :, 1], src[:, :, 0]).then_inc(wrot_made, 1)
            attention(1)
            attention(2)

        @block.scalar
        def _(act):
            def copy(out_, in_, bias=0.0, scale=1.0):
                return act.activation(out_, in_, ACT.Identity, bias=bias, scale=scale)

            def normalise(n):
                act.activation(idle[:, :], idle[:, :], ACT.Sqrt)
                act.wait_ge(var_ready, n + 1)
                act.activation(std[:, :], var[:, :], ACT.Sqrt).then_inc(std_ready, 1)
                act.wait_ge(shift_ready, n + 1)
                src, dst = NORMS[n]
                for tiles_ in ON_ACT:
                    for m in tiles_:
                        ins = copy(dst[:, m * P:(m + 1) * P], src[:, m * P:(m + 1) * P], shift[:, m:m + 1],
                                   rstd[:, m:m + 1])
                    ins.then_inc(scaled_act, 1)

            def turn_out(k):
                bias, scale = 0.0, 1.0
                if k in LNCOL:
                    g, b = LNCOL[k]
                    act.wait_ge(ld_late, N_LATE)
                    scale, bias = lncol[:, g:g + 1], lncol[:, b:b + 1]
                for b_ in range(4):
                    act.wait_ge(turned, 4 * k + b_ + 1)
                    copy(TURN[k][1][:, b_ * CW:(b_ + 1) * CW], ps[:, b_, :], bias, scale).then_inc(turned_out, 1)

            def project_out(n, j, p):
                kind, c = n // NC, n % NC
                dst = (QT, KT, VA)[kind][p][:, c * CW:(c + 1) * CW]
                bias = bqk_a[:, kind:kind + 1] if kind < 2 else 0.0
                copy(dst, ps[:, j % RING, :], bias).then_inc(a_read, 1)

            act.wait_ge(staging_cleared, 1)
            normalise(0)
            normalise(1)
            turn_out(0)
            act.wait_ge(a_weights, 48)
            for n in range(PROJ):
                act.wait_ge(a_ready, n + 1)
                project_out(n, n, 0)

            def z_out(head, pair, hh):
                act.wait_ge(a_pv, (head + 1) * NT)
                for c in range(NC):
                    ins = copy(ZA[AD * hh:AD * hh + AD, bass.ds(pair * S + c * CW, CW)],
                               ps[AD * (c % 2):AD * (c % 2) + AD, 6 + c // 2, :])
                ins.then_inc(a_zout, 1)

            def emit_pair(pair, p):
                first, last = is_int(pair) and pair == 0, is_int(pair) and pair == PAIRS - 1
                for r, (hh, i) in enumerate(ROWS):
                    R = pair * 2 * NT + r
                    j, n, after = (LAST_PLAN if last else PLAN)[r]
                    if i == LAG and not (first and hh == 0):
                        if hh:
                            z_out(pair * 2, pair, 0)
                        else:
                            z_out(pair * 2 - 1, pair - 1, 1)
                    act.wait_ge(a_negmax, R + 1)
                    if not (first and r < 4):
                        act.wait_ge(a_pv, R - 3)
                    for ci, (c, off) in enumerate(row_chunks(i)):
                        act.activation(probs[:, r % 4, c * CW + off:(c + 1) * CW], ps[:, (j + ci) % RING, off:],
                                       ACT.Exp, bias=anm[:, r % 4:r % 4 + 1],
                                       accum_out=als[:, r % 4, ci:ci + 1]).then_inc(a_read, 1)
                    if after is not None:
                        if r == PROJ_FROM:
                            act.wait_ge(a_weights, pair * 48 + 96)
                        act.wait_ge(a_ready, PROJ + pair * PER_PAIR + after + 1)
                        project_out(r - PROJ_FROM, after, 1 - p)
                if last:
                    z_out(PAIRS * 2 - 1, PAIRS - 1, 1)
            run_pairs(act, emit_pair)

            def conv():
                for c in range(NC):
                    act.wait_ge(conv_ready, c + 1)
                    copy(CT[:, c * CW:(c + 1) * CW], ps[:, 4 + c, :], conv_b[:, 0:1]).then_inc(conv_out, 1)

            def qkv(s):
                if s:
                    act.wait_ge(v_staged, H * s)
                def high(n):
                    if s == 1:
                        act.wait_ge(rotated, n + 1)
                        src, bias = T[2 * (n // NC)][:, (n % NC) * CW:(n % NC + 1) * CW], 0.0
                    else:
                        act.wait_ge(qkv_ready, QKV_BASE[s] + n + 1)
                        src, bias = ps[:, n, :], bqk[:, s, n // NC:n // NC + 1]
                    copy(part(n, 0), src, bias).then_inc(high_ready, 1)

                def middle(n):
                    act.wait_ge(rest_ready, 8 * s + n + 1)
                    copy(part(n, 1), rest(n)).then_inc(mid_ready, 1)

                for n in range(2 * NC):
                    high(n)
                    if n:
                        middle(n - 1)
                middle(2 * NC - 1)
                for c in range(NC):
                    act.wait_ge(qkv_ready, QKV_BASE[s + 1] - NC + c + 1)
                    copy(VALL[:, c * CW:(c + 1) * CW], ps[:, c, :]).then_inc(v_out, 1)

            def attention(s):
                def z_copy(g, p, k):
                    act.wait_ge(pv_done, (g + 1) * NT)
                    if not (is_int(g) and g < 2):
                        act.wait_ge(z_stored[p], (k + 8 * s) * 16)
                    copy(ZST[:, p, :], ps[:, 7, :]).then_inc(z_copied, 1)

                def emit(h, p, k):
                    g = H * s + h
                    first, last = is_int(h) and h == 0, is_int(h) and h == H - 1
                    for kt in range(NT):
                        if not (is_int(g) and g == 0 and kt < 4):
                            act.wait_ge(pv_done, g * NT + kt - 3)
                        for c in range(NC):
                            act.wait_ge(st_ready, g * NT * NC + kt * NC + c + 1)
                            act.activation(probs[:, kt % 4, c * CW:(c + 1) * CW], ps[:, st_bank(kt * NC + c), :],
                                           ACT.Exp, scale=SCALE).then_inc(exp_done, 1)
                        if kt == 0 and not first:
                            z_copy(g - 1, 1 - p, k if p else k - 1)
                    if last:
                        z_copy(g, p, k)
                run_heads(act, emit)

            def mixture(layer, n):
                act.wait_ge(shifted, layer + 1)
                if layer:
                    act.activation(ge[:, :, :], gl[:, :, :], ACT.Exp).then_inc(gate_exp, 1)
                else:
                    act.activation(ge[:, :, 0:E0], gl[:, :, 0:E0], ACT.Exp).then_inc(gate_exp, 1)
                for b_ in range(4):
                    act.wait_ge(wgt_turned, 4 * layer + b_ + 1)
                    copy(WT[0:n, b_ * CW:(b_ + 1) * CW], ps[0:n, b_, :]).then_inc(wgt_out, 1)

                def emit(e, p, k):
                    act.wait_ge(w_staged[p], (k + 4 * layer + 1) * 48)
                    for c in range(NC):
                        chunk = (e + E0 * layer) * NC + c
                        if not (is_int(e) and e == 0 and layer == 0 and c < 2):
                            act.wait_ge(y_ready, chunk - 1)
                        for f in range(FC):
                            act.wait_ge(h_ready, chunk * FC + f + 1)
                            act.activation(HT[c % 2][:, f * CW:(f + 1) * CW], ps[:, f, :],
                                           ACT.Gelu if layer else ACT.Relu,
                                           bias=B1S[:, p, f:f + 1]).then_inc(h_out, 1)
                run_experts(act, n, emit)

            act.wait_ge(ld_late, N_LATE)
            normalise(2)
            normalise(3)
            turn_out(1)
            conv()
            turn_out(2)
            qkv(0)
            attention(0)
            normalise(4)
            turn_out(3)
            mixture(0, E0)
            normalise(5)
            normalise(6)
            normalise(7)
            turn_out(4)
            qkv(1)
            attention(1)
            normalise(8)
            normalise(9)
            normalise(10)
            turn_out(5)
            qkv(2)
            attention(2)
            normalise(11)
            turn_out(6)
            mixture(1, E1)
            normalise(12)

        @block.tensor
        def _(pe):
            def mm(out_, lhsT, rhs, start=True, stop=True):
                return pe.matmul(out_, lhsT, rhs, start=start, stop=stop, skip_group_check=True)

            def turn(k):
                if k >= 1:
                    pe.wait_ge(turned_out, 4 * k)
                src = TURN[k][0]
                for n in range(NT):
                    if n % TPC == 0:
                        b = n // TPC + 1
                        if k == 2:
                            pe.wait_ge(conv_out, b)
                        else:
                            pe.wait_ge(scaled_dve, 4 * NORM_OF[k] + b)
                            pe.wait_ge(scaled_act, 4 * NORM_OF[k] + b)
                    ins = pe.transpose(ps[:, n // TPC, (n % TPC) * P:(n % TPC + 1) * P],
                                       src[:, n * P:(n + 1) * P], ident[:, :])
                    if n % TPC == TPC - 1:
                        ins.then_inc(turned, 1)

            def project(n, j, p):
                kind, c = n // NC, n % NC
                bank = ps[:, j % RING, :]
                w = w_a[:, kind * P:(kind + 1) * P]
                if kind < 2:
                    return mm(bank, w, XT[:, c * CW:(c + 1) * CW])
                for m in range(TPC):
                    tok = (c * TPC + m) * P
                    ins = mm(bank[:, m * P:(m + 1) * P], XT[:, tok:tok + P], w)
                return ins

            pe.wait_ge(consts_made, 1)
            turn(0)
            pe.wait_ge(turned_out, 4)
            pe.wait_ge(a_weights, 48)
            for n in range(PROJ):
                if n >= RING:
                    pe.wait_ge(a_read, n - RING + 1)
                project(n, n, 0).then_inc(a_ready, 1)

            def pv(pair, r, p):
                hh, i = ROWS[r]
                R = pair * 2 * NT + r
                pe.wait_ge(a_vscaled, R + 1)
                if i == 0 and not (is_int(pair) and pair == 0 and hh == 0):
                    pe.wait_ge(a_zout, pair * 2 + hh)
                for c, off in row_chunks(i):
                    ins = mm(ps[AD * (c % 2):AD * (c % 2) + AD, 6 + c // 2, off:], VR[:, r % 4, :],
                             probs[:, r % 4, c * CW + off:(c + 1) * CW], start=(i == 0), stop=(i == 4 * c + 3))
                ins.then_inc(a_pv, 1)

            def emit_pair(pair, p):
                first, last = is_int(pair) and pair == 0, is_int(pair) and pair == PAIRS - 1
                pe.wait_ge(a_read, pair * PER_PAIR + PROJ - 0)
                for r, (hh, i) in enumerate(ROWS):
                    j, n, after = (LAST_PLAN if last else PLAN)[r]
                    half = slice(AD * hh, AD * hh + AD)
                    for ci, (c, off) in enumerate(row_chunks(i)):
                        jj = j + ci
                        pe.wait_ge(a_read, ring_user_before(pair, jj))
                        bank = ps[:, jj % RING, :]
                        diagonal = c == i // TPC
                        ins = mm(bank[:, off:], KT[p][half, i * P:(i + 1) * P],
                                 QT[p][half, c * CW + off:(c + 1) * CW], stop=not diagonal)
                        if diagonal:
                            ins = mm(bank[:, off:off + P], identb[:, :], maskb[:, :], start=False)
                        ins.then_inc(a_ready, 1)
                    if after is not None:
                        if r == PROJ_FROM:
                            pe.wait_ge(a_weights, pair * 48 + 96)
                        pe.wait_ge(a_read, ring_user_before(pair, after))
                        project(r - PROJ_FROM, after, 1 - p).then_inc(a_ready, 1)
                    if r >= LAG:
                        pv(pair, r - LAG, p)
                    elif not first:
                        pv(pair - 1, r - LAG + 2 * NT, 1 - p)
                if last:
                    pv(pair, 2 * NT - 2, p)
                    pv(pair, 2 * NT - 1, p)
            run_pairs(pe, emit_pair)

            def project_tokens(k, src_ready, parts):
                for n in range(NT):
                    if n % TPC == 0:
                        src_ready(n // TPC)
                    for m, (lhs, rhs) in enumerate(parts):
                        ins = mm(ps[:, n // TPC, (n % TPC) * P:(n % TPC + 1) * P], lhs[:, n * P:(n + 1) * P],
                                 rhs, start=(m == 0), stop=(m == len(parts) - 1))
                    if n % TPC == TPC - 1:
                        ins.then_inc(proj_ready, 1)

            def heads_out(b):
                pe.wait_ge(a_zout, 2 * PAIRS)
                pe.wait_ge(ld_early, N_EARLY)
            project_tokens(0, heads_out, [(ZA[:, n * S:(n + 1) * S], wo_a[:, n * P:(n + 1) * P])
                                          for n in range(PAIRS)])

            def conv():
                pe.wait_ge(turned_out, 8)
                pe.wait_ge(ld_late, N_LATE)
                for c in range(NC):
                    for j in range(3):
                        ins = mm(ps[:, 4 + c, :], conv_w[:, j * P:(j + 1) * P], XTp[:, c * CW + j:c * CW + j + CW],
                                 start=(j == 0), stop=(j == 2))
                    ins.then_inc(conv_ready, 1)

            def qkv(s, turned_before):
                pe.wait_ge(turned_out, turned_before)
                if s == 1:
                    pe.wait_ge(wrot_made, 1)
                src = QKV_SRC[s]
                for n, name in enumerate(BLOCKS[s]):
                    w = {"q": wqkv[:, s, 0:P], "k": wqkv[:, s, P:2 * P], "v": wqkv[:, s, 2 * P:],
                         "qr": wrot[:, 0:P], "kr": wrot[:, P:]}[name]
                    for c in range(NC):
                        if n >= 2 and s == 1:
                            pe.wait_ge(turned_sin if n % 2 else turned_cos, 4 * (n // 2 - 1) + c + 1)
                        elif n >= 2:
                            pe.wait_ge(rest_ready, 8 * s + c + 1)
                        bank = ps[:, 4 * (n % 2) + c, :]
                        if name != "v":
                            ins = mm(bank, w, src[:, c * CW:(c + 1) * CW])
                        else:
                            for m in range(TPC):
                                tok = (c * TPC + m) * P
                                ins = mm(bank[:, m * P:(m + 1) * P], src[:, tok:tok + P], w)
                        ins.then_inc(qkv_ready, 1)

            def attention(s):
                def max_scores(g, p, q, js):
                    for j in js:
                        u = (g * NT + q) * NC + j
                        if q == 0 and j == 0 and not (is_int(g) and g == 0):
                            pe.wait_ge(m_copied, g)
                        if not (is_int(u) and u < NC):
                            pe.wait_ge(smax_done, u - NC + 1)
                        mm(ps[:, j, :], QS[p][:, q * P:(q + 1) * P], KS[p][:, j * CW:(j + 1) * CW]
                           ).then_inc(smax_ready, 1)

                def turn_max(g):
                    pe.wait_ge(m_ready, g + 1)
                    pe.transpose(ps[:, 0, 0:P // 2].bitcast(BF16), mb[:, :], identb[:, :]
                                 ).then_inc(m_turned, 1)

                def pv(g, p, kt):
                    pe.wait_ge(exp_done, g * NT * NC + kt * NC + NC)
                    if kt == 0 and not (is_int(g) and g == 0):
                        pe.wait_ge(z_copied, g)
                    for c in range(NC):
                        ins = mm(ps[32 * c:32 * c + VC, 7, :], VS[:, p, kt, :],
                                 probs[:, kt % 4, c * CW:(c + 1) * CW], start=(kt == 0), stop=(kt == NT - 1))
                    ins.then_inc(pv_done, 1)

                pe.wait_ge(v_out, 4 * (s + 1))
                pe.wait_ge(low_ready, 8 * (s + 1))
                pe.wait_ge(ones_loaded, 32)
                pe.wait_ge(qk_staged[0], 16 * N_STAGE_DMA * (8 * s + 1))
                for q in range(NT):
                    max_scores(H * s, 0, q, range(NC))
                turn_max(H * s)

                def emit(h, p, k):
                    g = H * s + h
                    first, last = is_int(h) and h == 0, is_int(h) and h == H - 1
                    kn = k + 1 if p else k
                    pe.wait_ge(max_rows[p], (k + 8 * s + 1) * 16)
                    pe.wait_ge(v_staged, g + 1)
                    for kt in range(NT):
                        if kt == MAX_FROM and not last:
                            pe.wait_ge(qk_staged[1 - p], (kn + 8 * s + 1) * 16 * N_STAGE_DMA)
                        for c in range(NC):
                            for q, j in [] if last else max_products(kt, c):
                                max_scores(g + 1, 1 - p, q, [j])
                            m = kt * NC + c
                            if not (is_int(g) and g == 0 and m < ST_RING):
                                pe.wait_ge(exp_done, g * NT * NC + st_read_before(m))
                            mm(ps[:, st_bank(m), :], KS[p][:, kt * P:(kt + 1) * P],
                               QS[p][:, c * CW:(c + 1) * CW]).then_inc(st_ready, 1)
                            if c == 3:
                                if kt:
                                    pv(g, p, kt - 1)
                                elif not first:
                                    pv(g - 1, 1 - p, NT - 1)
                        if kt == NT - 2 and not last:
                            turn_max(g + 1)
                    if last:
                        pv(g, p, NT - 1)
                run_heads(pe, emit)

            def mixture(layer, n, turned_before):
                pe.wait_ge(turned_out, turned_before)
                width = 10 if layer else E0
                for m in range(NT):
                    ins = mm(ps[:, 4, m * 16:m * 16 + width], XT[:, m * P:(m + 1) * P], gw[:, layer, 0:width])
                ins.then_inc(logits_ready, 1)
                pe.wait_ge(wgt_ready, layer + 1)
                for m in range(NT):
                    ins = pe.transpose(ps[0:n, m // TPC, (m % TPC) * P:(m % TPC + 1) * P], wgt[:, 0:n, m],
                                       ident[:, :])
                    if m % TPC == TPC - 1:
                        ins.then_inc(wgt_turned, 1)
                for m in range(NT):
                    if m % TPC == 0:
                        pe.wait_ge(wgt_out, 4 * layer + m // TPC + 1)
                    ins = mm(ps[:, 4 + m // TPC, (m % TPC) * P:(m % TPC + 1) * P], WT[0:n, m * P:(m + 1) * P],
                             b2s[0:n, layer, :])
                    if m % TPC == TPC - 1:
                        ins.then_inc(b2_ready, 1)
                pe.wait_ge(acc_started, layer + 1)

                def down(e, p, c):
                    chunk = (e + E0 * layer) * NC + c
                    pe.wait_ge(h_out, chunk * FC + FC)
                    if not (is_int(chunk) and chunk < 2):
                        pe.wait_ge(y_used, chunk - 1)
                    for m in range(TPC):
                        for f in range(FC):
                            ins = mm(ps[:, 4 + c % 2, m * P:(m + 1) * P],
                                     HT[c % 2][:, f * CW + m * P:f * CW + (m + 1) * P],
                                     W2S[p][:, f * P:(f + 1) * P], start=(f == 0), stop=(f == FC - 1))
                    ins.then_inc(y_ready, 1)

                def emit(e, p, k):
                    pe.wait_ge(w_staged[p], (k + 4 * layer + 1) * 48)
                    for c in range(NC):
                        for f in range(FC):
                            unit = ((e + E0 * layer) * NC + c) * FC + f
                            if not (is_int(unit) and unit < FC):
                                pe.wait_ge(h_out, unit - FC + 1)
                            mm(ps[:, f, :], W1S[p][:, f * P:(f + 1) * P], XT[:, c * CW:(c + 1) * CW]
                               ).then_inc(h_ready, 1)
                        if c:
                            down(e, p, c - 1)
                        elif not (is_int(e) and e == 0):
                            down(e - 1, 1 - p, NC - 1)
                run_experts(pe, n, emit)
                down(n - 1, (n - 1) % 2, NC - 1)

            def ctx_is_ready(k):
                return lambda b: pe.wait_ge(ctx_ready, 4 * (k - 1) + b + 1)

            turn(1)
            conv()
            turn(2)
            qkv(0, 12)
            attention(0)
            project_tokens(1, ctx_is_ready(1), [(ZT, wo[:, 0, :])])
            turn(3)
            mixture(0, E0, 16)
            turn(4)
            qkv(1, 20)
            attention(1)
            project_tokens(2, ctx_is_ready(2), [(ZT, wo[:, 1, :])])
            turn(5)
            qkv(2, 24)
            attention(2)
            project_tokens(3, ctx_is_ready(3), [(ZT, wo[:, 2, :])])
            turn(6)
            mixture(1, E1, 28)

        @block.vector
        def _(dve):
            steps = [0]
            norms = [0]

            def step(ins):
                ins.then_inc(dve_step, 1)
                steps[0] += 1
                dve.wait_ge(dve_step, steps[0])

            def tiles(a):
                return a.rearrange("p (t d) -> p t d", d=P)

            def tile(a, n):
                return a[:, n * P:(n + 1) * P]

            def moments(src):
                for n in range(NT):
                    ins = dve.bn_stats(stats[:, n, :], tile(src, n))
                step(ins)
                even, odd = stats[:, :, 0:3], stats[:, :, 3:6]
                dve.tensor_tensor(half[:, 0, :], even[:, :, 1], odd[:, :, 1], ALU.add)
                dve.tensor_tensor(half[:, 1, :], even[:, :, 1], odd[:, :, 1], ALU.subtract)
                step(dve.tensor_tensor(half[:, 2, :], even[:, :, 2], odd[:, :, 2], ALU.add))
                dve.tensor_scalar(mean[:, :], half[:, 0, :], 0.5, None, ALU.mult)
                step(dve.tensor_tensor(half[:, 1, :], half[:, 1, :], half[:, 1, :], ALU.mult))
                step(dve.scalar_tensor_tensor(out=half[:, 2, :], in0=half[:, 2, :], scalar=4.0 / P,
                                              in1=half[:, 1, :], op0=ALU.mult, op1=ALU.add))

            def scale():
                n = norms[0]
                norms[0] += 1
                src, dst = NORMS[n]
                dve.wait_ge(std_ready, n + 1)
                step(dve.reciprocal(rstd[:, :], std[:, :]))
                if n == RMS:
                    dve.memset(shift[:, :], 0.0).then_inc(shift_ready, 1)
                else:
                    dve.scalar_tensor_tensor(out=shift[:, :], in0=mean[:, :], scalar=-1.0, in1=rstd[:, :],
                                             op0=ALU.mult, op1=ALU.mult).then_inc(shift_ready, 1)
                for b, on_act in enumerate(ON_ACT):
                    for m in range(b * TPC, (b + 1) * TPC):
                        if m in on_act:
                            continue
                        if n == RMS:
                            ins = dve.tensor_scalar(tile(dst, m), tile(src, m), rstd[:, m:m + 1], None, ALU.mult)
                        else:
                            ins = dve.tensor_scalar(tile(dst, m), tile(src, m), mean[:, m:m + 1],
                                                    rstd[:, m:m + 1], ALU.subtract, ALU.mult)
                    ins.then_inc(scaled_dve, 1)
                dve.wait_ge(scaled_dve, 4 * n + 4)
                dve.wait_ge(scaled_act, 4 * n + 4)

            def layer_norm():
                moments(NORMS[norms[0]][0])
                dve.tensor_scalar(var[:, :], half[:, 2, :], 0.25, EPS, ALU.mult, ALU.add).then_inc(var_ready, 1)
                scale()

            def rms_norm():
                moments(NORMS[norms[0]][0])
                step(dve.tensor_scalar(var[:, :], half[:, 2, :], 0.25, RMS_EPS, ALU.mult, ALU.add))
                step(dve.tensor_tensor(half[:, 0, :], mean[:, :], mean[:, :], ALU.mult))
                dve.tensor_tensor(var[:, :], var[:, :], half[:, 0, :], ALU.add).then_inc(var_ready, 1)
                scale()

            def along(row, n=NT):
                return row.unsqueeze(1).broadcast_to([P, n, P])

            def projected(k, dst, bias):
                for b in range(4):
                    dve.wait_ge(proj_ready, 4 * k + b + 1)
                    d = dst[:, b * CW:(b + 1) * CW]
                    if bias is None:
                        ins = dve.tensor_copy(d, ps[:, b, :])
                    else:
                        ins = dve.tensor_tensor(tiles(d), tiles(ps[:, b, :]), along(bias, TPC), ALU.add)
                step(ins)

            def add(dst, a, b):
                step(dve.tensor_tensor(dst, a, b, ALU.add))

            x, xh, y = X[:, :], XH[:, :], Y[:, :]
            dve.wait_ge(staging_cleared, 1)
            dve.wait_ge(ld_x, 16)
            layer_norm()
            rms_norm()

            def normalise(pair, r, p, plan=PLAN):
                hh, i = ROWS[r]
                R = pair * 2 * NT + r
                j, n, _ = plan[r]
                dve.wait_ge(a_read, pair * PER_PAIR + PROJ + j + n)
                q = r % 4
                dve.tensor_reduce(asum[:, q:q + 1], als[:, q, 0:n], X_AXIS, ALU.add).then_inc(a_sum, 1)
                dve.wait_ge(a_sum, R + 1)
                dve.reciprocal(arl[:, q:q + 1], asum[:, q:q + 1]).then_inc(a_rsum, 1)
                dve.wait_ge(a_rsum, R + 1)
                if not (is_int(R) and R < 4):
                    dve.wait_ge(a_pv, R - 3)
                dve.tensor_scalar(VR[:, q, :], VA[p][:, i * P + AD * hh:i * P + AD * hh + AD], arl[:, q:q + 1],
                                  None, ALU.mult).then_inc(a_vscaled, 1)

            def emit_pair(pair, p):
                first, last = is_int(pair) and pair == 0, is_int(pair) and pair == PAIRS - 1
                maxima = 0
                for r, (hh, i) in enumerate(ROWS):
                    R = pair * 2 * NT + r
                    j, n, _ = (LAST_PLAN if last else PLAN)[r]
                    q = r % 4
                    for ci, (c, off) in enumerate(row_chunks(i)):
                        dve.wait_ge(a_ready, pair * PER_PAIR + PROJ + j + ci + 1)
                        if n == 1:
                            dve.tensor_reduce(anm[:, q:q + 1], ps[:, (j + ci) % RING, off:], X_AXIS, ALU.max,
                                              negate=True).then_inc(a_negmax, 1)
                        else:
                            dve.tensor_reduce(amx[:, q, ci:ci + 1], ps[:, (j + ci) % RING, off:], X_AXIS, ALU.max
                                              ).then_inc(a_max, 1)
                            maxima += 1
                    if n > 1:
                        dve.wait_ge(a_max, pair * MAXIMA + maxima)
                        dve.tensor_reduce(anm[:, q:q + 1], amx[:, q, 0:n], X_AXIS, ALU.max, negate=True
                                          ).then_inc(a_negmax, 1)
                    if r == 0:
                        dve.wait_ge(a_vbiased, pair + 1)
                    if r:
                        normalise(pair, r - 1, p, LAST_PLAN if last else PLAN)
                    elif not first:
                        normalise(pair - 1, 2 * NT - 1, 1 - p)
                if last:
                    normalise(pair, 2 * NT - 1, p, LAST_PLAN)
            MAXIMA = 2 * sum(len(row_chunks(i)) for i in range(NT) if len(row_chunks(i)) > 1)
            run_pairs(dve, emit_pair)

            dve.wait_ge(ld_early, N_EARLY)
            dve.wait_ge(a_pv, 2 * NT * PAIRS)
            projected(0, y, bo_a[:, :])
            layer_norm()
            add(x, x, xh)
            layer_norm()

            dve.wait_ge(ld_late, N_LATE)

            def split(s):
                if s == 1:
                    dve.wait_ge(tables_loaded, 32)

                def rotate(n):
                    k, c = n // NC, n % NC
                    at = slice(c * CW, (c + 1) * CW)
                    dve.wait_ge(qkv_ready, QKV_BASE[1] + 8 * k + c + 1)
                    dve.tensor_tensor(T[2 * k][:, at], ps[:, c, :], COS[:, at], ALU.mult).then_inc(turned_cos, 1)
                    dve.wait_ge(qkv_ready, QKV_BASE[1] + 8 * k + 4 + c + 1)
                    dve.tensor_tensor(T[2 * k + 1][:, at], ps[:, 4 + c, :], SIN[:, at], ALU.mult
                                      ).then_inc(turned_sin, 1)

                def take_high(n):
                    dve.wait_ge(high_ready, 8 * s + n + 1)
                    if s == 1:
                        ins = dve.tensor_tensor(rest(n), rest(n), part(n, 0), ALU.subtract)
                    else:
                        ins = dve.scalar_tensor_tensor(out=rest(n), in0=ps[:, n, :],
                                                       scalar=bqk[:, s, n // NC:n // NC + 1], in1=part(n, 0),
                                                       op0=ALU.add, op1=ALU.subtract)
                    ins.then_inc(rest_ready, 1)

                def take_middle(n):
                    dve.wait_ge(mid_ready, 8 * s + n + 1)
                    dve.tensor_tensor(part(n, 2), rest(n), part(n, 1), ALU.subtract).then_inc(low_ready, 1)

                lag = 2 if s == 1 else 0
                for n in range(2 * NC + lag + 1):
                    if s == 1 and n < 2 * NC:
                        rotate(n)
                    if lag <= n < 2 * NC + lag:
                        take_high(n - lag)
                    if n > lag:
                        take_middle(n - lag - 1)

            def attention(s):
                def maxima(g):
                    for q in range(NT):
                        for j in range(NC):
                            dve.wait_ge(smax_ready, (g * NT + q) * NC + j + 1)
                            dve.tensor_reduce(mx[:, q, j:j + 1], ps[:, j, :], X_AXIS, ALU.max
                                              ).then_inc(smax_done, 1)
                    dve.wait_ge(smax_done, (g + 1) * NT * NC)
                    dve.tensor_reduce(nm[:, :], mx[:, :, :], X_AXIS, ALU.max, negate=True).then_inc(m_step, 1)
                    dve.wait_ge(m_step, g * 4 + 1)
                    dve.tensor_copy(mb[:, 0:NT], nm[:, :]).then_inc(m_step, 1)
                    dve.wait_ge(m_step, g * 4 + 2)
                    dve.tensor_tensor(nr[:, :], nm[:, :], mb[:, 0:NT], ALU.subtract).then_inc(m_step, 1)
                    dve.wait_ge(m_step, g * 4 + 3)
                    dve.tensor_copy(mb[:, NT:2 * NT], nr[:, :]).then_inc(m_step, 1)
                    dve.wait_ge(m_step, g * 4 + 4)
                    dve.tensor_tensor(mb[:, 2 * NT:3 * NT], nr[:, :], mb[:, NT:2 * NT], ALU.subtract).then_inc(m_ready, 1)

                def copy_rows(g, before):
                    dve.wait_ge(m_turned, g + 1)
                    if before:
                        dve.wait_ge(*before)
                    dve.tensor_copy(mT[:, :], ps[0:3 * NT, 0, 0:P // 2].bitcast(BF16)).then_inc(m_copied, 1)

                maxima(H * s)
                copy_rows(H * s, (max_rows[1], 16 * 8 * s) if s else None)

                def emit(h, p, k):
                    g = H * s + h
                    if is_int(h) and h == H - 1:
                        return
                    maxima(g + 1)
                    copy_rows(g + 1, (max_rows[p], (k + 8 * s + 1) * 16))
                run_heads(dve, emit)
                for c in range(NC):
                    at = slice(c * CW, (c + 1) * CW)
                    dve.wait_ge(z_loaded[c], 32 * (s + 1))
                    dve.reciprocal(ZS[:, at], ZS[:, at]).then_inc(z_inverted, 1)
                    dve.wait_ge(z_inverted, NC * s + c + 1)
                    dve.tensor_tensor(ZT[:, at], ZT[:, at], ZS[:, at], ALU.mult).then_inc(ctx_ready, 1)

            def gates(layer):
                dve.wait_ge(logits_ready, layer + 1)
                raw = ps[:, 4, 0:NT * 16].rearrange("p (t e) -> p t e", e=16)
                L, G = gl[:, :, 0:E0], ge[:, :, 0:E0]

                def wide(a, n=E0):
                    return a.unsqueeze(2).broadcast_to([P, NT, n])

                if layer:
                    dve.tensor_copy(L, raw[:, :, 0:E0])
                    step(dve.tensor_tensor(gl[:, :, E0:10], raw[:, :, E0:10],
                                           gb[:, E0:10].unsqueeze(1).broadcast_to([P, NT, 2]), ALU.add))
                else:
                    step(dve.tensor_tensor(L, raw[:, :, 0:E0], gb[:, 0:E0].unsqueeze(1).broadcast_to([P, NT, E0]),
                                           ALU.add))
                step(dve.tensor_reduce(gm[:, :], L, X_AXIS, ALU.max))
                if layer:
                    step(dve.tensor_reduce(g2[:, :], gl[:, :, E0:10], X_AXIS, ALU.max))
                    step(dve.tensor_tensor(gl[:, :, E0:10], gl[:, :, E0:10], wide(g2[:, :], 2), ALU.subtract))
                dve.tensor_tensor(L, L, wide(gm[:, :]), ALU.subtract).then_inc(shifted, 1)
                dve.wait_ge(gate_exp, layer + 1)
                step(dve.tensor_reduce(gs[:, :], G, X_AXIS, ALU.add))
                step(dve.reciprocal(gs[:, :], gs[:, :]))
                if not layer:
                    dve.tensor_tensor(WPE[:, :, 0:E0], G, wide(gs[:, :]), ALU.mult).then_inc(wgt_ready, 1)
                    return
                step(dve.tensor_tensor(gp[:, :, :], G, wide(gs[:, :]), ALU.mult))
                step(dve.tensor_reduce(gm[:, :], gp[:, :, :], X_AXIS, ALU.max))
                step(dve.tensor_tensor(gp[:, :, :], gp[:, :, :], wide(gm[:, :]), ALU.is_equal))
                step(dve.tensor_tensor(gp[:, :, :], gp[:, :, :], rank[:, :].unsqueeze(1).broadcast_to([P, NT, E0]),
                                       ALU.mult))
                step(dve.tensor_reduce(g2[:, :], gp[:, :, :], X_AXIS, ALU.max))
                step(dve.tensor_tensor(gp[:, :, :], gp[:, :, :], wide(g2[:, :]), ALU.is_equal))
                step(dve.tensor_reduce(gs[:, :], ge[:, :, E0:10], X_AXIS, ALU.add))
                step(dve.reciprocal(gs[:, :], gs[:, :]))
                step(dve.tensor_tensor(ge[:, :, E0:10], ge[:, :, E0:10], wide(gs[:, :], 2), ALU.mult))
                step(dve.tensor_tensor(gm[:, :], gm[:, :], ge[:, :, E0], ALU.mult))
                dve.tensor_tensor(WPE[:, :, 0:E0], gp[:, :, :], wide(gm[:, :]), ALU.mult)
                dve.tensor_copy(wgt[:, E0, :], ge[:, :, E0 + 1]).then_inc(wgt_ready, 1)

            def mixture(layer, n):
                gates(layer)
                for b in range(4):
                    dve.wait_ge(b2_ready, 4 * layer + b + 1)
                    ins = dve.tensor_copy(ACC[:, b * CW:(b + 1) * CW], ps[:, 4 + b, :])
                ins.then_inc(acc_started, 1)
                dve.wait_ge(acc_started, layer + 1)
                scalars = wgt[:, :, :].rearrange("p e t -> p (e t)")

                def emit(e, p, k):
                    for c in range(NC):
                        chunk = (e + E0 * layer) * NC + c
                        dve.wait_ge(y_ready, chunk + 1)
                        if not (is_int(chunk) and chunk < 1):
                            dve.wait_ge(y_used, chunk)
                        for m in range(TPC):
                            a = tile(ACC, c * TPC + m)
                            ins = dve.scalar_tensor_tensor(
                                out=a, in0=ps[:, 4 + c % 2, m * P:(m + 1) * P],
                                scalar=scalars[:, bass.ds(e * NT + c * TPC + m, 1)], in1=a, op0=ALU.mult, op1=ALU.add)
                        ins.then_inc(y_used, 1)
                run_experts(dve, n, emit)
                dve.wait_ge(y_used, (E0 * layer + n) * NC)

            split(0)
            attention(0)
            projected(1, y, bo[:, 0, :])
            add(y, y, CM)
            layer_norm()
            step(dve.tensor_tensor(tiles(CM), tiles(xh), along(lnrow[:, 0, :]), ALU.mult))
            step(dve.tensor_tensor(tiles(CM), tiles(CM), along(lnrow[:, 1, :]), ALU.add))
            mixture(0, E0)
            add(y, CM, ACC)
            layer_norm()
            step(dve.tensor_tensor(tiles(xh), tiles(xh), along(lnrow[:, 2, :]), ALU.mult))
            step(dve.tensor_tensor(tiles(y), tiles(xh), along(lnrow[:, 3, :]), ALU.add))
            layer_norm()
            add(x, x, xh)
            layer_norm()
            split(1)
            attention(1)
            projected(2, y, None)
            layer_norm()
            add(x, x, xh)
            layer_norm()
            layer_norm()
            split(2)
            attention(2)
            projected(3, y, bo[:, 1, :])
            add(CM, CM, y)
            layer_norm()
            mixture(1, E1)
            add(y, CM, ACC)
            layer_norm()
            dve.tensor_tensor(x, x, xh, ALU.add).then_inc(final_ready, 1)


def kernel(**inputs):
    import numpy as np
    import concourse.bacc as bacc
    from concourse import mybir as _mybir
    from concourse.bass_utils import run_bass_kernel_spmd

    g = {k: np.asarray(v) for k, v in inputs.items()}
    a = {}
    a["x"] = g["L0_attn_x"].reshape(S, P)
    w = g["L0_attn_W_qkv"].reshape(PAIRS, 2, AD, 3, P)
    a["a_w"] = w.transpose(0, 4, 3, 1, 2).reshape(PAIRS, P, 3 * P)
    b = g["L0_attn_b_qkv"].reshape(PAIRS, 2 * AD, 3)
    a["a_bqk"] = b[:, :, 0:2]
    a["a_bv"] = b[:, :, 2]
    a["a_wo"] = g["L0_attn_W_o"].T.reshape(PAIRS, P, P).transpose(1, 0, 2).reshape(P, PAIRS * P)
    a["a_bo"] = g["L0_attn_b_o"]
    a["conv_w"] = g["L0_ffn_conv_w"].transpose(1, 2, 0).reshape(P, 3 * P)
    a["conv_b"] = g["L0_ffn_conv_b"].reshape(P, 1)
    a["wqkv0"] = g["L0_ffn_wqkv"].T
    a["wqkv1"] = g["L1_attn_w_qkv"]
    a["wqkv2"] = g["L1_ffn_Wqkv"]
    for n, name in (("0", "L0_ffn_bqkv"), ("2", "L1_ffn_bqkv")):
        b = g[name].reshape(3, P)
        a["bqk" + n] = b[0:2].T
        a["bv" + n] = b[2]
    a["wo0"], a["bo0"] = g["L0_ffn_wo"].T, g["L0_ffn_bo"]
    a["wo1"] = g["L1_attn_w_proj"]
    a["wo2"], a["bo2"] = g["L1_ffn_Wo"], g["L1_ffn_bo"]
    a["ln_b1_g"], a["ln_b1_b"] = g["L0_ffn_ln1_g"], g["L0_ffn_ln1_b"]
    a["ln_b2_g"], a["ln_b2_b"] = g["L0_ffn_ln2_g"], g["L0_ffn_ln2_b"]
    a["lncol"] = np.stack([g["L0_ffn_ln1_g"], g["L0_ffn_ln1_b"], g["L1_ffn_ln1_g"], g["L1_ffn_ln1_b"],
                           g["L1_ffn_ln2_g"], g["L1_ffn_ln2_b"]], axis=1)
    a["gate_w0"] = g["L0_ffn_gate_w"]
    a["gate_w1"] = np.concatenate([g["L1_ffn_gate_w"], g["L1_ffn_coef_w"]], axis=1)
    a["gate_b"], a["coef_b"] = g["L0_ffn_gate_b"], g["L1_ffn_coef_b"]
    a["b2_0"] = g["L0_ffn_b2"]
    a["b2_1"] = np.concatenate([g["L1_ffn_b2"], g["L1_ffn_rb2"][None]], axis=0)
    a["w1"] = np.concatenate([g["L0_ffn_w1"], g["L1_ffn_W1"], g["L1_ffn_rW1"][None]], axis=0)
    w2 = np.concatenate([g["L0_ffn_w2"], g["L1_ffn_W2"], g["L1_ffn_rW2"][None]], axis=0)
    a["w2"] = w2.reshape(-1, FC, P, P).transpose(0, 2, 1, 3).reshape(-1, P, FC * P)
    b1 = np.concatenate([g["L0_ffn_b1"], g["L1_ffn_b1"], g["L1_ffn_rb1"][None]], axis=0)
    a["b1"] = b1.reshape(-1, FC, P).transpose(0, 2, 1)
    inv_freq = (np.float32(1.0) / np.float32(10000.0) ** (np.arange(0, DH, 2, dtype=np.float32) / np.float32(DH))
                ).astype(np.float32)
    freqs = np.arange(S, dtype=np.float32)[:, None] * inv_freq[None, :]
    a["cos"] = np.tile(np.repeat(np.cos(freqs), 2, axis=1), (1, H)).T
    a["sin"] = np.tile(np.repeat(np.sin(freqs), 2, axis=1), (1, H)).T
    a["rank"] = np.arange(E0, 0, -1).astype(np.float32)
    bf = _mybir.dt.np(BF16) if hasattr(_mybir.dt, "np") else np.dtype("bfloat16")
    a["ones"] = np.ones((3, S), dtype=bf)
    a["zeros"] = np.zeros((H, 3, S), dtype=bf)

    nc = bacc.Bacc("TRN2", target_bir_lowering=False, num_devices=1)
    arrays, t = {}, {}
    for name, v in a.items():
        v = np.ascontiguousarray(v)
        arrays[f"in_{name}"] = v
        t[name] = nc.dram_tensor(f"in_{name}", v.shape, _mybir.dt.from_np(v.dtype), kind="ExternalInput").ap()
    out = nc.dram_tensor("out_0", (S, P), F32, kind="ExternalOutput").ap()
    sandwich_kernel(nc, t, out)
    r = run_bass_kernel_spmd(nc, [arrays], core_ids=[0])
    return r.results[0]["out_0"].reshape(1, S, P)
```

```python
from contextlib import ExitStack

import concourse.bass as bass
from concourse import mybir

F32 = mybir.dt.float32
F32R = mybir.dt.float32r
BF16 = mybir.dt.bfloat16
ALU = mybir.AluOpType
ACT = mybir.ActivationFunctionType
X_AXIS = mybir.AxisListType.X

P = 128
S = 2048
NT = S // P
CW = 512
NC = S // CW
TPC = CW // P
EPS = 1e-5
RMS_EPS = 1.1920929e-07
MASKED = -1e30

AD = 64
PAIRS = 8
RING = 6
LAG = 3
QK, VP = NC, 2
PROJ = VP + QK
PROJ_AFTER = {2: 0, 3: 1, 4: 2, 5: 3, 6: 4, 7: 5}

H = 16
DH = 8
SLOTS = 6
MROW = SLOTS * DH
VC = 32
SCALE = float(DH) ** -0.5

E0, E1 = 8, 9
FFN = 512
FC = FFN // P

def row_chunks(i):
    return [(c, P * (i % TPC) if c == i // TPC else 0) for c in range(i // TPC, NC)]


FIRST_CHUNK = [sum(len(row_chunks(m)) for m in range(i)) for i in range(NT)]
PER_HEAD = sum(len(row_chunks(i)) for i in range(NT))
USERS = []
for _i in range(NT):
    USERS += [("scores", FIRST_CHUNK[_i] + ci) for ci in range(len(row_chunks(_i)))]
    USERS += [("projection", PROJ_AFTER[_i])] if _i in PROJ_AFTER else []


def taken_after(i):
    return [n for row, n in PROJ_AFTER.items() if i == row + 1]


def place(kind, n):
    return USERS.index((kind, n))


def ring_bank(kind, n):
    return place(kind, n) % RING


def user_before(j, first, last):
    q = j - RING
    while q >= 0 and last and USERS[q][0] == "projection":
        q -= RING
    if q >= 0:
        return USERS[q] + (False,)
    return None if first else USERS[max(q for q in range(len(USERS)) if q % RING == j % RING)] + (True,)


def run_heads(eng, emit):
    emit(0, 0, 0)
    with eng.Fori(0, (H - 2) // 2) as i:
        emit(i * 2 + 1, 1, i)
        emit(i * 2 + 2, 0, i + 1)
    emit(H - 1, 1, H // 2 - 1)


def run_experts(eng, n, emit):
    emit(0, 0, 0)
    emit(1, 1, 0)
    with eng.Fori(0, 3) as i:
        emit(i * 2 + 2, 0, i + 1)
        emit(i * 2 + 3, 1, i + 1)
    if n == E1:
        emit(8, 0, 4)


MAX_FROM, MAX_GROUPS = 2, 12


def max_products(kt, c):
    slot, slots, n = (kt - MAX_FROM) * NC + c, MAX_GROUPS * NC, NT * NC
    if not 0 <= slot < slots:
        return []
    return [(m // NC, m % NC) for m in range(slot * n // slots, (slot + 1) * n // slots)]


ST_RING = 3


def st_bank(m):
    return 4 + m % ST_RING


def st_read_before(m):
    n = NT * NC
    return m - ST_RING + 1 if m >= ST_RING else max(j for j in range(-n, 0) if (j + n) % ST_RING == m % ST_RING) + 1


def is_int(x):
    return isinstance(x, int)


def sandwich_kernel(nc, t, out):
    ctx = ExitStack()
    with ctx:
        def sb(name, shape, dt=F32):
            return ctx.enter_context(nc.sbuf_tensor(name, shape, dt))

        def sem(name):
            return ctx.enter_context(nc.semaphore(name))

        q_dram = nc.dram_tensor("q_dram", (3, H, 3 * DH + 3, S), BF16, kind="Internal").ap()
        k_dram = nc.dram_tensor("k_dram", (3, H, 3 * DH, S), BF16, kind="Internal").ap()
        z_dram = nc.dram_tensor("z_dram", (3, H, P, CW), F32, kind="Internal").ap()

        ps = ctx.enter_context(nc.psum_tensor("ps", [P, 8, CW], F32))

        X = sb("X", [P, S])
        XH = sb("XH", [P, S])
        XTp = sb("XTp", [P, S + 2])
        XT = XTp[:, 1:S + 1]
        Y = sb("Y", [P, S])
        probs = sb("probs", [P, 4, S])
        arena = sb("arena", [P, 15 * S // 2])
        QS = [sb(f"QS{p}", [P, S], BF16) for p in range(2)]
        KS = [sb(f"KS{p}", [P, S], BF16) for p in range(2)]
        VS = sb("VS", [P, 2, NT, VC])
        QA = [sb(f"QA{p}", [P, S], F32R) for p in range(2)]
        QB = [sb(f"QB{p}", [P, S], F32R) for p in range(2)]
        KA = [sb(f"KA{p}", [P, S], F32R) for p in range(2)]
        VA = [Y[:, 0:NT * AD], Y[:, NT * AD:2 * NT * AD]]
        ZA = [arena[:, n * S:(n + 1) * S] for n in range(PAIRS - 1)] + [XH[:, :]]

        def z_place(pair, hh, c):
            if is_int(pair):
                return ZA[pair][AD * hh:AD * hh + AD, c * CW:(c + 1) * CW]
            return arena[AD * hh:AD * hh + AD, bass.ds(pair * S + c * CW, CW)]
        Z_ACT, Z_DVE = (0, 1), (2, 3)
        CT = arena[:, 0 * S:1 * S]
        CM = arena[:, 1 * S:2 * S]
        T = [arena[:, (2 + n) * S:(3 + n) * S] for n in range(4)]
        ZT, ZS = T[0], T[1]
        COS, SIN = CT, probs[:, 0, :]
        flat = probs[:, :, :].rearrange("p a t -> p (a t)")
        PARTS = [flat[:, S:5 * S // 2].bitcast(BF16), flat[:, 5 * S // 2:4 * S].bitcast(BF16)]
        ACC = T[2]
        VALL = Y
        HT = [probs[:, 0, :], probs[:, 1, :]]
        W1S = [probs[:, 2, 0:FFN], probs[:, 2, FFN:2 * FFN]]
        W2S = [probs[:, 2, 2 * FFN:3 * FFN], probs[:, 2, 3 * FFN:4 * FFN]]
        ZST = T[3][:, 0:2 * CW].rearrange("p (n c) -> p n c", n=2)
        late = arena[:, 6 * S:15 * S // 2]
        B1S = sb("B1S", [P, 2, FC])
        WT = probs[0:E1, 3, :]

        w_a = sb("w_a", [P, 3 * AD])
        bqk_a = sb("bqk_a", [P, 1])
        bv_a = sb("bv_a", [P, AD])
        wo_a = VS[:, :, :, :].rearrange("p a t c -> p (a t c)")
        bo_a = sb("bo_a", [P, P])
        conv_w = late[:, 0:3 * P]
        conv_b = sb("conv_b", [P, 1])
        wqkv = late[:, 3 * P:12 * P].rearrange("p (s n) -> p s n", s=3)
        wrot = late[:, 12 * P:14 * P]
        bqk = sb("bqk", [P, 3, 2])
        bv = late[:, 14 * P:16 * P].rearrange("p (s n) -> p s n", s=2)
        wo = late[:, 16 * P:19 * P].rearrange("p (s n) -> p s n", s=3)
        bo = late[:, 19 * P:21 * P].rearrange("p (s n) -> p s n", s=2)
        lnrow = sb("lnrow", [P, 4, P])
        lncol = sb("lncol", [P, 6])
        gw = sb("gw", [P, 2, 10])
        gb = sb("gb", [P, 10])
        rank = sb("rank", [P, E0])
        b2s = sb("b2s", [E1, 2, P])
        ident = sb("ident", [P, P])
        identb = sb("identb", [P, P], BF16)
        maskb = sb("maskb", [P, P], BF16)

        stats = sb("stats", [P, NT, 6])
        mean = sb("mean", [P, NT])
        shift = sb("shift", [P, NT])
        half = sb("half", [P, 3, NT])
        idle = sb("idle", [P, 1])
        ones = sb("ones", [P, 1])
        var = sb("var", [P, NT])
        std = sb("std", [P, NT])
        rstd = sb("rstd", [P, NT])
        amx = sb("amx", [P, 4, NC])
        anm = sb("anm", [P, 4])
        als = sb("als", [P, 4, NC])
        asum = sb("asum", [P, 4])
        arl = sb("arl", [P, 4])
        VR = sb("VR", [P, 4, AD])
        mx = sb("mx", [P, NT, NC])
        nm = sb("nm", [P, NT])
        nr = sb("nr", [P, NT])
        mb = sb("mb", [P, P], BF16)
        mT = sb("mT", [3 * NT, P], BF16)
        gl = sb("gl", [P, NT, 10])
        ge = sb("ge", [P, NT, 10])
        gp = sb("gp", [P, NT, E0])
        gm = sb("gm", [P, NT])
        gs = sb("gs", [P, NT])
        g2 = sb("g2", [P, NT])
        wgt = sb("wgt", [P, E1, NT])
        WPE = wgt[:, :, :].rearrange("p e t -> p t e")

        ld_x = sem("ld_x")
        ld_early = sem("ld_early")
        ld_late = sem("ld_late")
        consts_made = sem("consts_made")
        pool_step = sem("pool_step")
        dve_step = sem("dve_step")
        ones_loaded = sem("ones_loaded")
        staging_cleared = sem("staging_cleared")
        tables_loaded = sem("tables_loaded")
        wrot_made = sem("wrot_made")
        var_ready = sem("var_ready")
        std_ready = sem("std_ready")
        shift_ready = sem("shift_ready")
        scaled_dve = sem("scaled_dve")
        scaled_act = sem("scaled_act")
        turned = sem("turned")
        turned_out = sem("turned_out")
        proj_ready = sem("proj_ready")
        conv_ready = sem("conv_ready")
        conv_out = sem("conv_out")
        a_weights = sem("a_weights")
        a_ready = sem("a_ready")
        a_max = sem("a_max")
        a_negmax = sem("a_negmax")
        a_read = sem("a_read")
        a_sum = sem("a_sum")
        a_rsum = sem("a_rsum")
        a_vscaled = sem("a_vscaled")
        a_projected = sem("a_projected")
        a_high = sem("a_high")
        a_used = sem("a_used")
        a_swapped = sem("a_swapped")
        a_pv = sem("a_pv")
        a_zout_act = sem("a_zout_act")
        a_zout_dve = sem("a_zout_dve")
        qkv_ready = sem("qkv_ready")
        v_out = sem("v_out")
        high_ready = sem("high_ready")
        rest_ready = sem("rest_ready")
        mid_ready = sem("mid_ready")
        low_ready = sem("low_ready")
        turned_cos = sem("turned_cos")
        turned_sin = sem("turned_sin")
        rotated = sem("rotated")
        zeros_stored = sem("zeros_stored")
        parts_stored = sem("parts_stored")
        v_biased = sem("v_biased")
        qk_staged = [sem(f"qk_staged{p}") for p in range(2)]
        max_rows = [sem(f"max_rows{p}") for p in range(2)]
        smax_ready = sem("smax_ready")
        smax_done = sem("smax_done")
        m_step = sem("m_step")
        m_ready = sem("m_ready")
        m_turned = sem("m_turned")
        m_copied = sem("m_copied")
        st_ready = sem("st_ready")
        exp_done = sem("exp_done")
        pv_done = sem("pv_done")
        z_copied = sem("z_copied")
        z_stored = [sem(f"z_stored{p}") for p in range(2)]
        z_loaded = [sem(f"z_loaded{c}") for c in range(NC)]
        z_inverted = sem("z_inverted")
        v_staged = sem("v_staged")
        ctx_ready = sem("ctx_ready")
        logits_ready = sem("logits_ready")
        shifted = sem("shifted")
        gate_exp = sem("gate_exp")
        wgt_ready = sem("wgt_ready")
        wgt_turned = sem("wgt_turned")
        wgt_out = sem("wgt_out")
        b2_ready = sem("b2_ready")
        acc_started = sem("acc_started")
        w_staged = [sem(f"w_staged{p}") for p in range(2)]
        h_ready = sem("h_ready")
        h_out = sem("h_out")
        y_ready = sem("y_ready")
        y_used = sem("y_used")
        final_ready = sem("final_ready")
        stored = sem("stored")

        def bc(ap):
            return ap.partition_broadcast(P)

        EARLY_LOADS = [(wo_a, t["a_wo"]), (bo_a[:, :], bc(t["a_bo"]))]
        LATE_LOADS = [
            (conv_w, t["conv_w"]), (conv_b[:, :], t["conv_b"]),
            (wqkv[:, 0, :], t["wqkv0"]), (wqkv[:, 1, :], t["wqkv1"]), (wqkv[:, 2, :], t["wqkv2"]),
            (bqk[:, 0, :], t["bqk0"]), (bqk[:, 2, :], t["bqk2"]),
            (bv[:, 0, :], bc(t["bv0"])), (bv[:, 1, :], bc(t["bv2"])),
            (wo[:, 0, :], t["wo0"]), (wo[:, 1, :], t["wo1"]), (wo[:, 2, :], t["wo2"]),
            (bo[:, 0, :], bc(t["bo0"])), (bo[:, 1, :], bc(t["bo2"])),
            (lnrow[:, 0, :], bc(t["ln_b1_g"])), (lnrow[:, 1, :], bc(t["ln_b1_b"])),
            (lnrow[:, 2, :], bc(t["ln_b2_g"])), (lnrow[:, 3, :], bc(t["ln_b2_b"])),
            (lncol[:, :], t["lncol"]),
            (gw[:, 0, 0:E0], t["gate_w0"]), (gw[:, 1, :], t["gate_w1"]),
            (gb[:, 0:E0], bc(t["gate_b"])), (gb[:, E0:10], bc(t["coef_b"])),
            (rank[:, :], bc(t["rank"])),
            (b2s[0:E0, 0, :], t["b2_0"]), (b2s[:, 1, :], t["b2_1"]),
        ]
        N_EARLY, N_LATE = 16 * len(EARLY_LOADS), 16 * len(LATE_LOADS)

        LNCOL = {3: (0, 1), 5: (2, 3), 6: (4, 5)}
        TURN = [(XH, XT), (XH, XT), (CT, CM), (XH, XT), (XH, XT), (XH, XT), (XH, XT)]
        NORMS = [(X, XH), (XH, XH), (Y, XH), (X, XH), (Y, XH), (Y, XH), (Y, XH), (X, XH), (Y, XH),
                 (X, CM), (CM, XH), (CM, XH), (Y, XH)]
        RMS = 1
        NORM_OF = {0: 1, 1: 3, 3: 4, 4: 7, 5: 10, 6: 11}
        ON_ACT = [(3,), (6, 7), (11,), (14, 15)]
        BLOCKS = [["q", "k", "v"], ["q", "qr", "k", "kr", "v"], ["q", "k", "v"]]
        QKV_BASE = [0, 12, 32, 44]
        QKV_SRC = [CT, XT, XT]

        def part(n, which):
            at = which * S + (n % NC) * CW
            return PARTS[n // NC][:, at:at + CW]

        def rest(n):
            return T[2 * (n // NC)][:, (n % NC) * CW:(n % NC + 1) * CW]

        N_STAGE_DMA = 8

        block = ctx.enter_context(nc.Block())

        @block.sync
        def _(sp):
            sp.dma_start(X[:, :].rearrange("p (t d) -> p t d", d=P),
                         t["x"].rearrange("(t p) d -> p t d", p=P)).then_inc(ld_x, 16)

            def load_head(n):
                if not (is_int(n) and n == 0):
                    sp.wait_ge(a_used, PROJ * n)
                at = bass.ds(n, 1)
                sp.dma_start(w_a[:, :], t["a_w"][at].rearrange("a p n -> (a p) n")).then_inc(a_weights, 16)
                sp.dma_start(bqk_a[:, :], t["a_bqk"][at].rearrange("a p n -> (a p) n")).then_inc(a_weights, 16)
                sp.dma_start(bv_a[:, :], t["a_bv"][at].rearrange("a n -> (a n)").partition_broadcast(P)
                             ).then_inc(a_weights, 16)

            load_head(0)
            for dst, src in EARLY_LOADS:
                sp.dma_start(dst, src).then_inc(ld_early, 16)
            for s in range(3):
                sp.dma_start(q_dram[s, :, 3 * DH:, :], t["zeros"]).then_inc(zeros_stored, 16)
            sp.wait_ge(staging_cleared, 1)
            for p in range(2):
                sp.dma_start(KS[p][MROW:MROW + 3, :], t["ones"]).then_inc(ones_loaded, 16)
            with sp.Fori(1, H) as n:
                load_head(n)

            def stage(s, h, p):
                at = bass.ds(h, 1)

                def rows(dst, row, src, a, b):
                    sp.dma_start(dst[p][row:row + b - a, :], src[s, at, a:b].rearrange("a d t -> (a d) t")
                                 ).then_inc(qk_staged[p], 16)

                rows(QS, 0, q_dram, 0, 2 * DH)
                rows(KS, DH, k_dram, 0, 3 * DH)
                rows(KS, 0, k_dram, 0, DH)
                rows(QS, 2 * DH, q_dram, 0, DH)
                rows(QS, 3 * DH, q_dram, 0, 2 * DH)
                rows(KS, 4 * DH, k_dram, DH, 2 * DH)
                rows(KS, 5 * DH, k_dram, 0, DH)
                rows(QS, 5 * DH, q_dram, 2 * DH, 3 * DH + 3)

            def put_max_rows(g, p):
                sp.wait_ge(m_copied, g + 1)
                sp.dma_start(QS[p][MROW:MROW + 3, :], mT[:, :]).then_inc(max_rows[p], 16)

            def store_z(s, h, g, p):
                sp.wait_ge(z_copied, g + 1)
                sp.dma_start(z_dram[s, bass.ds(h, 1)].rearrange("a p t -> (a p) t"), ZST[:, p, :]
                             ).then_inc(z_stored[p], 16)

            def experts(layer, n):
                def emit(e, p, k):
                    x = E0 * layer + e
                    if is_int(x) and x < 2:
                        sp.wait_ge(pv_done, NT * H)
                    elif is_int(e) and e < 2:
                        sp.wait_ge(pv_done, NT * H * 3)
                    if not (is_int(e) and e < 2):
                        sp.wait_ge(y_ready, x * NC - NC)
                    at = bass.ds(x, 1)
                    sp.dma_start(W1S[p], t["w1"][at].rearrange("a p n -> (a p) n")).then_inc(w_staged[p], 16)
                    sp.dma_start(W2S[p], t["w2"][at].rearrange("a p n -> (a p) n")).then_inc(w_staged[p], 16)
                    sp.dma_start(B1S[:, p, :], t["b1"][at].rearrange("a p n -> (a p) n")).then_inc(w_staged[p], 16)
                run_experts(sp, n, emit)

            def attention(s):
                for n, dram in enumerate((q_dram, k_dram)):
                    for part, done, count in ((0, high_ready, 8 * s + 4 * n + 4), (1, mid_ready, 8 * s + 4 * n + 4),
                                              (2, low_ready, 8 * s + 4 * n + 4)):
                        sp.wait_ge(done, count)
                        sp.dma_start(dram[s, :, part * DH:(part + 1) * DH, :], PARTS[n][:, part * S:(part + 1) * S]
                                     ).then_inc(parts_stored, 16)
                sp.wait_ge(parts_stored, 96 * (s + 1))
                sp.wait_ge(zeros_stored, 48)
                stage(s, 0, 0)
                stage(s, 1, 1)
                put_max_rows(H * s, 0)

                def emit(h, p, k):
                    g = H * s + h
                    first, last = is_int(h) and h == 0, is_int(h) and h == H - 1
                    if not first and not last:
                        sp.wait_ge(st_ready, g * NC * NT)
                        stage(s, h + 1, 1 - p)
                    if not first:
                        store_z(s, h - 1, g - 1, 1 - p)
                    if not last:
                        put_max_rows(g + 1, 1 - p)
                    if last:
                        store_z(s, h, g, p)
                run_heads(sp, emit)
                for p in range(2):
                    sp.wait_ge(z_stored[p], 16 * (H // 2) * (s + 1))
                for c in range(NC):
                    for n, dst in enumerate((ZS, ZT)):
                        row = 32 * c + DH * (1 - n)
                        sp.dma_start(dst[:, c * CW:(c + 1) * CW], z_dram[s, :, row:row + DH, :]
                                     ).then_inc(z_loaded[c], 16)

            sp.wait_ge(proj_ready, 4)
            for dst, src in LATE_LOADS:
                sp.dma_start(dst, src).then_inc(ld_late, 16)
            attention(0)
            experts(0, E0)
            sp.wait_ge(y_ready, NC * E0)
            sp.dma_start(COS, t["cos"]).then_inc(tables_loaded, 16)
            sp.dma_start(SIN, t["sin"]).then_inc(tables_loaded, 16)
            attention(1)
            attention(2)
            experts(1, E1)
            sp.wait_ge(final_ready, 1)
            sp.dma_start(out.rearrange("(t p) d -> p t d", p=P),
                         X[:, :].rearrange("p (t d) -> p t d", d=P)).then_inc(stored, 16)
            sp.wait_ge(stored, 16)

        @block.gpsimd
        def _(pool):
            steps = [0]

            def step(ins):
                ins.then_inc(pool_step, 1)
                steps[0] += 1
                pool.wait_ge(pool_step, steps[0])

            pool.memset(XTp[:, 0:1], 0.0)
            pool.memset(XTp[:, S + 1:S + 2], 0.0)
            pool.memset(ident[:, :], 0.0)
            pool.memset(identb[:, :], 0.0)
            step(pool.memset(maskb[:, :], 0.0))
            pool.affine_select(out=ident[:, :], in_=ident[:, :], compare_op=ALU.not_equal, fill=1.0,
                               base=0, pattern=[[-1, P]], channel_multiplier=1)
            pool.affine_select(out=identb[:, :], in_=identb[:, :], compare_op=ALU.not_equal, fill=1.0,
                               base=0, pattern=[[-1, P]], channel_multiplier=1)
            pool.affine_select(out=maskb[:, :], in_=maskb[:, :], compare_op=ALU.is_ge, fill=MASKED,
                               base=0, pattern=[[1, P]], channel_multiplier=-1).then_inc(consts_made, 1)
            for p in range(2):
                pool.memset(QS[p][:, :], 0.0)
                pool.memset(KS[p][:, :], 0.0)
            pool.memset(mb[:, :], 0.0)
            pool.memset(ones[:, :], 1.0)
            pool.memset(idle[:, :], 1.0).then_inc(staging_cleared, 1)
            pool.wait_ge(staging_cleared, 1)

            def swap(head, p):
                for n in range(QK):
                    pool.wait_ge(a_used, head * PROJ + VP + n + 1)
                    at = slice(n * CW, (n + 1) * CW)
                    for a, b in ((slice(0, AD), slice(AD, P)), (slice(AD, P), slice(0, AD))):
                        ins = pool.tensor_tensor(QB[p][a, at], QA[p][b, at].bitcast(F32),
                                                 ones[b, :].broadcast_to([AD, CW]), ALU.mult)
                    ins.then_inc(a_swapped, 1)

            swap(0, 0)

            def emit_head(h, p, k):
                if not (is_int(h) and h == H - 1):
                    swap(h + 1, 1 - p)
            run_heads(pool, emit_head)
            pool.wait_ge(proj_ready, 4)
            step(pool.memset(VS[:, :, :, :], 1.0))

            def attention(s):
                if s == 1:
                    for n in range(2 * NC):
                        pool.wait_ge(turned_sin, n + 1)
                        q = T[0][:, n * CW:(n + 1) * CW] if n < NC else T[2][:, (n - NC) * CW:(n - NC + 1) * CW]
                        r = T[1][:, n * CW:(n + 1) * CW] if n < NC else T[3][:, (n - NC) * CW:(n - NC + 1) * CW]
                        pool.tensor_tensor(q, q, r, ALU.add).then_inc(rotated, 1)
                pool.wait_ge(ld_late, N_LATE)
                pool.wait_ge(v_out, 4 * (s + 1))
                if s != 1:
                    v = VALL[:, :].rearrange("p (t d) -> p t d", d=P)
                    pool.tensor_tensor(v, v, bv[:, s // 2, :].unsqueeze(1).broadcast_to([P, NT, P]), ALU.add
                                       ).then_inc(v_biased, 1)
                    pool.wait_ge(v_biased, s // 2 + 1)

                def emit(h, p, k):
                    g = H * s + h
                    if not is_int(g) or g >= 2:
                        pool.wait_ge(pv_done, (g - 1) * NT)
                    src = VALL[:, :].rearrange("p (t d) -> p t d", d=P)[:, :, bass.ds(h * DH, DH)]
                    pool.tensor_copy(VS[:, p, :, 0:DH], src).then_inc(v_staged, 1)
                run_heads(pool, emit)

            attention(0)
            pool.wait_ge(ld_late, N_LATE)
            src = wqkv[:, 1, 0:2 * P].rearrange("p (n two) -> p n two", two=2)
            dst = wrot.rearrange("p (n two) -> p n two", two=2)
            pool.tensor_scalar(dst[:, :, 0], src[:, :, 1], -1.0, None, ALU.mult)
            pool.tensor_copy(dst[:, :, 1], src[:, :, 0]).then_inc(wrot_made, 1)
            attention(1)
            attention(2)

        @block.scalar
        def _(act):
            def copy(out_, in_, bias=0.0, scale=1.0):
                return act.activation(out_, in_, ACT.Identity, bias=bias, scale=scale)

            def normalise(n):
                act.activation(idle[:, :], idle[:, :], ACT.Sqrt)
                act.wait_ge(var_ready, n + 1)
                act.activation(std[:, :], var[:, :], ACT.Sqrt).then_inc(std_ready, 1)
                act.wait_ge(shift_ready, n + 1)
                src, dst = NORMS[n]
                for tiles_ in ON_ACT:
                    for m in tiles_:
                        ins = copy(dst[:, m * P:(m + 1) * P], src[:, m * P:(m + 1) * P], shift[:, m:m + 1],
                                   rstd[:, m:m + 1])
                    ins.then_inc(scaled_act, 1)

            def turn_out(k):
                bias, scale = 0.0, 1.0
                if k in LNCOL:
                    g, b = LNCOL[k]
                    act.wait_ge(ld_late, N_LATE)
                    scale, bias = lncol[:, g:g + 1], lncol[:, b:b + 1]
                for b_ in range(4):
                    act.wait_ge(turned, 4 * k + b_ + 1)
                    copy(TURN[k][1][:, b_ * CW:(b_ + 1) * CW], ps[:, b_, :], bias, scale).then_inc(turned_out, 1)

            def high_parts(head, n, p, bank):
                act.wait_ge(a_projected, head * PROJ + VP + n + 1)
                at = slice(n * CW, (n + 1) * CW)
                copy(QA[p][0:AD, at], ps[0:AD, bank, :], bqk_a[0:AD, :])
                copy(KA[p][AD:P, at], ps[AD:P, bank, :], bqk_a[AD:P, :]).then_inc(a_high, 1)

            act.wait_ge(staging_cleared, 1)
            normalise(0)
            normalise(1)
            turn_out(0)
            act.wait_ge(a_weights, 48)
            for n in range(QK):
                high_parts(0, n, 0, 4 + (VP + n) % 4)

            def z_out(head, pair, hh):
                act.wait_ge(a_pv, (head + 1) * NT)
                for c in Z_ACT:
                    ins = copy(z_place(pair, hh, c), ps[AD * (c % 2):AD * (c % 2) + AD, 6 + c // 2, :])
                ins.then_inc(a_zout_act, 1)

            def emit_head(h, p, k):
                first, last = is_int(h) and h == 0, is_int(h) and h == H - 1
                for i in range(NT):
                    R = h * NT + i
                    if i == LAG and not first:
                        z_out(h - 1, k if p else k - 1, 1 - p)
                    act.wait_ge(a_negmax, R + 1)
                    if not (first and i < 4):
                        act.wait_ge(a_pv, R - 3)
                    for ci, (c, off) in enumerate(row_chunks(i)):
                        act.activation(probs[:, i % 4, c * CW + off:(c + 1) * CW],
                                       ps[:, ring_bank("scores", FIRST_CHUNK[i] + ci), off:],
                                       ACT.Exp, bias=anm[:, i % 4:i % 4 + 1],
                                       accum_out=als[:, i % 4, ci:ci + 1]).then_inc(a_read, 1)
                    n = PROJ_AFTER.get(i, -1)
                    if n >= VP and not last:
                        high_parts(h + 1, n - VP, 1 - p, ring_bank("projection", n))
                if last:
                    z_out(h, k, 1)
            run_heads(act, emit_head)

            def conv():
                for c in range(NC):
                    act.wait_ge(conv_ready, c + 1)
                    copy(CT[:, c * CW:(c + 1) * CW], ps[:, 4 + c, :], conv_b[:, 0:1]).then_inc(conv_out, 1)

            def qkv(s):
                if s:
                    act.wait_ge(v_staged, H * s)
                def high(n):
                    if s == 1:
                        act.wait_ge(rotated, n + 1)
                        src, bias = T[2 * (n // NC)][:, (n % NC) * CW:(n % NC + 1) * CW], 0.0
                    else:
                        act.wait_ge(qkv_ready, QKV_BASE[s] + n + 1)
                        src, bias = ps[:, n, :], bqk[:, s, n // NC:n // NC + 1]
                    copy(part(n, 0), src, bias).then_inc(high_ready, 1)

                def middle(n):
                    act.wait_ge(rest_ready, 8 * s + n + 1)
                    copy(part(n, 1), rest(n)).then_inc(mid_ready, 1)

                for n in range(2 * NC):
                    high(n)
                    if n:
                        middle(n - 1)
                middle(2 * NC - 1)
                for c in range(NC):
                    act.wait_ge(qkv_ready, QKV_BASE[s + 1] - NC + c + 1)
                    copy(VALL[:, c * CW:(c + 1) * CW], ps[:, c, :]).then_inc(v_out, 1)

            def attention(s):
                def z_copy(g, p, k):
                    act.wait_ge(pv_done, (g + 1) * NT)
                    if not (is_int(g) and g < 2):
                        act.wait_ge(z_stored[p], (k + 8 * s) * 16)
                    copy(ZST[:, p, :], ps[:, 7, :]).then_inc(z_copied, 1)

                def emit(h, p, k):
                    g = H * s + h
                    first, last = is_int(h) and h == 0, is_int(h) and h == H - 1
                    for kt in range(NT):
                        if not (is_int(g) and g == 0 and kt < 4):
                            act.wait_ge(pv_done, g * NT + kt - 3)
                        for c in range(NC):
                            act.wait_ge(st_ready, g * NT * NC + kt * NC + c + 1)
                            act.activation(probs[:, kt % 4, c * CW:(c + 1) * CW], ps[:, st_bank(kt * NC + c), :],
                                           ACT.Exp, scale=SCALE).then_inc(exp_done, 1)
                        if kt == 0 and not first:
                            z_copy(g - 1, 1 - p, k if p else k - 1)
                    if last:
                        z_copy(g, p, k)
                run_heads(act, emit)

            def mixture(layer, n):
                act.wait_ge(shifted, layer + 1)
                if layer:
                    act.activation(ge[:, :, :], gl[:, :, :], ACT.Exp).then_inc(gate_exp, 1)
                else:
                    act.activation(ge[:, :, 0:E0], gl[:, :, 0:E0], ACT.Exp).then_inc(gate_exp, 1)
                for b_ in range(4):
                    act.wait_ge(wgt_turned, 4 * layer + b_ + 1)
                    copy(WT[0:n, b_ * CW:(b_ + 1) * CW], ps[0:n, b_, :]).then_inc(wgt_out, 1)

                def emit(e, p, k):
                    act.wait_ge(w_staged[p], (k + 4 * layer + 1) * 48)
                    for c in range(NC):
                        chunk = (e + E0 * layer) * NC + c
                        if not (is_int(e) and e == 0 and layer == 0 and c < 2):
                            act.wait_ge(y_ready, chunk - 1)
                        for f in range(FC):
                            act.wait_ge(h_ready, chunk * FC + f + 1)
                            act.activation(HT[c % 2][:, f * CW:(f + 1) * CW], ps[:, f, :],
                                           ACT.Gelu if layer else ACT.Relu,
                                           bias=B1S[:, p, f:f + 1]).then_inc(h_out, 1)
                run_experts(act, n, emit)

            act.wait_ge(ld_late, N_LATE)
            normalise(2)
            normalise(3)
            turn_out(1)
            conv()
            turn_out(2)
            qkv(0)
            attention(0)
            normalise(4)
            turn_out(3)
            mixture(0, E0)
            normalise(5)
            normalise(6)
            normalise(7)
            turn_out(4)
            qkv(1)
            attention(1)
            normalise(8)
            normalise(9)
            normalise(10)
            turn_out(5)
            qkv(2)
            attention(2)
            normalise(11)
            turn_out(6)
            mixture(1, E1)
            normalise(12)

        @block.tensor
        def _(pe):
            def mm(out_, lhsT, rhs, start=True, stop=True):
                return pe.matmul(out_, lhsT, rhs, start=start, stop=stop, skip_group_check=True)

            def turn(k):
                if k >= 1:
                    pe.wait_ge(turned_out, 4 * k)
                src = TURN[k][0]
                for n in range(NT):
                    if n % TPC == 0:
                        b = n // TPC + 1
                        if k == 2:
                            pe.wait_ge(conv_out, b)
                        else:
                            pe.wait_ge(scaled_dve, 4 * NORM_OF[k] + b)
                            pe.wait_ge(scaled_act, 4 * NORM_OF[k] + b)
                    ins = pe.transpose(ps[:, n // TPC, (n % TPC) * P:(n % TPC + 1) * P],
                                       src[:, n * P:(n + 1) * P], ident[:, :])
                    if n % TPC == TPC - 1:
                        ins.then_inc(turned, 1)

            def project(n, bank):
                if n >= VP:
                    c = n - VP
                    ins = mm(ps[:, bank, :], w_a[:, 0:2 * AD], XT[:, c * CW:(c + 1) * CW])
                else:
                    for m in range(NT // VP):
                        tok = (n * NT // VP + m) * P
                        ins = mm(ps[:, bank, m * AD:(m + 1) * AD], XT[:, tok:tok + P], w_a[:, 2 * AD:])
                ins.then_inc(a_projected, 1)

            pe.wait_ge(consts_made, 1)
            turn(0)
            pe.wait_ge(turned_out, 4)
            pe.wait_ge(a_weights, 48)
            for n in range(PROJ):
                if n >= 4:
                    pe.wait_ge(a_used, n - 3)
                project(n, 4 + n % 4)

            def pv(h, i):
                pe.wait_ge(a_vscaled, h * NT + i + 1)
                if i == 0 and not (is_int(h) and h == 0):
                    pe.wait_ge(a_zout_act, h)
                    pe.wait_ge(a_zout_dve, h)
                for c, off in row_chunks(i):
                    ins = mm(ps[AD * (c % 2):AD * (c % 2) + AD, 6 + c // 2, off:], VR[:, i % 4, :],
                             probs[:, i % 4, c * CW + off:(c + 1) * CW], start=(i == 0), stop=(i == 4 * c + 3))
                ins.then_inc(a_pv, 1)

            def bank_is_free(h, kind, n):
                user = user_before(place(kind, n), is_int(h) and h == 0, is_int(h) and h == H - 1)
                if user is None:
                    return
                kind, n, before = user
                at = h - 1 if before else h
                if kind == "scores":
                    pe.wait_ge(a_read, at * PER_HEAD + n + 1)
                else:
                    pe.wait_ge(a_used, at * PROJ + PROJ + n + 1)

            def emit_head(h, p, k):
                first, last = is_int(h) and h == 0, is_int(h) and h == H - 1
                pe.wait_ge(a_used, h * PROJ + PROJ)
                pe.wait_ge(a_swapped, h * QK + QK)
                for i in range(NT):
                    for ci, (c, off) in enumerate(row_chunks(i)):
                        j = FIRST_CHUNK[i] + ci
                        bank_is_free(h, "scores", j)
                        bank = ps[:, ring_bank("scores", j), :]
                        diagonal = c == i // TPC
                        keys, queries = slice(i * P, (i + 1) * P), slice(c * CW + off, (c + 1) * CW)
                        mm(bank[:, off:], KA[p][:, keys], QA[p][:, queries], stop=False)
                        ins = mm(bank[:, off:], KA[p][:, keys], QB[p][:, queries], start=False, stop=not diagonal)
                        if diagonal:
                            ins = mm(bank[:, off:off + P], identb[:, :], maskb[:, :], start=False)
                        ins.then_inc(a_ready, 1)
                    if i in PROJ_AFTER and not last:
                        n = PROJ_AFTER[i]
                        if n == 0:
                            pe.wait_ge(a_weights, h * 48 + 96)
                        bank_is_free(h, "projection", n)
                        project(n, ring_bank("projection", n))
                    if i >= LAG:
                        pv(h, i - LAG)
                    elif not first:
                        pv(h - 1, i - LAG + NT)
                if last:
                    for i in range(NT - LAG, NT):
                        pv(h, i)
            run_heads(pe, emit_head)

            def project_tokens(k, src_ready, parts):
                for n in range(NT):
                    if n % TPC == 0:
                        src_ready(n // TPC)
                    for m, (lhs, rhs) in enumerate(parts):
                        ins = mm(ps[:, n // TPC, (n % TPC) * P:(n % TPC + 1) * P], lhs[:, n * P:(n + 1) * P],
                                 rhs, start=(m == 0), stop=(m == len(parts) - 1))
                    if n % TPC == TPC - 1:
                        ins.then_inc(proj_ready, 1)

            def heads_out(b):
                pe.wait_ge(a_zout_act, H)
                pe.wait_ge(a_zout_dve, H)
                pe.wait_ge(ld_early, N_EARLY)
            project_tokens(0, heads_out, [(ZA[n], wo_a[:, n * P:(n + 1) * P])
                                          for n in range(PAIRS)])

            def conv():
                pe.wait_ge(turned_out, 8)
                pe.wait_ge(ld_late, N_LATE)
                for c in range(NC):
                    for j in range(3):
                        ins = mm(ps[:, 4 + c, :], conv_w[:, j * P:(j + 1) * P], XTp[:, c * CW + j:c * CW + j + CW],
                                 start=(j == 0), stop=(j == 2))
                    ins.then_inc(conv_ready, 1)

            def qkv(s, turned_before):
                pe.wait_ge(turned_out, turned_before)
                if s == 1:
                    pe.wait_ge(wrot_made, 1)
                src = QKV_SRC[s]
                for n, name in enumerate(BLOCKS[s]):
                    w = {"q": wqkv[:, s, 0:P], "k": wqkv[:, s, P:2 * P], "v": wqkv[:, s, 2 * P:],
                         "qr": wrot[:, 0:P], "kr": wrot[:, P:]}[name]
                    for c in range(NC):
                        if n >= 2 and s == 1:
                            pe.wait_ge(turned_sin if n % 2 else turned_cos, 4 * (n // 2 - 1) + c + 1)
                        elif n >= 2:
                            pe.wait_ge(rest_ready, 8 * s + c + 1)
                        bank = ps[:, 4 * (n % 2) + c, :]
                        if name != "v":
                            ins = mm(bank, w, src[:, c * CW:(c + 1) * CW])
                        else:
                            for m in range(TPC):
                                tok = (c * TPC + m) * P
                                ins = mm(bank[:, m * P:(m + 1) * P], src[:, tok:tok + P], w)
                        ins.then_inc(qkv_ready, 1)

            def attention(s):
                def max_scores(g, p, q, js):
                    for j in js:
                        u = (g * NT + q) * NC + j
                        if q == 0 and j == 0 and not (is_int(g) and g == 0):
                            pe.wait_ge(m_copied, g)
                        if not (is_int(u) and u < NC):
                            pe.wait_ge(smax_done, u - NC + 1)
                        mm(ps[:, j, :], QS[p][:, q * P:(q + 1) * P], KS[p][:, j * CW:(j + 1) * CW]
                           ).then_inc(smax_ready, 1)

                def turn_max(g):
                    pe.wait_ge(m_ready, g + 1)
                    pe.transpose(ps[:, 0, 0:P // 2].bitcast(BF16), mb[:, :], identb[:, :]
                                 ).then_inc(m_turned, 1)

                def pv(g, p, kt):
                    pe.wait_ge(exp_done, g * NT * NC + kt * NC + NC)
                    if kt == 0 and not (is_int(g) and g == 0):
                        pe.wait_ge(z_copied, g)
                    for c in range(NC):
                        ins = mm(ps[32 * c:32 * c + VC, 7, :], VS[:, p, kt, :],
                                 probs[:, kt % 4, c * CW:(c + 1) * CW], start=(kt == 0), stop=(kt == NT - 1))
                    ins.then_inc(pv_done, 1)

                pe.wait_ge(v_out, 4 * (s + 1))
                pe.wait_ge(low_ready, 8 * (s + 1))
                pe.wait_ge(ones_loaded, 32)
                pe.wait_ge(qk_staged[0], 16 * N_STAGE_DMA * (8 * s + 1))
                for q in range(NT):
                    max_scores(H * s, 0, q, range(NC))
                turn_max(H * s)

                def emit(h, p, k):
                    g = H * s + h
                    first, last = is_int(h) and h == 0, is_int(h) and h == H - 1
                    kn = k + 1 if p else k
                    pe.wait_ge(max_rows[p], (k + 8 * s + 1) * 16)
                    pe.wait_ge(v_staged, g + 1)
                    for kt in range(NT):
                        if kt == MAX_FROM and not last:
                            pe.wait_ge(qk_staged[1 - p], (kn + 8 * s + 1) * 16 * N_STAGE_DMA)
                        for c in range(NC):
                            for q, j in [] if last else max_products(kt, c):
                                max_scores(g + 1, 1 - p, q, [j])
                            m = kt * NC + c
                            if not (is_int(g) and g == 0 and m < ST_RING):
                                pe.wait_ge(exp_done, g * NT * NC + st_read_before(m))
                            mm(ps[:, st_bank(m), :], KS[p][:, kt * P:(kt + 1) * P],
                               QS[p][:, c * CW:(c + 1) * CW]).then_inc(st_ready, 1)
                            if c == 3:
                                if kt:
                                    pv(g, p, kt - 1)
                                elif not first:
                                    pv(g - 1, 1 - p, NT - 1)
                        if kt == NT - 2 and not last:
                            turn_max(g + 1)
                    if last:
                        pv(g, p, NT - 1)
                run_heads(pe, emit)

            def mixture(layer, n, turned_before):
                pe.wait_ge(turned_out, turned_before)
                width = 10 if layer else E0
                for m in range(NT):
                    ins = mm(ps[:, 4, m * 16:m * 16 + width], XT[:, m * P:(m + 1) * P], gw[:, layer, 0:width])
                ins.then_inc(logits_ready, 1)
                pe.wait_ge(wgt_ready, layer + 1)
                for m in range(NT):
                    ins = pe.transpose(ps[0:n, m // TPC, (m % TPC) * P:(m % TPC + 1) * P], wgt[:, 0:n, m],
                                       ident[:, :])
                    if m % TPC == TPC - 1:
                        ins.then_inc(wgt_turned, 1)
                for m in range(NT):
                    if m % TPC == 0:
                        pe.wait_ge(wgt_out, 4 * layer + m // TPC + 1)
                    ins = mm(ps[:, 4 + m // TPC, (m % TPC) * P:(m % TPC + 1) * P], WT[0:n, m * P:(m + 1) * P],
                             b2s[0:n, layer, :])
                    if m % TPC == TPC - 1:
                        ins.then_inc(b2_ready, 1)
                pe.wait_ge(acc_started, layer + 1)

                def down(e, p, c):
                    chunk = (e + E0 * layer) * NC + c
                    pe.wait_ge(h_out, chunk * FC + FC)
                    if not (is_int(chunk) and chunk < 2):
                        pe.wait_ge(y_used, chunk - 1)
                    for m in range(TPC):
                        for f in range(FC):
                            ins = mm(ps[:, 4 + c % 2, m * P:(m + 1) * P],
                                     HT[c % 2][:, f * CW + m * P:f * CW + (m + 1) * P],
                                     W2S[p][:, f * P:(f + 1) * P], start=(f == 0), stop=(f == FC - 1))
                    ins.then_inc(y_ready, 1)

                def emit(e, p, k):
                    pe.wait_ge(w_staged[p], (k + 4 * layer + 1) * 48)
                    for c in range(NC):
                        for f in range(FC):
                            unit = ((e + E0 * layer) * NC + c) * FC + f
                            if not (is_int(unit) and unit < FC):
                                pe.wait_ge(h_out, unit - FC + 1)
                            mm(ps[:, f, :], W1S[p][:, f * P:(f + 1) * P], XT[:, c * CW:(c + 1) * CW]
                               ).then_inc(h_ready, 1)
                        if c:
                            down(e, p, c - 1)
                        elif not (is_int(e) and e == 0):
                            down(e - 1, 1 - p, NC - 1)
                run_experts(pe, n, emit)
                down(n - 1, (n - 1) % 2, NC - 1)

            def ctx_is_ready(k):
                return lambda b: pe.wait_ge(ctx_ready, 4 * (k - 1) + b + 1)

            turn(1)
            conv()
            turn(2)
            qkv(0, 12)
            attention(0)
            project_tokens(1, ctx_is_ready(1), [(ZT, wo[:, 0, :])])
            turn(3)
            mixture(0, E0, 16)
            turn(4)
            qkv(1, 20)
            attention(1)
            project_tokens(2, ctx_is_ready(2), [(ZT, wo[:, 1, :])])
            turn(5)
            qkv(2, 24)
            attention(2)
            project_tokens(3, ctx_is_ready(3), [(ZT, wo[:, 2, :])])
            turn(6)
            mixture(1, E1, 28)

        @block.vector
        def _(dve):
            steps = [0]
            norms = [0]

            def step(ins):
                ins.then_inc(dve_step, 1)
                steps[0] += 1
                dve.wait_ge(dve_step, steps[0])

            def tiles(a):
                return a.rearrange("p (t d) -> p t d", d=P)

            def tile(a, n):
                return a[:, n * P:(n + 1) * P]

            def moments(src):
                for n in range(NT):
                    ins = dve.bn_stats(stats[:, n, :], tile(src, n))
                step(ins)
                even, odd = stats[:, :, 0:3], stats[:, :, 3:6]
                dve.tensor_tensor(half[:, 0, :], even[:, :, 1], odd[:, :, 1], ALU.add)
                dve.tensor_tensor(half[:, 1, :], even[:, :, 1], odd[:, :, 1], ALU.subtract)
                step(dve.tensor_tensor(half[:, 2, :], even[:, :, 2], odd[:, :, 2], ALU.add))
                dve.tensor_scalar(mean[:, :], half[:, 0, :], 0.5, None, ALU.mult)
                step(dve.tensor_tensor(half[:, 1, :], half[:, 1, :], half[:, 1, :], ALU.mult))
                step(dve.scalar_tensor_tensor(out=half[:, 2, :], in0=half[:, 2, :], scalar=4.0 / P,
                                              in1=half[:, 1, :], op0=ALU.mult, op1=ALU.add))

            def scale():
                n = norms[0]
                norms[0] += 1
                src, dst = NORMS[n]
                dve.wait_ge(std_ready, n + 1)
                step(dve.reciprocal(rstd[:, :], std[:, :]))
                if n == RMS:
                    dve.memset(shift[:, :], 0.0).then_inc(shift_ready, 1)
                else:
                    dve.scalar_tensor_tensor(out=shift[:, :], in0=mean[:, :], scalar=-1.0, in1=rstd[:, :],
                                             op0=ALU.mult, op1=ALU.mult).then_inc(shift_ready, 1)
                for b, on_act in enumerate(ON_ACT):
                    for m in range(b * TPC, (b + 1) * TPC):
                        if m in on_act:
                            continue
                        if n == RMS:
                            ins = dve.tensor_scalar(tile(dst, m), tile(src, m), rstd[:, m:m + 1], None, ALU.mult)
                        else:
                            ins = dve.tensor_scalar(tile(dst, m), tile(src, m), mean[:, m:m + 1],
                                                    rstd[:, m:m + 1], ALU.subtract, ALU.mult)
                    ins.then_inc(scaled_dve, 1)
                dve.wait_ge(scaled_dve, 4 * n + 4)
                dve.wait_ge(scaled_act, 4 * n + 4)

            def layer_norm():
                moments(NORMS[norms[0]][0])
                dve.tensor_scalar(var[:, :], half[:, 2, :], 0.25, EPS, ALU.mult, ALU.add).then_inc(var_ready, 1)
                scale()

            def rms_norm():
                moments(NORMS[norms[0]][0])
                step(dve.tensor_scalar(var[:, :], half[:, 2, :], 0.25, RMS_EPS, ALU.mult, ALU.add))
                step(dve.tensor_tensor(half[:, 0, :], mean[:, :], mean[:, :], ALU.mult))
                dve.tensor_tensor(var[:, :], var[:, :], half[:, 0, :], ALU.add).then_inc(var_ready, 1)
                scale()

            def along(row, n=NT):
                return row.unsqueeze(1).broadcast_to([P, n, P])

            def projected(k, dst, bias):
                for b in range(4):
                    dve.wait_ge(proj_ready, 4 * k + b + 1)
                    d = dst[:, b * CW:(b + 1) * CW]
                    if bias is None:
                        ins = dve.tensor_copy(d, ps[:, b, :])
                    else:
                        ins = dve.tensor_tensor(tiles(d), tiles(ps[:, b, :]), along(bias, TPC), ALU.add)
                step(ins)

            def add(dst, a, b):
                step(dve.tensor_tensor(dst, a, b, ALU.add))

            x, xh, y = X[:, :], XH[:, :], Y[:, :]
            dve.wait_ge(staging_cleared, 1)
            dve.wait_ge(ld_x, 16)
            layer_norm()
            rms_norm()

            MANY = sum(len(row_chunks(i)) > 1 for i in range(NT))

            def normalise(h, i, p):
                R = h * NT + i
                n = len(row_chunks(i))
                dve.wait_ge(a_read, h * PER_HEAD + FIRST_CHUNK[i] + n)
                q = i % 4
                if n > 1:
                    dve.tensor_reduce(asum[:, q:q + 1], als[:, q, 0:n], X_AXIS, ALU.add).then_inc(a_sum, 1)
                    dve.wait_ge(a_sum, h * MANY + i + 1)
                total = asum[:, q:q + 1] if n > 1 else als[:, q, 0:1]
                dve.reciprocal(arl[:, q:q + 1], total).then_inc(a_rsum, 1)
                dve.wait_ge(a_rsum, R + 1)
                if not (is_int(R) and R < 4):
                    dve.wait_ge(a_pv, R - 3)
                dve.tensor_scalar(VR[:, q, :], VA[p][:, i * AD:(i + 1) * AD], arl[:, q:q + 1],
                                  None, ALU.mult).then_inc(a_vscaled, 1)

            def z_out(head, pair, hh):
                dve.wait_ge(a_pv, (head + 1) * NT)
                for c in Z_DVE:
                    ins = dve.tensor_copy(z_place(pair, hh, c), ps[AD * (c % 2):AD * (c % 2) + AD, 6 + c // 2, :])
                ins.then_inc(a_zout_dve, 1)

            def take_projection(head, n, p, bank):
                if n < VP:
                    dve.wait_ge(a_projected, head * PROJ + n + 1)
                    v = VA[p][:, n * CW:(n + 1) * CW].rearrange("p (t d) -> p t d", d=AD)
                    dve.tensor_tensor(v, ps[:, bank, :].rearrange("p (t d) -> p t d", d=AD),
                                      bv_a[:, :].unsqueeze(1).broadcast_to([P, NT // VP, AD]), ALU.add
                                      ).then_inc(a_used, 1)
                    return
                dve.wait_ge(a_high, head * QK + n - VP + 1)
                at = slice((n - VP) * CW, (n - VP + 1) * CW)

                def low(dst, rows, high):
                    return dve.scalar_tensor_tensor(out=dst, in0=ps[rows, bank, :], scalar=bqk_a[rows, :],
                                                    in1=high, op0=ALU.add, op1=ALU.subtract)
                q_rows, k_rows = slice(0, AD), slice(AD, P)
                low(QA[p][AD:P, at], q_rows, QA[p][0:AD, at].bitcast(F32))
                low(KA[p][0:AD, at], k_rows, KA[p][AD:P, at].bitcast(F32)).then_inc(a_used, 1)

            for n in range(PROJ):
                take_projection(0, n, 0, 4 + n % 4)

            def emit_head(h, p, k):
                first, last = is_int(h) and h == 0, is_int(h) and h == H - 1
                maxima = 0
                for i in range(NT):
                    if i == LAG and not first:
                        z_out(h - 1, k if p else k - 1, 1 - p)
                    chunks = row_chunks(i)
                    n, q = len(chunks), i % 4
                    for ci, (c, off) in enumerate(chunks):
                        j = FIRST_CHUNK[i] + ci
                        dve.wait_ge(a_ready, h * PER_HEAD + j + 1)
                        if n == 1:
                            dve.tensor_reduce(anm[:, q:q + 1], ps[:, ring_bank("scores", j), off:], X_AXIS, ALU.max,
                                              negate=True).then_inc(a_negmax, 1)
                        else:
                            dve.tensor_reduce(amx[:, q, ci:ci + 1], ps[:, ring_bank("scores", j), off:], X_AXIS, ALU.max
                                              ).then_inc(a_max, 1)
                            maxima += 1
                    if n > 1:
                        dve.wait_ge(a_max, h * MAXIMA + maxima)
                        dve.tensor_reduce(anm[:, q:q + 1], amx[:, q, 0:n], X_AXIS, ALU.max, negate=True
                                          ).then_inc(a_negmax, 1)
                    if i == 0:
                        dve.wait_ge(a_used, h * PROJ + PROJ)
                    for n in [] if last else taken_after(i):
                        take_projection(h + 1, n, 1 - p, ring_bank("projection", n))
                    if i:
                        normalise(h, i - 1, p)
                    elif not first:
                        normalise(h - 1, NT - 1, 1 - p)
                if last:
                    normalise(h, NT - 1, p)
                    z_out(h, k, 1)
            MAXIMA = sum(len(row_chunks(i)) for i in range(NT) if len(row_chunks(i)) > 1)
            run_heads(dve, emit_head)

            dve.wait_ge(ld_early, N_EARLY)
            dve.wait_ge(a_pv, NT * H)
            projected(0, y, bo_a[:, :])
            layer_norm()
            add(x, x, xh)
            layer_norm()

            dve.wait_ge(ld_late, N_LATE)

            def split(s):
                if s == 1:
                    dve.wait_ge(tables_loaded, 32)

                def rotate(n):
                    k, c = n // NC, n % NC
                    at = slice(c * CW, (c + 1) * CW)
                    dve.wait_ge(qkv_ready, QKV_BASE[1] + 8 * k + c + 1)
                    dve.tensor_tensor(T[2 * k][:, at], ps[:, c, :], COS[:, at], ALU.mult).then_inc(turned_cos, 1)
                    dve.wait_ge(qkv_ready, QKV_BASE[1] + 8 * k + 4 + c + 1)
                    dve.tensor_tensor(T[2 * k + 1][:, at], ps[:, 4 + c, :], SIN[:, at], ALU.mult
                                      ).then_inc(turned_sin, 1)

                def take_high(n):
                    dve.wait_ge(high_ready, 8 * s + n + 1)
                    if s == 1:
                        ins = dve.tensor_tensor(rest(n), rest(n), part(n, 0), ALU.subtract)
                    else:
                        ins = dve.scalar_tensor_tensor(out=rest(n), in0=ps[:, n, :],
                                                       scalar=bqk[:, s, n // NC:n // NC + 1], in1=part(n, 0),
                                                       op0=ALU.add, op1=ALU.subtract)
                    ins.then_inc(rest_ready, 1)

                def take_middle(n):
                    dve.wait_ge(mid_ready, 8 * s + n + 1)
                    dve.tensor_tensor(part(n, 2), rest(n), part(n, 1), ALU.subtract).then_inc(low_ready, 1)

                lag = 2 if s == 1 else 0
                for n in range(2 * NC + lag + 1):
                    if s == 1 and n < 2 * NC:
                        rotate(n)
                    if lag <= n < 2 * NC + lag:
                        take_high(n - lag)
                    if n > lag:
                        take_middle(n - lag - 1)

            def attention(s):
                def maxima(g):
                    for q in range(NT):
                        for j in range(NC):
                            dve.wait_ge(smax_ready, (g * NT + q) * NC + j + 1)
                            dve.tensor_reduce(mx[:, q, j:j + 1], ps[:, j, :], X_AXIS, ALU.max
                                              ).then_inc(smax_done, 1)
                    dve.wait_ge(smax_done, (g + 1) * NT * NC)
                    dve.tensor_reduce(nm[:, :], mx[:, :, :], X_AXIS, ALU.max, negate=True).then_inc(m_step, 1)
                    dve.wait_ge(m_step, g * 4 + 1)
                    dve.tensor_copy(mb[:, 0:NT], nm[:, :]).then_inc(m_step, 1)
                    dve.wait_ge(m_step, g * 4 + 2)
                    dve.tensor_tensor(nr[:, :], nm[:, :], mb[:, 0:NT], ALU.subtract).then_inc(m_step, 1)
                    dve.wait_ge(m_step, g * 4 + 3)
                    dve.tensor_copy(mb[:, NT:2 * NT], nr[:, :]).then_inc(m_step, 1)
                    dve.wait_ge(m_step, g * 4 + 4)
                    dve.tensor_tensor(mb[:, 2 * NT:3 * NT], nr[:, :], mb[:, NT:2 * NT], ALU.subtract).then_inc(m_ready, 1)

                def copy_rows(g, before):
                    dve.wait_ge(m_turned, g + 1)
                    if before:
                        dve.wait_ge(*before)
                    dve.tensor_copy(mT[:, :], ps[0:3 * NT, 0, 0:P // 2].bitcast(BF16)).then_inc(m_copied, 1)

                maxima(H * s)
                copy_rows(H * s, (max_rows[1], 16 * 8 * s) if s else None)

                def emit(h, p, k):
                    g = H * s + h
                    if is_int(h) and h == H - 1:
                        return
                    maxima(g + 1)
                    copy_rows(g + 1, (max_rows[p], (k + 8 * s + 1) * 16))
                run_heads(dve, emit)
                for c in range(NC):
                    at = slice(c * CW, (c + 1) * CW)
                    dve.wait_ge(z_loaded[c], 32 * (s + 1))
                    dve.reciprocal(ZS[:, at], ZS[:, at]).then_inc(z_inverted, 1)
                    dve.wait_ge(z_inverted, NC * s + c + 1)
                    dve.tensor_tensor(ZT[:, at], ZT[:, at], ZS[:, at], ALU.mult).then_inc(ctx_ready, 1)

            def gates(layer):
                dve.wait_ge(logits_ready, layer + 1)
                raw = ps[:, 4, 0:NT * 16].rearrange("p (t e) -> p t e", e=16)
                L, G = gl[:, :, 0:E0], ge[:, :, 0:E0]

                def wide(a, n=E0):
                    return a.unsqueeze(2).broadcast_to([P, NT, n])

                if layer:
                    dve.tensor_copy(L, raw[:, :, 0:E0])
                    step(dve.tensor_tensor(gl[:, :, E0:10], raw[:, :, E0:10],
                                           gb[:, E0:10].unsqueeze(1).broadcast_to([P, NT, 2]), ALU.add))
                else:
                    step(dve.tensor_tensor(L, raw[:, :, 0:E0], gb[:, 0:E0].unsqueeze(1).broadcast_to([P, NT, E0]),
                                           ALU.add))
                step(dve.tensor_reduce(gm[:, :], L, X_AXIS, ALU.max))
                if layer:
                    step(dve.tensor_reduce(g2[:, :], gl[:, :, E0:10], X_AXIS, ALU.max))
                    step(dve.tensor_tensor(gl[:, :, E0:10], gl[:, :, E0:10], wide(g2[:, :], 2), ALU.subtract))
                dve.tensor_tensor(L, L, wide(gm[:, :]), ALU.subtract).then_inc(shifted, 1)
                dve.wait_ge(gate_exp, layer + 1)
                step(dve.tensor_reduce(gs[:, :], G, X_AXIS, ALU.add))
                step(dve.reciprocal(gs[:, :], gs[:, :]))
                if not layer:
                    dve.tensor_tensor(WPE[:, :, 0:E0], G, wide(gs[:, :]), ALU.mult).then_inc(wgt_ready, 1)
                    return
                step(dve.tensor_tensor(gp[:, :, :], G, wide(gs[:, :]), ALU.mult))
                step(dve.tensor_reduce(gm[:, :], gp[:, :, :], X_AXIS, ALU.max))
                step(dve.tensor_tensor(gp[:, :, :], gp[:, :, :], wide(gm[:, :]), ALU.is_equal))
                step(dve.tensor_tensor(gp[:, :, :], gp[:, :, :], rank[:, :].unsqueeze(1).broadcast_to([P, NT, E0]),
                                       ALU.mult))
                step(dve.tensor_reduce(g2[:, :], gp[:, :, :], X_AXIS, ALU.max))
                step(dve.tensor_tensor(gp[:, :, :], gp[:, :, :], wide(g2[:, :]), ALU.is_equal))
                step(dve.tensor_reduce(gs[:, :], ge[:, :, E0:10], X_AXIS, ALU.add))
                step(dve.reciprocal(gs[:, :], gs[:, :]))
                step(dve.tensor_tensor(ge[:, :, E0:10], ge[:, :, E0:10], wide(gs[:, :], 2), ALU.mult))
                step(dve.tensor_tensor(gm[:, :], gm[:, :], ge[:, :, E0], ALU.mult))
                dve.tensor_tensor(WPE[:, :, 0:E0], gp[:, :, :], wide(gm[:, :]), ALU.mult)
                dve.tensor_copy(wgt[:, E0, :], ge[:, :, E0 + 1]).then_inc(wgt_ready, 1)

            def mixture(layer, n):
                gates(layer)
                for b in range(4):
                    dve.wait_ge(b2_ready, 4 * layer + b + 1)
                    ins = dve.tensor_copy(ACC[:, b * CW:(b + 1) * CW], ps[:, 4 + b, :])
                ins.then_inc(acc_started, 1)
                dve.wait_ge(acc_started, layer + 1)
                scalars = wgt[:, :, :].rearrange("p e t -> p (e t)")

                def emit(e, p, k):
                    for c in range(NC):
                        chunk = (e + E0 * layer) * NC + c
                        dve.wait_ge(y_ready, chunk + 1)
                        if not (is_int(chunk) and chunk < 1):
                            dve.wait_ge(y_used, chunk)
                        for m in range(TPC):
                            a = tile(ACC, c * TPC + m)
                            ins = dve.scalar_tensor_tensor(
                                out=a, in0=ps[:, 4 + c % 2, m * P:(m + 1) * P],
                                scalar=scalars[:, bass.ds(e * NT + c * TPC + m, 1)], in1=a, op0=ALU.mult, op1=ALU.add)
                        ins.then_inc(y_used, 1)
                run_experts(dve, n, emit)
                dve.wait_ge(y_used, (E0 * layer + n) * NC)

            split(0)
            attention(0)
            projected(1, y, bo[:, 0, :])
            add(y, y, CM)
            layer_norm()
            step(dve.tensor_tensor(tiles(CM), tiles(xh), along(lnrow[:, 0, :]), ALU.mult))
            step(dve.tensor_tensor(tiles(CM), tiles(CM), along(lnrow[:, 1, :]), ALU.add))
            mixture(0, E0)
            add(y, CM, ACC)
            layer_norm()
            step(dve.tensor_tensor(tiles(xh), tiles(xh), along(lnrow[:, 2, :]), ALU.mult))
            step(dve.tensor_tensor(tiles(y), tiles(xh), along(lnrow[:, 3, :]), ALU.add))
            layer_norm()
            add(x, x, xh)
            layer_norm()
            split(1)
            attention(1)
            projected(2, y, None)
            layer_norm()
            add(x, x, xh)
            layer_norm()
            layer_norm()
            split(2)
            attention(2)
            projected(3, y, bo[:, 1, :])
            add(CM, CM, y)
            layer_norm()
            mixture(1, E1)
            add(y, CM, ACC)
            layer_norm()
            dve.tensor_tensor(x, x, xh, ALU.add).then_inc(final_ready, 1)


def kernel(**inputs):
    import numpy as np
    import concourse.bacc as bacc
    from concourse import mybir as _mybir
    from concourse.bass_utils import run_bass_kernel_spmd

    g = {k: np.asarray(v) for k, v in inputs.items()}
    a = {}
    a["x"] = g["L0_attn_x"].reshape(S, P)
    w = g["L0_attn_W_qkv"].reshape(H, AD, 3, P)
    a["a_w"] = w.transpose(0, 3, 2, 1).reshape(H, P, 3 * AD)
    b = g["L0_attn_b_qkv"].reshape(H, AD, 3)
    a["a_bqk"] = b[:, :, 0:2].transpose(0, 2, 1).reshape(H, 2 * AD, 1)
    a["a_bv"] = b[:, :, 2]
    a["a_wo"] = g["L0_attn_W_o"].T.reshape(PAIRS, P, P).transpose(1, 0, 2).reshape(P, PAIRS * P)
    a["a_bo"] = g["L0_attn_b_o"]
    a["conv_w"] = g["L0_ffn_conv_w"].transpose(1, 2, 0).reshape(P, 3 * P)
    a["conv_b"] = g["L0_ffn_conv_b"].reshape(P, 1)
    a["wqkv0"] = g["L0_ffn_wqkv"].T
    a["wqkv1"] = g["L1_attn_w_qkv"]
    a["wqkv2"] = g["L1_ffn_Wqkv"]
    for n, name in (("0", "L0_ffn_bqkv"), ("2", "L1_ffn_bqkv")):
        b = g[name].reshape(3, P)
        a["bqk" + n] = b[0:2].T
        a["bv" + n] = b[2]
    a["wo0"], a["bo0"] = g["L0_ffn_wo"].T, g["L0_ffn_bo"]
    a["wo1"] = g["L1_attn_w_proj"]
    a["wo2"], a["bo2"] = g["L1_ffn_Wo"], g["L1_ffn_bo"]
    a["ln_b1_g"], a["ln_b1_b"] = g["L0_ffn_ln1_g"], g["L0_ffn_ln1_b"]
    a["ln_b2_g"], a["ln_b2_b"] = g["L0_ffn_ln2_g"], g["L0_ffn_ln2_b"]
    a["lncol"] = np.stack([g["L0_ffn_ln1_g"], g["L0_ffn_ln1_b"], g["L1_ffn_ln1_g"], g["L1_ffn_ln1_b"],
                           g["L1_ffn_ln2_g"], g["L1_ffn_ln2_b"]], axis=1)
    a["gate_w0"] = g["L0_ffn_gate_w"]
    a["gate_w1"] = np.concatenate([g["L1_ffn_gate_w"], g["L1_ffn_coef_w"]], axis=1)
    a["gate_b"], a["coef_b"] = g["L0_ffn_gate_b"], g["L1_ffn_coef_b"]
    a["b2_0"] = g["L0_ffn_b2"]
    a["b2_1"] = np.concatenate([g["L1_ffn_b2"], g["L1_ffn_rb2"][None]], axis=0)
    a["w1"] = np.concatenate([g["L0_ffn_w1"], g["L1_ffn_W1"], g["L1_ffn_rW1"][None]], axis=0)
    w2 = np.concatenate([g["L0_ffn_w2"], g["L1_ffn_W2"], g["L1_ffn_rW2"][None]], axis=0)
    a["w2"] = w2.reshape(-1, FC, P, P).transpose(0, 2, 1, 3).reshape(-1, P, FC * P)
    b1 = np.concatenate([g["L0_ffn_b1"], g["L1_ffn_b1"], g["L1_ffn_rb1"][None]], axis=0)
    a["b1"] = b1.reshape(-1, FC, P).transpose(0, 2, 1)
    inv_freq = (np.float32(1.0) / np.float32(10000.0) ** (np.arange(0, DH, 2, dtype=np.float32) / np.float32(DH))
                ).astype(np.float32)
    freqs = np.arange(S, dtype=np.float32)[:, None] * inv_freq[None, :]
    a["cos"] = np.tile(np.repeat(np.cos(freqs), 2, axis=1), (1, H)).T
    a["sin"] = np.tile(np.repeat(np.sin(freqs), 2, axis=1), (1, H)).T
    a["rank"] = np.arange(E0, 0, -1).astype(np.float32)
    bf = _mybir.dt.np(BF16) if hasattr(_mybir.dt, "np") else np.dtype("bfloat16")
    a["ones"] = np.ones((3, S), dtype=bf)
    a["zeros"] = np.zeros((H, 3, S), dtype=bf)

    nc = bacc.Bacc("TRN2", target_bir_lowering=False, num_devices=1)
    arrays, t = {}, {}
    for name, v in a.items():
        v = np.ascontiguousarray(v)
        arrays[f"in_{name}"] = v
        t[name] = nc.dram_tensor(f"in_{name}", v.shape, _mybir.dt.from_np(v.dtype), kind="ExternalInput").ap()
    out = nc.dram_tensor("out_0", (S, P), F32, kind="ExternalOutput").ap()
    sandwich_kernel(nc, t, out)
    r = run_bass_kernel_spmd(nc, [arrays], core_ids=[0])
    return r.results[0]["out_0"].reshape(1, S, P)
```
